# Optimizing a Trainium2 kernel written in Bass

```python
import numpy as np
import jax
import jax.numpy as jnp

def _softmax(x, axis=-1):
    return jax.nn.softmax(x, axis=axis)

def _gelu(x):
    return jax.nn.gelu(x, approximate=True)

def _silu(x):
    return jax.nn.silu(x)

def _sigmoid(x):
    return jax.nn.sigmoid(x)

def _layernorm(x, axis=-1, eps=1e-05):
    m = jnp.mean(x, axis=axis, keepdims=True)
    v = jnp.var(x, axis=axis, keepdims=True)
    return (x - m) / jnp.sqrt(v + eps)

def _scatter_add(tgt, idx, src, axis=0):
    return tgt.at[idx].add(src)

def _segment_sum(src, seg, n):
    return jax.ops.segment_sum(src, seg, n)
kernel_name = 'mk_gnn_preln_d4_gnn_r16_704b61'

def setup_inputs(seed: int=0):
    np.random.seed(seed)
    _w = jnp.asarray

    def _rec_inputs():
        import jax
        import jax.numpy as jnp
        _gk = jax.random.key(seed)
        x = -0.0002928 + 1 * jax.random.normal(jax.random.fold_in(_gk, 1), (512, 512), jnp.float32)
        src = jax.random.randint(jax.random.fold_in(_gk, 2), (16384,), 0, 512, jnp.int32)
        dst = jnp.minimum((512 * jax.random.uniform(jax.random.fold_in(_gk, 3), (16384,)) ** 2.0).astype(jnp.int32), 8191)
        _o = jnp.argsort(dst, stable=True)
        src = src[_o]
        dst = dst[_o]
        edge_type_2 = jax.random.randint(jax.random.fold_in(_gk, 12), (16384,), 0, 2, jnp.int32)
        edge_weight = jax.random.uniform(jax.random.fold_in(_gk, 13), (16384,), jnp.float32, 0.0, 0.999994)
        node_vec1 = jax.random.uniform(jax.random.fold_in(_gk, 14), (512, 1), jnp.float32, 0.0, 0.999957)
        return (x, src, dst, edge_type_2, edge_weight, node_vec1)
    x, src, dst, edge_type_2, edge_weight, node_vec1 = _rec_inputs()

    def _L0_gnn_setup():
        import jax, jax.numpy as jnp
        import numpy as np
        N_NODES = 512
        D_MODEL = 512
        N_LAYERS = 2
        N_EDGES = 16384
        LEAKY_SLOPE = 0.01

        def _normalized_adj(edge_index, edge_weights, num_nodes):
            A = jnp.zeros((num_nodes, num_nodes), dtype=edge_weights.dtype)
            A = A.at[edge_index[0], edge_index[1]].add(edge_weights)
            deg = jnp.sum(A, axis=1)
            dinv = jnp.where(deg > 0, deg ** (-0.5), 0.0)
            return dinv[:, None] * A * dinv[None, :]
        key = jax.random.key(seed)
        ks = jax.random.split(key, 6)
        x = jax.random.normal(ks[0], (N_NODES, D_MODEL), dtype=jnp.float32)
        edge_weights = jax.random.uniform(ks[1], (N_EDGES,), dtype=jnp.float32)
        edge_index = jax.random.randint(ks[2], (2, N_EDGES), 0, N_NODES, dtype=jnp.int64)
        scale = 0.02
        W_gcn = jax.random.normal(ks[3], (N_LAYERS, D_MODEL, D_MODEL), dtype=jnp.float32) * scale
        b_gcn = jnp.zeros((N_LAYERS, D_MODEL), dtype=jnp.float32)
        W_mlp = jax.random.normal(ks[4], (N_LAYERS, D_MODEL, D_MODEL), dtype=jnp.float32) * scale
        b_mlp = jnp.zeros((N_LAYERS, D_MODEL), dtype=jnp.float32)
        return {'x': x, 'edge_weights': edge_weights, 'W_gcn': W_gcn, 'b_gcn': b_gcn, 'W_mlp': W_mlp, 'b_mlp': b_mlp, 'edge_index': edge_index}
    _L0_gnn_all = _L0_gnn_setup()
    _L0_gnn_in = {k: v for k, v in _L0_gnn_all.items() if k in ('W_gcn', 'b_gcn', 'W_mlp', 'b_mlp')}
    del _L0_gnn_all

    def _L1_gnn_setup():
        import jax, jax.numpy as jnp
        import numpy as np
        N_NODES = 40962
        LATENT_DIM = 512
        N_EDGES = 40962
        NUM_BLOCKS = 4
        NUM_HEADS = 4
        NUM_FREQ = 32
        BASE_PERIOD = 16
        NOISE_EMB_DIM = 16
        EPS = 1e-05

        def _cond_layer_norm(x, cond, sw, sb, bw, bb):
            mu = jnp.mean(x, axis=-1, keepdims=True)
            var = jnp.var(x, axis=-1, keepdims=True)
            xn = (x - mu) * jax.lax.rsqrt(var + EPS)
            scale = cond @ sw + sb
            bias = cond @ bw + bb
            return xn * (1.0 + scale) + bias

        def _sparse_attention(x, src, dst, wq, bq, wk, bk, wv, bv, wo, bo):
            N, D = x.shape
            H, Dh = (NUM_HEADS, D // NUM_HEADS)
            q = (x @ wq + bq).reshape(N, H, Dh) * Dh ** (-0.5)
            k = (x @ wk + bk).reshape(N, H, Dh)
            v = (x @ wv + bv).reshape(N, H, Dh)
            scores = jnp.einsum('ehd,ehd->eh', q[src], k[dst])
            smax = jax.ops.segment_max(scores, src, num_segments=N)
            ex = jnp.exp(scores - smax[src])
            denom = jax.ops.segment_sum(ex, src, num_segments=N)
            attn = ex / denom[src]
            out = jax.ops.segment_sum(attn[:, :, None] * v[dst], src, num_segments=N)
            return out.reshape(N, D) @ wo + bo

        def _forward(x, edge_index, noise_levels, f_w1, f_b1, f_w2, f_b2, s1_w, s1_b, b1_w, b1_b, wq, bq, wk, bk, wv, bv, wo, bo, s2_w, s2_b, b2_w, b2_b, m_w1, m_b1, m_w2, m_b2):
            src, dst = (edge_index[0], edge_index[1])
            freqs = jnp.arange(1, NUM_FREQ + 1, dtype=x.dtype) * (2.0 * np.pi / BASE_PERIOD)
            ph = noise_levels * freqs
            emb = jnp.concatenate([jnp.sin(ph), jnp.cos(ph)], axis=-1)
            cond = jax.nn.silu(emb @ f_w1 + f_b1) @ f_w2 + f_b2
            for i in range(NUM_BLOCKS):
                y = _cond_layer_norm(x, cond, s1_w[i], s1_b[i], b1_w[i], b1_b[i])
                y = _sparse_attention(y, src, dst, wq[i], bq[i], wk[i], bk[i], wv[i], bv[i], wo[i], bo[i])
                x = x + y
                y = _cond_layer_norm(x, cond, s2_w[i], s2_b[i], b2_w[i], b2_b[i])
                y = jax.nn.relu(y @ m_w1[i] + m_b1[i]) @ m_w2[i] + m_b2[i]
                x = x + y
            return x
        key = jax.random.key(seed)
        ks = jax.random.split(key, 20)

        def w(k, shape, s=0.02):
            return jax.random.normal(k, shape, dtype=jnp.float32) * s
        D, B, C = (LATENT_DIM, NUM_BLOCKS, NOISE_EMB_DIM)
        z = lambda *s: jnp.zeros(s, jnp.float32)
        return {'latent_mesh_nodes': jax.random.normal(ks[0], (N_NODES, D), dtype=jnp.float32), 'edge_index': jax.random.randint(ks[1], (2, N_EDGES), 0, N_NODES, dtype=jnp.int32), 'noise_levels': jax.random.uniform(ks[2], (N_NODES, 1), dtype=jnp.float32), 'f_w1': w(ks[3], (2 * NUM_FREQ, C)), 'f_b1': z(C), 'f_w2': w(ks[4], (C, C)), 'f_b2': z(C), 's1_w': w(ks[5], (B, C, D)), 's1_b': z(B, D), 'b1_w': w(ks[6], (B, C, D)), 'b1_b': z(B, D), 'wq': w(ks[7], (B, D, D)), 'bq': z(B, D), 'wk': w(ks[8], (B, D, D)), 'bk': z(B, D), 'wv': w(ks[9], (B, D, D)), 'bv': z(B, D), 'wo': w(ks[10], (B, D, D)), 'bo': z(B, D), 's2_w': w(ks[11], (B, C, D)), 's2_b': z(B, D), 'b2_w': w(ks[12], (B, C, D)), 'b2_b': z(B, D), 'm_w1': w(ks[13], (B, D, D)), 'm_b1': z(B, D), 'm_w2': w(ks[14], (B, D, D)), 'm_b2': z(B, D)}
    _L1_gnn_all = _L1_gnn_setup()
    _L1_gnn_in = {k: v for k, v in _L1_gnn_all.items() if k in ('f_w1', 'f_b1', 'f_w2', 'f_b2', 's1_w', 's1_b', 'b1_w', 'b1_b', 'wq', 'bq', 'wk', 'bk', 'wv', 'bv', 'wo', 'bo', 's2_w', 's2_b', 'b2_w', 'b2_b', 'm_w1', 'm_b1', 'm_w2', 'm_b2')}
    del _L1_gnn_all

    def _L2_gnn_setup():
        import jax, jax.numpy as jnp
        import numpy as np
        N = 512
        D = 512
        E = 16384
        STEPS = 3
        key = jax.random.key(seed)
        k1, k2, k3 = jax.random.split(key, 3)
        x = jax.random.normal(k1, (N, D), dtype=jnp.float32)
        edge_index = jax.random.randint(k2, (2, E), 0, N, dtype=jnp.int32)
        W = jax.random.normal(k3, (D, D), dtype=jnp.float32) / np.sqrt(D)
        b = jnp.zeros((D,), dtype=jnp.float32)
        diffusion_weights = jnp.ones((STEPS + 1,), dtype=jnp.float32) / (STEPS + 1)
        return {'x': x, 'edge_index': edge_index, 'W': W, 'b': b, 'diffusion_weights': diffusion_weights}
    _L2_gnn_all = _L2_gnn_setup()
    _L2_gnn_in = {k: v for k, v in _L2_gnn_all.items() if k in ('W', 'b', 'diffusion_weights')}
    del _L2_gnn_all

    def _L3_gnn_setup():
        import jax, jax.numpy as jnp
        import numpy as np
        NUM_RELATIONS = 2
        NUM_BASES = 30
        HIDDEN = 512
        N_NODES = 625
        N_EDGES = 10000

        def rgcn_gate_layer(x, row, col, edge_type, basis, att, gate_w, root, bias):
            H = x.shape[1]
            w = jnp.einsum('rb,bio->rio', att, basis)
            x_j = x[col]
            msgs = []
            for r in range(NUM_RELATIONS):
                gate = jax.nn.sigmoid(x_j @ gate_w[r, :, 0])
                msgs.append(gate[:, None] * x_j @ w[r])
            msg = jnp.where((edge_type == 0)[:, None], msgs[0], msgs[1])
            agg = jax.ops.segment_sum(msg, row, num_segments=x.shape[0])
            return agg + x @ root + bias
        key = jax.random.key(seed)
        ks = jax.random.split(key, 16)
        H, R, B = (HIDDEN, NUM_RELATIONS, NUM_BASES)
        bound = 1.0 / np.sqrt(B * H)
        u = lambda k, shape: jax.random.uniform(k, shape, jnp.float32, -bound, bound)
        inp = {'x': jax.random.normal(ks[0], (N_NODES, H), jnp.float32), 'edge_index': jax.random.randint(ks[1], (2, N_EDGES), 0, N_NODES, jnp.int32), 'edge_type': jax.random.randint(ks[2], (N_EDGES,), 0, R, jnp.int32), 'basis1': u(ks[3], (B, H, H)), 'att1': u(ks[4], (R, B)), 'gate_w1': u(ks[5], (R, H, 1)), 'root1': u(ks[6], (H, H)), 'bias1': u(ks[7], (H,)), 'basis2': u(ks[8], (B, H, H)), 'att2': u(ks[9], (R, B)), 'gate_w2': u(ks[10], (R, H, 1)), 'root2': u(ks[11], (H, H)), 'bias2': u(ks[12], (H,))}
        return inp
    _L3_gnn_all = _L3_gnn_setup()
    _L3_gnn_in = {k: v for k, v in _L3_gnn_all.items() if k in ('basis1', 'att1', 'gate_w1', 'root1', 'bias1', 'basis2', 'att2', 'gate_w2', 'root2', 'bias2')}
    del _L3_gnn_all
    return {'x': x, 'src': src, 'dst': dst, 'edge_type_2': edge_type_2, 'edge_weight': edge_weight, 'node_vec1': node_vec1, 'L0_gnn_W_gcn': _L0_gnn_in['W_gcn'], 'L0_gnn_b_gcn': _L0_gnn_in['b_gcn'], 'L0_gnn_W_mlp': _L0_gnn_in['W_mlp'], 'L0_gnn_b_mlp': _L0_gnn_in['b_mlp'], 'L1_gnn_f_w1': _L1_gnn_in['f_w1'], 'L1_gnn_f_b1': _L1_gnn_in['f_b1'], 'L1_gnn_f_w2': _L1_gnn_in['f_w2'], 'L1_gnn_f_b2': _L1_gnn_in['f_b2'], 'L1_gnn_s1_w': _L1_gnn_in['s1_w'], 'L1_gnn_s1_b': _L1_gnn_in['s1_b'], 'L1_gnn_b1_w': _L1_gnn_in['b1_w'], 'L1_gnn_b1_b': _L1_gnn_in['b1_b'], 'L1_gnn_wq': _L1_gnn_in['wq'], 'L1_gnn_bq': _L1_gnn_in['bq'], 'L1_gnn_wk': _L1_gnn_in['wk'], 'L1_gnn_bk': _L1_gnn_in['bk'], 'L1_gnn_wv': _L1_gnn_in['wv'], 'L1_gnn_bv': _L1_gnn_in['bv'], 'L1_gnn_wo': _L1_gnn_in['wo'], 'L1_gnn_bo': _L1_gnn_in['bo'], 'L1_gnn_s2_w': _L1_gnn_in['s2_w'], 'L1_gnn_s2_b': _L1_gnn_in['s2_b'], 'L1_gnn_b2_w': _L1_gnn_in['b2_w'], 'L1_gnn_b2_b': _L1_gnn_in['b2_b'], 'L1_gnn_m_w1': _L1_gnn_in['m_w1'], 'L1_gnn_m_b1': _L1_gnn_in['m_b1'], 'L1_gnn_m_w2': _L1_gnn_in['m_w2'], 'L1_gnn_m_b2': _L1_gnn_in['m_b2'], 'L2_gnn_W': _L2_gnn_in['W'], 'L2_gnn_b': _L2_gnn_in['b'], 'L2_gnn_diffusion_weights': _L2_gnn_in['diffusion_weights'], 'L3_gnn_basis1': _L3_gnn_in['basis1'], 'L3_gnn_att1': _L3_gnn_in['att1'], 'L3_gnn_gate_w1': _L3_gnn_in['gate_w1'], 'L3_gnn_root1': _L3_gnn_in['root1'], 'L3_gnn_bias1': _L3_gnn_in['bias1'], 'L3_gnn_basis2': _L3_gnn_in['basis2'], 'L3_gnn_att2': _L3_gnn_in['att2'], 'L3_gnn_gate_w2': _L3_gnn_in['gate_w2'], 'L3_gnn_root2': _L3_gnn_in['root2'], 'L3_gnn_bias2': _L3_gnn_in['bias2']}

def reference(x, src, dst, edge_type_2, edge_weight, node_vec1, L0_gnn_W_gcn, L0_gnn_b_gcn, L0_gnn_W_mlp, L0_gnn_b_mlp, L1_gnn_f_w1, L1_gnn_f_b1, L1_gnn_f_w2, L1_gnn_f_b2, L1_gnn_s1_w, L1_gnn_s1_b, L1_gnn_b1_w, L1_gnn_b1_b, L1_gnn_wq, L1_gnn_bq, L1_gnn_wk, L1_gnn_bk, L1_gnn_wv, L1_gnn_bv, L1_gnn_wo, L1_gnn_bo, L1_gnn_s2_w, L1_gnn_s2_b, L1_gnn_b2_w, L1_gnn_b2_b, L1_gnn_m_w1, L1_gnn_m_b1, L1_gnn_m_w2, L1_gnn_m_b2, L2_gnn_W, L2_gnn_b, L2_gnn_diffusion_weights, L3_gnn_basis1, L3_gnn_att1, L3_gnn_gate_w1, L3_gnn_root1, L3_gnn_bias1, L3_gnn_basis2, L3_gnn_att2, L3_gnn_gate_w2, L3_gnn_root2, L3_gnn_bias2):
    import jax
    import jax.numpy as jnp

    def _L0_gnn_ref(x, edge_weights, W_gcn, b_gcn, W_mlp, b_mlp, edge_index):
        import jax, jax.numpy as jnp
        import numpy as np
        N_NODES = 512
        D_MODEL = 512
        N_LAYERS = 2
        N_EDGES = 16384
        LEAKY_SLOPE = 0.01

        def _normalized_adj(edge_index, edge_weights, num_nodes):
            A = jnp.zeros((num_nodes, num_nodes), dtype=edge_weights.dtype)
            A = A.at[edge_index[0], edge_index[1]].add(edge_weights)
            deg = jnp.sum(A, axis=1)
            dinv = jnp.where(deg > 0, deg ** (-0.5), 0.0)
            return dinv[:, None] * A * dinv[None, :]
        N = x.shape[0]
        A_norm = _normalized_adj(edge_index, edge_weights, N)
        h = x
        for l in range(W_gcn.shape[0]):
            h = A_norm @ h
            h = h @ W_gcn[l] + b_gcn[l]
            h = jax.nn.leaky_relu(h @ W_mlp[l] + b_mlp[l], negative_slope=LEAKY_SLOPE)
        return h

    def _L1_gnn_ref(latent_mesh_nodes, edge_index, noise_levels, f_w1, f_b1, f_w2, f_b2, s1_w, s1_b, b1_w, b1_b, wq, bq, wk, bk, wv, bv, wo, bo, s2_w, s2_b, b2_w, b2_b, m_w1, m_b1, m_w2, m_b2):
        import jax, jax.numpy as jnp
        import numpy as np
        N_NODES = 40962
        LATENT_DIM = 512
        N_EDGES = 40962
        NUM_BLOCKS = 4
        NUM_HEADS = 4
        NUM_FREQ = 32
        BASE_PERIOD = 16
        NOISE_EMB_DIM = 16
        EPS = 1e-05

        def _cond_layer_norm(x, cond, sw, sb, bw, bb):
            mu = jnp.mean(x, axis=-1, keepdims=True)
            var = jnp.var(x, axis=-1, keepdims=True)
            xn = (x - mu) * jax.lax.rsqrt(var + EPS)
            scale = cond @ sw + sb
            bias = cond @ bw + bb
            return xn * (1.0 + scale) + bias

        def _sparse_attention(x, src, dst, wq, bq, wk, bk, wv, bv, wo, bo):
            N, D = x.shape
            H, Dh = (NUM_HEADS, D // NUM_HEADS)
            q = (x @ wq + bq).reshape(N, H, Dh) * Dh ** (-0.5)
            k = (x @ wk + bk).reshape(N, H, Dh)
            v = (x @ wv + bv).reshape(N, H, Dh)
            scores = jnp.einsum('ehd,ehd->eh', q[src], k[dst])
            smax = jax.ops.segment_max(scores, src, num_segments=N)
            ex = jnp.exp(scores - smax[src])
            denom = jax.ops.segment_sum(ex, src, num_segments=N)
            attn = ex / denom[src]
            out = jax.ops.segment_sum(attn[:, :, None] * v[dst], src, num_segments=N)
            return out.reshape(N, D) @ wo + bo

        def _forward(x, edge_index, noise_levels, f_w1, f_b1, f_w2, f_b2, s1_w, s1_b, b1_w, b1_b, wq, bq, wk, bk, wv, bv, wo, bo, s2_w, s2_b, b2_w, b2_b, m_w1, m_b1, m_w2, m_b2):
            src, dst = (edge_index[0], edge_index[1])
            freqs = jnp.arange(1, NUM_FREQ + 1, dtype=x.dtype) * (2.0 * np.pi / BASE_PERIOD)
            ph = noise_levels * freqs
            emb = jnp.concatenate([jnp.sin(ph), jnp.cos(ph)], axis=-1)
            cond = jax.nn.silu(emb @ f_w1 + f_b1) @ f_w2 + f_b2
            for i in range(NUM_BLOCKS):
                y = _cond_layer_norm(x, cond, s1_w[i], s1_b[i], b1_w[i], b1_b[i])
                y = _sparse_attention(y, src, dst, wq[i], bq[i], wk[i], bk[i], wv[i], bv[i], wo[i], bo[i])
                x = x + y
                y = _cond_layer_norm(x, cond, s2_w[i], s2_b[i], b2_w[i], b2_b[i])
                y = jax.nn.relu(y @ m_w1[i] + m_b1[i]) @ m_w2[i] + m_b2[i]
                x = x + y
            return x
        return _forward(latent_mesh_nodes, edge_index, noise_levels, f_w1, f_b1, f_w2, f_b2, s1_w, s1_b, b1_w, b1_b, wq, bq, wk, bk, wv, bv, wo, bo, s2_w, s2_b, b2_w, b2_b, m_w1, m_b1, m_w2, m_b2)

    def _L2_gnn_ref(x, edge_index, W, b, diffusion_weights):
        import jax, jax.numpy as jnp
        import numpy as np
        N = 512
        D = 512
        E = 16384
        STEPS = 3
        h = x @ W + b
        row, col = (edge_index[0], edge_index[1])
        adj = jnp.zeros((N, N), dtype=h.dtype)
        adj = adj.at[row, col].set(1.0)
        adj = adj.at[col, row].set(1.0)
        adj = adj + jnp.eye(N, dtype=h.dtype)
        row_sum = adj.sum(axis=1, keepdims=True)
        adj = adj / jnp.maximum(row_sum, 1.0)
        out = diffusion_weights[0] * h
        cur = h
        for i in range(STEPS):
            cur = adj @ cur
            out = out + diffusion_weights[i + 1] * cur
        return jax.nn.relu(out)

    def _L3_gnn_ref(x, edge_index, edge_type, basis1, att1, gate_w1, root1, bias1, basis2, att2, gate_w2, root2, bias2):
        import jax, jax.numpy as jnp
        import numpy as np
        NUM_RELATIONS = 2
        NUM_BASES = 30
        HIDDEN = 512
        N_NODES = 625
        N_EDGES = 10000

        def rgcn_gate_layer(x, row, col, edge_type, basis, att, gate_w, root, bias):
            H = x.shape[1]
            w = jnp.einsum('rb,bio->rio', att, basis)
            x_j = x[col]
            msgs = []
            for r in range(NUM_RELATIONS):
                gate = jax.nn.sigmoid(x_j @ gate_w[r, :, 0])
                msgs.append(gate[:, None] * x_j @ w[r])
            msg = jnp.where((edge_type == 0)[:, None], msgs[0], msgs[1])
            agg = jax.ops.segment_sum(msg, row, num_segments=x.shape[0])
            return agg + x @ root + bias
        row, col = (edge_index[0], edge_index[1])
        h = jax.nn.relu(rgcn_gate_layer(x, row, col, edge_type, basis1, att1, gate_w1, root1, bias1))
        out = rgcn_gate_layer(h, row, col, edge_type, basis2, att2, gate_w2, root2, bias2)
        return out
    edge_index = jnp.stack([src, dst])
    h = jnp.maximum(_layernorm(x, axis=-1), 0.0)
    x = x + _L0_gnn_ref(h, edge_weight, L0_gnn_W_gcn, L0_gnn_b_gcn, L0_gnn_W_mlp, L0_gnn_b_mlp, edge_index)
    h = jnp.maximum(_layernorm(x, axis=-1), 0.0)
    x = x + _L1_gnn_ref(h, edge_index, node_vec1, L1_gnn_f_w1, L1_gnn_f_b1, L1_gnn_f_w2, L1_gnn_f_b2, L1_gnn_s1_w, L1_gnn_s1_b, L1_gnn_b1_w, L1_gnn_b1_b, L1_gnn_wq, L1_gnn_bq, L1_gnn_wk, L1_gnn_bk, L1_gnn_wv, L1_gnn_bv, L1_gnn_wo, L1_gnn_bo, L1_gnn_s2_w, L1_gnn_s2_b, L1_gnn_b2_w, L1_gnn_b2_b, L1_gnn_m_w1, L1_gnn_m_b1, L1_gnn_m_w2, L1_gnn_m_b2)
    h = jnp.maximum(_layernorm(x, axis=-1), 0.0)
    x = x + _L2_gnn_ref(h, edge_index, L2_gnn_W, L2_gnn_b, L2_gnn_diffusion_weights)
    h = jnp.maximum(_layernorm(x, axis=-1), 0.0)
    x = x + _L3_gnn_ref(h, edge_index, edge_type_2, L3_gnn_basis1, L3_gnn_att1, L3_gnn_gate_w1, L3_gnn_root1, L3_gnn_bias1, L3_gnn_basis2, L3_gnn_att2, L3_gnn_gate_w2, L3_gnn_root2, L3_gnn_bias2)
    return x

_drawn_inputs = setup_inputs


def setup_inputs(seed=0):
    import zlib

    import numpy as np

    out = dict(_drawn_inputs(seed))
    spreads = {'L0_gnn_b_gcn': (0.0, 0.1),
     'L0_gnn_b_mlp': (0.0, 0.1),
     'L1_gnn_f_b1': (0.0, 0.8),
     'L1_gnn_f_b2': (0.0, 0.8),
     'L1_gnn_s1_b': (0.0, 0.795),
     'L1_gnn_b1_b': (0.0, 0.298),
     'L1_gnn_bq': (0.0, 0.8),
     'L1_gnn_bk': (0.0, 2.0),
     'L1_gnn_bv': (0.0, 0.1),
     'L1_gnn_bo': (0.0, 0.1),
     'L1_gnn_s2_b': (0.0, 0.451),
     'L1_gnn_b2_b': (0.0, 0.451),
     'L1_gnn_m_b1': (0.0, 0.1),
     'L1_gnn_m_b2': (0.0, 0.1),
     'L2_gnn_b': (0.0, 0.1),
     'L2_gnn_diffusion_weights': (0.25, 0.6)}
    factors = {'edge_weight': 8.0,
     'node_vec1': 8.0,
     'L0_gnn_W_gcn': 4.994,
     'L1_gnn_f_w1': 8.0,
     'L1_gnn_f_w2': 8.0,
     'L1_gnn_s1_w': 8.0,
     'L1_gnn_b1_w': 8.0,
     'L1_gnn_wq': 6.137,
     'L1_gnn_wk': 6.032,
     'L1_gnn_s2_w': 8.0,
     'L1_gnn_b2_w': 8.0,
     'L3_gnn_basis1': 8.0,
     'L3_gnn_att1': 8.0,
     'L3_gnn_gate_w1': 8.0,
     'L3_gnn_root1': 8.0,
     'L3_gnn_bias1': 8.0,
     'L3_gnn_basis2': 8.0,
     'L3_gnn_att2': 8.0,
     'L3_gnn_gate_w2': 8.0,
     'L3_gnn_root2': 8.0,
     'L3_gnn_bias2': 35.218}
    for name, (base, spread) in spreads.items():
        noise = np.random.default_rng([zlib.crc32(name.encode()), seed]).standard_normal(out[name].shape)
        drawn = base * np.exp(spread * noise) if base else spread * noise
        out[name] = jnp.asarray(drawn.astype(out[name].dtype))
    for name, factor in factors.items():
        out[name] = (out[name] * factor).astype(out[name].dtype)
    return out
```

```python
from contextlib import ExitStack

import concourse.bass as bass
from concourse import mybir

ALU = mybir.AluOpType
ACT = mybir.ActivationFunctionType
AX = mybir.AxisListType
F32 = mybir.dt.float32
F32R = mybir.dt.float32r
I32 = mybir.dt.int32
I16 = mybir.dt.int16
U8 = mybir.dt.uint8

P = 128
NODES = 512
D = 512
NT = NODES // P
KT = D // P
EDGES = 16384
ET = EDGES // P
GRP = 2
NG = ET // GRP
HEADS = 4
DH = D // HEADS
BLOCKS = 4
FREQS = 32
PERIOD = 16
COND = 16
BASES = 30
STEPS = 3
RING = 7
EPS = 1e-5
SCALE = DH ** -0.5
NOEDGE = -1e30
MAGIC = 1.5 * 2 ** 23
TURN = 6.283185


class Tiles:

    def __init__(self, names, base, banks=RING):
        self.at = {n: j for j, n in enumerate(names)}
        self.base, self.n, self.banks = base, len(names), banks
        self.end = base + len(names)

    def bank(self, name):
        return self.at[name] % self.banks


def l1_order():
    o = []
    ln = lambda s, t: [("S" + s, t), ("B" + s, t)]
    o += ln("a", 0) + ln("a", 1) + [("Ta", 0)] + ln("a", 2) + [("v", 0), ("Ta", 1)] + ln("a", 3)
    o += [("v", 1), ("Ta", 2), ("v", 2), ("Ta", 3), ("v", 3)]
    for h in range(HEADS):
        o += [("q", h), ("k", h)]
        if h:
            o += [("PT", h - 1, m) for m in range(NT)] + [("PV", h - 1)]
        o += [("s", h, j) for j in range(NT)]
    o += [("PT", HEADS - 1, m) for m in range(NT)] + [("PV", HEADS - 1)]
    o += [("o", 0)] + ln("b", 0) + [("o", 1)] + ln("b", 1) + [("Tb", 0), ("o", 2)] + ln("b", 2)
    o += [("Tb", 1), ("o", 3)] + ln("b", 3) + [("Tb", 2), ("Tb", 3)]
    o += [("M", m) for m in range(KT)] + [("X", t) for t in range(NT)]
    return o


def program(nc, x_d, src_d, dst_d, type_d, w_d, noise_d, l0, l1, l2, l3, out_d, mix_d):
    top = ExitStack()
    with top:
        def sb(name, shape, dt=F32, ctx=top):
            return ctx.enter_context(nc.sbuf_tensor(name, shape, dt))

        def sem(name):
            return top.enter_context(nc.semaphore(name))

        pre = Tiles(["tab", "z1", "z2"], 0)
        mid = Tiles(["deg", "dinv"], pre.end)
        n0 = Tiles([(s, l, t) for l in range(2) for s in ("G", "U", "H") for t in range(4)], mid.end)
        cnt = Tiles([("C", j) for j in range(NT)], n0.end)
        order1 = l1_order()
        n1 = Tiles(order1, cnt.end)
        assert n1.n % RING == 0
        PER = n1.n
        n2 = Tiles([("T", t) for t in range(4)] + [("A", k, t) for k in range(STEPS + 1) for t in range(4)],
                   n1.base + BLOCKS * PER)
        n3 = Tiles([("T", t) for t in range(4)]
                   + [n for l in range(2) for n in [("g", l)] + [("Z", l, r, t) for r in range(2) for t in range(4)]
                      + [("R", l, t) for t in range(4)]], n2.end)

        def highs(names, base):
            return {n: base + j for j, n in enumerate(names)}, base + len(names)

        hi0, e = highs([n for n in n0.at if n[0] != "H" or n[1] == 0], 0)
        HI1 = e
        names1 = [n for n in order1 if n[0] in ("Ta", "v", "q", "k", "PT", "PV", "Tb", "M")]
        hi1 = {n: j for j, n in enumerate(names1)}
        PERH = len(names1)
        hi2, e = highs([n for n in n2.at if n[0] == "T" or n[1] < STEPS], HI1 + BLOCKS * PERH)
        hi3, e = highs([n for n in n3.at if n[0] in ("T", "Z") or (n[0] == "R" and n[1] == 0)], e)

        x = sb("x", [P, NT, D])
        mask = sb("mask", [P, NT, NODES])
        CT = [sb(f"CT{r}", [P, NT, NODES], I16) for r in range(2)]
        adj = sb("adj", [P, NT, NODES], U8)
        ident = sb("ident", [P, P])
        ones = sb("ones", [P, P])
        sel = sb("sel", [P, 7, P], F32R)
        stk = sb("stk", [P, NODES], F32R)
        bias_rows = sb("bias_rows", [P, D], F32R)
        rowno = sb("rowno", [P, 1], I32)
        minus_odd = sb("minus_odd", [P, 1])
        minus_low = sb("minus_low", [P, 1])
        minus_loww = sb("minus_loww", [P, 1])
        half = sb("half", [P, NT])
        hasedge = sb("hasedge", [P, NT])
        rinv = sb("rinv", [P, NT])
        stats = sb("stats", [P, NT, 6])
        mv = sb("mv", [P, NT, 2])
        ve = sb("ve", [P, NT])
        rstd = sb("rstd", [P, NT])
        pace = sb("pace", [P, 64])
        nmin = sb("nmin", [P, NT])
        rsum = sb("rsum", [P, NT])
        rden = sb("rden", [P, NT])
        dw = sb("dw", [P, STEPS + 1])
        rdw = sb("rdw", [P, STEPS, NT])
        gw = sb("gw", [P, 2, KT, 2])
        gwh = sb("gwh", [P, 2, KT, 2], F32R)
        gwl = sb("gwl", [P, 2, KT, 2], F32R)
        ge = sb("ge", [P, 2 * NT])
        gate = sb("gate", [P, 2 * NT])
        wraw = [sb(f"wraw{s}", [P, KT, D]) for s in range(2)]
        wh = [sb(f"wh{s}", [P, KT, D], F32R) for s in range(3)]
        wl = [sb(f"wl{s}", [P, KT, D], F32R) for s in range(3)]

        cg = ExitStack()
        craw = sb("craw", [P, 2, D], ctx=cg)
        cond = sb("cond", [P, 4, D], F32R, ctx=cg)
        braw = sb("braw", [P, D], ctx=cg)
        brow = sb("brow", [P, D], F32R, ctx=cg)
        ec = ExitStack()
        Araw = sb("Araw", [P, NT, NODES], ctx=ec)
        Csum = sb("Csum", [P, NT, NODES], ctx=ec)
        ec2 = ExitStack()
        eint = sb("eint", [P, 3, P], I32, ctx=ec2)
        ewt = sb("ewt", [P, P], ctx=ec2)
        efl = sb("efl", [P, 3, P], ctx=ec2)
        srcT = sb("srcT", [P, ET], ctx=ec2)
        dstT = sb("dstT", [P, ET], ctx=ec2)
        whiT = sb("whiT", [P, ET], F32R, ctx=ec2)
        wloT = sb("wloT", [P, ET], ctx=ec2)
        isr = [sb(f"isr{r}", [P, ET], ctx=ec2) for r in range(2)]
        iota = sb("iota", [P, NODES], ctx=ec2)
        zero_l = sb("zero_l", [P, P], F32R, ctx=ec2)
        ohs = sb("ohs", [P, 2, GRP, NODES], F32R, ctx=ec2)
        ohd = sb("ohd", [P, 2, GRP, 4, P], F32R, ctx=ec2)
        basis = [sb(f"basis{s}", [P, KT, D], ctx=ec2) for s in range(2)]
        macc = sb("macc", [P, 2, KT * D], ctx=ec2)
        att = sb("att", [P, 2, 2, BASES], ctx=ec2)
        bias_raw = sb("bias_raw", [P, D], ctx=ec2)
        selv = sb("selv", [P, 2, 7, P], ctx=ec2)
        noise = sb("noise", [2 * FREQS, NODES], ctx=ec2)
        rnd = sb("rnd", [2 * FREQS, NODES], ctx=ec2)
        freq = sb("freq", [2 * FREQS, 1], ctx=ec2)
        quarter = sb("quarter", [2 * FREQS, 1], ctx=ec2)
        fw1 = sb("fw1", [2 * FREQS, COND], ctx=ec2)
        fb1 = sb("fb1", [COND, 1], ctx=ec2)
        fw2 = sb("fw2", [COND, P], ctx=ec2)
        cb = sb("cb", [P, 1], ctx=ec2)
        sil = [sb(f"sil{i}", [COND, NODES], ctx=ec2) for i in range(2)]
        ec2.close()
        An_h = sb("An_h", [P, NT, NODES], F32R, ctx=ec)
        An_l = sb("An_l", [P, NT, NODES], F32R, ctx=ec)
        hb_h = [sb(f"hb_h{i}", [P, NT, D], F32R, ctx=ec) for i in range(2)]
        hb_l = [sb(f"hb_l{i}", [P, NT, D], F32R, ctx=ec) for i in range(2)]
        D2 = sb("D2", [P, NODES], ctx=ec)
        xn0 = sb("xn0", [P, NT, D], ctx=ec)
        slope = sb("slope", [P, 2, D], ctx=ec)
        hv = sb("hv", [P, 2, D], ctx=ec)
        dg = sb("dg", [P, 4, NT], ctx=ec)
        diag = sb("diag", [P, NT, P], ctx=ec)
        ec.close()
        c1 = ExitStack()
        xl = sb("xl", [P, NT, D], ctx=c1)
        yp = sb("yp", [P, NT, D], ctx=c1)
        yT_h = sb("yT_h", [P, KT, NODES], F32R, ctx=c1)
        yT_l = sb("yT_l", [P, KT, NODES], F32R, ctx=c1)
        vm_h = sb("vm_h", [P, NT, D], F32R, ctx=c1)
        vm_l = sb("vm_l", [P, NT, D], F32R, ctx=c1)
        qk_h = sb("qk_h", [P, 2, NODES], F32R, ctx=c1)
        qk_l = sb("qk_l", [P, 2, NODES], F32R, ctx=c1)
        PT_h = sb("PT_h", [P, NT, NODES], F32R, ctx=c1)
        PT_l = sb("PT_l", [P, NT, NODES], F32R, ctx=c1)
        oT_h = sb("oT_h", [P, HEADS, NODES], F32R, ctx=c1)
        oT_l = sb("oT_l", [P, HEADS, NODES], F32R, ctx=c1)
        c1.close()
        cc = ExitStack()
        Cskip = sb("Cskip", [P, 2 * NT, NODES], ctx=cc)
        ctmp = [sb(f"ctmp{i}", [P, NODES], ctx=cc) for i in range(4)]
        rowsum = sb("rowsum", [P, 2, NT], ctx=cc)
        cc.close()
        cg.close()
        c2 = ExitStack()
        y2 = sb("y2", [P, NT, D], ctx=c2)
        y2T_h = sb("y2T_h", [P, KT, NODES], F32R, ctx=c2)
        y2T_l = sb("y2T_l", [P, KT, NODES], F32R, ctx=c2)
        adj_r = sb("adj_r", [P, NT, NODES], F32R, ctx=c2)
        cur_h = sb("cur_h", [P, 2, NT, D], F32R, ctx=c2)
        cur_l = sb("cur_l", [P, 2, NT, D], F32R, ctx=c2)
        acc2 = sb("acc2", [P, NT, D], ctx=c2)
        c2.close()
        c3 = ExitStack()
        Z_h = sb("Z_h", [P, 2, NT, D], F32R, ctx=c3)
        Z_l = sb("Z_l", [P, 2, NT, D], F32R, ctx=c3)
        C_h = sb("C_h", [P, 2, NT, NODES], F32R, ctx=c3)
        C_l = sb("C_l", [P, 2, NT, NODES], F32R, ctx=c3)
        hT_h = [sb("hT_h0", [P, KT, NODES], F32R, ctx=c3)]
        hT_l = [sb("hT_l0", [P, KT, NODES], F32R, ctx=c3)]
        c3y = ExitStack()
        y3 = sb("y3", [P, NT, D], ctx=c3y)
        c3y.close()
        hT_h.append(sb("hT_h1", [P, KT, NODES], F32R, ctx=c3))
        hT_l.append(sb("hT_l1", [P, KT, NODES], F32R, ctx=c3))
        c3.close()

        ring = top.enter_context(nc.psum_tensor("ring", [P, RING, 512], F32))
        edge_ps = [ring[:, 4, :], ring[:, 5, :], ring[:, 6, :]]

        const_ready = sem("const_ready")
        const_step = sem("const_step")
        sel_step = sem("sel_step")
        small_loaded = sem("small_loaded")
        x_loaded = sem("x_loaded")
        edges_loaded = sem("edges_loaded")
        tile_ready = sem("tile_ready")
        tile_taken = sem("tile_taken")
        hi_ready = sem("hi_ready")
        table_ready = sem("table_ready")
        whi_ready = sem("whi_ready")
        onehot_ready = sem("onehot_ready")
        onehot_used = sem("onehot_used")
        pass_ready = sem("pass_ready")
        pass_act = sem("pass_act")
        pass_dve = sem("pass_dve")
        basis_loaded = [sem(f"basis_loaded{s}") for s in range(2)]
        basis_used = sem("basis_used")
        mixed = sem("mixed")
        mix_stored = sem("mix_stored")
        emb_step = sem("emb_step")
        emb_act = sem("emb_act")
        deg_step = sem("deg_step")
        deg_act = sem("deg_act")
        deg_pool = sem("deg_pool")
        cnt_step = sem("cnt_step")
        cnt_act = sem("cnt_act")
        weight_loaded = [sem(f"weight_loaded{s}") for s in range(2)]
        weight_hi = sem("weight_hi")
        weight_lo = sem("weight_lo")
        ln_stats = sem("ln_stats")
        ln_mv = sem("ln_mv")
        ln_var = sem("ln_var")
        ln_rstd = sem("ln_rstd")
        ln_xn = sem("ln_xn")
        h0_hi = sem("h0_hi")
        h0_ready = sem("h0_ready")
        slope_ready = sem("slope_ready")
        leaky_ready = sem("leaky_ready")
        xl_ready = sem("xl_ready")
        cond_clear = sem("cond_clear")
        cond_loaded = sem("cond_loaded")
        cond_hi = sem("cond_hi")
        cond_ready = sem("cond_ready")
        braw_loaded = sem("braw_loaded")
        brow_hi = sem("brow_hi")
        brow_ready = sem("brow_ready")
        exp_ready = sem("exp_ready")
        rden_ready = sem("rden_ready")
        probs_ready = sem("probs_ready")
        y_ready = sem("y_ready")
        l2_step = sem("l2_step")
        c_hi = sem("c_hi")
        c_ready = sem("c_ready")
        gate_exp = sem("gate_exp")
        gate_step = sem("gate_step")
        out_stored = sem("out_stored")

        block = top.enter_context(nc.Block())

        def rows(ap):
            return ap.rearrange("(t p) n -> p t n", p=P)

        W1 = 4
        W2 = W1 + 6 * BLOCKS
        W3 = W2 + 1
        slot = lambda w: (w + 2) % 3

        def last_use(w):
            if w < W1:
                return n0.base + n0.at[(("U", "H")[w % 2], w // 2, 3)]
            if w < W2:
                i, j = divmod(w - W1, 6)
                return n1.base + i * PER + n1.at[(("v", "q", "k", "o", "M", "X")[j], 3)]
            if w == W2:
                return n2.base + n2.at[("A", 0, 3)]
            l, j = divmod(w - W3, 3)
            return n3.base + n3.at[("Z", l, j, 3) if j < 2 else ("R", l, 3)]

        @block.sync
        def _(sp):
            for t, d in enumerate((src_d, dst_d, type_d)):
                sp.dma_start(eint[:, t, :], d.rearrange("(t p) -> t p", p=P)).then_inc(edges_loaded, 16)
            sp.dma_start(ewt[:], w_d.rearrange("(t p) -> t p", p=P)).then_inc(edges_loaded, 16)
            sp.dma_start(x[:], rows(x_d)).then_inc(x_loaded, 16)

            def load_weight(w, src, even):
                if not (isinstance(w, int) and w < 2):
                    sp.wait_ge(weight_lo, w - 1)
                sp.dma_start(wraw[even][:], rows(src)).then_inc(weight_loaded[even], 16)

            load_weight(0, l0["W_gcn"][0], 0)
            load_weight(1, l0["W_mlp"][0], 1)
            sp.wait_ge(const_ready, 1)
            n_small = [0]

            def small(dst, src):
                sp.dma_start(dst, src, allow_slow_non_contiguous=True).then_inc(small_loaded, 16)
                n_small[0] += 1

            for l in range(2):
                for r in range(2):
                    small(att[:, l, r, :], l3["att"][l][r:r + 1, :].broadcast_to([P, BASES]))
                    small(gw[:, l, :, r], l3["gate_w"][l][r, :, 0].rearrange("(k p) -> p k", p=P))
            vecs = [l0["b_gcn"][0:1], l0["b_mlp"][0:1], l0["b_gcn"][1:2], l0["b_mlp"][1:2]]
            vecs += [b.rearrange("(a d) -> a d", a=1) for b in (l2["b"], l3["bias"][0], l3["bias"][1])]
            for j, v in enumerate(vecs):
                small(bias_raw[2 * j:2 * j + 2, :], v.broadcast_to([2, D]))
            small(noise[:], noise_d.rearrange("n a -> a n").broadcast_to([2 * FREQS, NODES]))
            small(fw1[:], l1["f_w1"])
            small(fb1[:], l1["f_b1"].rearrange("(c a) -> c a", a=1))
            for g in range(3):
                small(fw2[:, 32 * g:32 * g + COND], l1["f_w2"])
                small(cb[32 * g:32 * g + COND, :], l1["f_b2"].rearrange("(c a) -> c a", a=1))
            small(dw[:], l2["dw"].rearrange("(a d) -> a d", a=1).broadcast_to([P, STEPS + 1]))
            assert n_small[0] == SMALL

            def load_cond(b, n, ready):
                if ready is not None:
                    sp.wait_ge(cond_ready, ready)
                for k in range(2):
                    w_, b_ = l1[("s", "b")[k] + f"{n + 1}_w"], l1[("s", "b")[k] + f"{n + 1}_b"]
                    for g in range(3):
                        sp.dma_start(craw[32 * g:32 * g + COND, k, :],
                                     w_[bass.ds(b, 1)].rearrange("a c d -> (a c) d")).then_inc(cond_loaded, 16)
                    sp.dma_start(craw[96:98, k, :], b_[bass.ds(b, 1)].broadcast_to([2, D])).then_inc(cond_loaded, 16)

            sp.wait_ge(cond_clear, 1)
            load_cond(0, 0, None)
            load_cond(0, 1, 1)

            for l in range(2):
                src = l3["basis"][l]
                with sp.Fori(0, BASES // 2) as q:
                    for s in range(2):
                        sp.wait_ge(basis_used, q * 2 + (BASES * l + s + 1))
                        sp.dma_start(basis[s][:], src[bass.ds(q * 2 + s, 1)].rearrange("a (t p) n -> p (a t) n", p=P)
                                     ).then_inc(basis_loaded[s], 16)
                sp.wait_ge(mixed, 2 * l + 2)
                for r in range(2):
                    sp.dma_start(mix_d[l, r], macc[:, r, :]).then_inc(mix_stored, 16)
            load_weight(2, l0["W_gcn"][1], 0)
            load_weight(3, l0["W_mlp"][1], 1)
            load_weight(W1, l1["wv"][0], 0)
            load_weight(W1 + 1, l1["wq"][0], 1)

            def block_loads(i, nxt, nxt_v, nxt_q):
                sp.wait_ge(brow_ready, i)
                for j, name in enumerate(("bv", "bq", "bk", "bo", "m_b1", "m_b2")):
                    sp.dma_start(braw[2 * j:2 * j + 2, :], l1[name][bass.ds(i, 1)].broadcast_to([2, D])
                                 ).then_inc(braw_loaded, 16)
                w = lambda name: l1[name][bass.ds(i, 1)].rearrange("a k n -> (a k) n")
                load_weight(i * 6 + (W1 + 2), w("wk"), 0)
                load_weight(i * 6 + (W1 + 3), w("wo"), 1)
                load_weight(i * 6 + (W1 + 4), w("m_w1"), 0)
                load_weight(i * 6 + (W1 + 5), w("m_w2"), 1)
                load_cond(nxt, 0, i * 2 + 2)
                load_weight(i * 6 + (W1 + 6), nxt_v, 0)
                load_cond(nxt, 1, i * 2 + 3)
                load_weight(i * 6 + (W1 + 7), nxt_q, 1)

            with sp.Fori(0, BLOCKS - 1) as i:
                nx = lambda name: l1[name][bass.ds(i + 1, 1)].rearrange("a k n -> (a k) n")
                block_loads(i, i + 1, nx("wv"), nx("wq"))
            sp.wait_ge(mix_stored, 64)
            mixw = lambda l, r: mix_d[l, r].rearrange("p (k n) -> p k n", k=KT)
            wsrc = []
            for l in range(2):
                wsrc += [mixw(l, 0), mixw(l, 1), rows(l3["root"][l])]

            def load_last(w, src):
                sp.wait_ge(weight_lo, w - 1)
                sp.dma_start(wraw[w % 2][:], src).then_inc(weight_loaded[w % 2], 16)

            i = BLOCKS - 1
            sp.wait_ge(brow_ready, i)
            for j, name in enumerate(("bv", "bq", "bk", "bo", "m_b1", "m_b2")):
                sp.dma_start(braw[2 * j:2 * j + 2, :], l1[name][i:i + 1].broadcast_to([2, D])).then_inc(braw_loaded, 16)
            for j, name in enumerate(("wk", "wo", "m_w1", "m_w2")):
                load_last(i * 6 + W1 + 2 + j, rows(l1[name][i]))
            load_cond(i, 0, i * 2 + 2)
            load_last(W2, rows(l2["W"]))
            load_cond(i, 1, i * 2 + 3)
            for j in range(6):
                load_last(W3 + j, wsrc[j])
            for t in range(NT):
                sp.wait_ge(tile_taken, n3.base + n3.at[("R", 1, t)] + 1)
                sp.dma_start(out_d[t * P:(t + 1) * P, :], x[:, t, :]).then_inc(out_stored, 16)
            sp.wait_ge(out_stored, 16 * NT)

        @block.gpsimd
        def _(pool):
            g = nc.gpsimd
            for clear in (bias_raw, fw2, cb, craw, braw, ones, half, zero_l, minus_low, minus_loww, ident, quarter):
                v = clear[:].bitcast(F32) if clear is zero_l else clear[:]
                last = g.memset(v, 1.0 if clear is ones else -0.5 if clear is half else 0.0)
            last.then_inc(const_step, 1)
            pool.wait_ge(const_step, 1)
            g.memset(cb[96:99, :], 1.0).then_inc(const_ready, 1)
            pool.wait_ge(const_ready, 1)
            g.affine_select(out=craw[:, 0, :], in_=craw[:, 0, :], compare_op=ALU.not_equal, fill=1.0, base=-98,
                            pattern=[[0, D]], channel_multiplier=1).then_inc(cond_clear, 1)
            pool.wait_ge(cond_clear, 1)
            g.memset(quarter[FREQS:2 * FREQS, :], 0.25).then_inc(const_step, 1)
            pool.wait_ge(const_step, 2)
            g.memset(minus_low[64:96, :], -1.0).then_inc(const_step, 1)
            pool.wait_ge(const_step, 3)
            g.memset(minus_loww[32:64, :], -1.0).then_inc(const_step, 1)
            pool.wait_ge(const_step, 4)
            g.affine_select(out=minus_loww[:], in_=minus_loww[:], compare_op=ALU.not_equal, fill=-1.0, base=-97,
                            pattern=[[0, 1]], channel_multiplier=1)
            g.affine_select(out=ident[:], in_=ident[:], compare_op=ALU.not_equal, fill=1.0, base=0,
                            pattern=[[-1, P]], channel_multiplier=1)
            g.iota(iota[:], [[1, NODES]], base=0, channel_multiplier=0, allow_small_or_imprecise_dtypes=True)
            g.iota(selv[:, 0, :, :], [[-2, 7], [0, P]], base=0, channel_multiplier=1, allow_small_or_imprecise_dtypes=True)
            g.iota(rowno[:], [[0, 1]], base=0, channel_multiplier=1)
            g.iota(freq[0:FREQS, :], [[0, 1]], base=1, channel_multiplier=1, allow_small_or_imprecise_dtypes=True
                   ).then_inc(const_step, 1)
            pool.wait_ge(const_step, 5)
            g.iota(freq[FREQS:2 * FREQS, :], [[0, 1]], base=1, channel_multiplier=1, allow_small_or_imprecise_dtypes=True
                   ).then_inc(const_ready, 1)

            def low_weight(w, s, r):
                pool.wait_ge(weight_hi, w + 1)
                g.tensor_tensor(wl[s][:], wraw[r][:], wh[s][:].bitcast(F32), ALU.subtract).then_inc(weight_lo, 1)

            def inverse_root(n, t):
                pool.wait_ge(ln_var, n + 1)
                g.tensor_tensor(rstd[:, t:t + 1], ve[:, t:t + 1], half[:, 0:1], ALU.pow).then_inc(ln_rstd, 1)

            for w in range(2):
                low_weight(w, slot(w), w % 2)
            for t in range(NT):
                inverse_root(t, t)
            pool.wait_ge(deg_step, 1)
            g.tensor_tensor(dg[:, 2, :], dg[:, 1, :], half[:], ALU.pow).then_inc(deg_pool, 1)
            for w in range(2, W1 + 2):
                low_weight(w, slot(w), w % 2)
            for t in range(NT):
                inverse_root(NT + t, t)
            with pool.Fori(0, BLOCKS) as i:
                for t in range(NT):
                    inverse_root(i * 8 + (8 + t), t)
                for j in (2, 3, 4):
                    low_weight(i * 6 + (W1 + j), j % 3, j % 2)
                for t in range(NT):
                    inverse_root(i * 8 + (12 + t), t)
                for j in (5, 6, 7):
                    low_weight(i * 6 + (W1 + j), j % 3, j % 2)
            low_weight(W3 + 1, slot(W3 + 1), (W3 + 1) % 2)
            for t in range(NT):
                inverse_root(40 + t, t)
            low_weight(W3 + 2, slot(W3 + 2), (W3 + 2) % 2)
            for t in range(NT):
                inverse_root(44 + t, t)
            for w in range(W3 + 3, W3 + 6):
                low_weight(w, slot(w), w % 2)

        @block.scalar
        def _(act):
            a = nc.scalar

            def high_weight(w, s, r, half_w, freed):
                act.wait_ge(weight_loaded[r], half_w * 16 + 16)
                if freed is not None:
                    act.wait_ge(tile_ready, freed)
                a.activation(wh[s][:], wraw[r][:], ACT.Copy).then_inc(weight_hi, 1)

            def hw(w):
                high_weight(w, slot(w), w % 2, w // 2, last_use(w - 3) + 1 if w >= 3 else None)

            def bank(T, name):
                return ring[:, T.bank(name), :]

            def high(T, base, name, out, func=ACT.Copy, **kw):
                act.wait_ge(tile_ready, base + (T.at[name] + 1))
                src = bank(T, name)
                if len(out.shape) == 3:
                    src = src.rearrange("p (a b) -> p a b", a=out.shape[1])
                a.activation(out, src, func, **kw).then_inc(hi_ready, 1)

            act.wait_ge(emb_step, 4)
            a.activation(rnd[:], noise[:], ACT.Sin, scale=TURN).then_inc(emb_act, 1)
            act.wait_ge(tile_ready, pre.base + pre.at["tab"] + 1)
            a.activation(whiT[:], ring[:, pre.bank("tab"), 3 * P:4 * P], ACT.Copy).then_inc(whi_ready, 1)
            act.wait_ge(tile_taken, pre.base + pre.at["z1"] + 1)
            a.activation(sil[0][:], sil[1][:], ACT.Exp, scale=-1.0).then_inc(emb_act, 1)
            hw(0)
            hw(1)
            for m in range(NT):
                act.wait_ge(pass_ready, m + 1)
                a.activation(CT[0][:, m, :], edge_ps[1], ACT.Copy).then_inc(pass_act, 1)
                a.activation(Araw[:, m, :], edge_ps[0], ACT.Copy).then_inc(pass_act, 1)

            for t in range(NT):
                act.wait_ge(ln_xn, t + 1)
                a.activation(hb_h[0][:, t, :], xn0[:, t, :], ACT.Relu).then_inc(h0_hi, 1)
            for m in range(NT):
                act.wait_ge(deg_step, 7 + m)
                a.activation(An_h[:, m, :], Araw[:, m, :], ACT.Copy).then_inc(deg_act, 1)
            for l in range(2):
                g_, u_ = hb_h[1 - l], hb_h[l]
                for m in range(KT):
                    high(n0, n0.base, ("G", l, m), g_[:, m, :])
                hw((2, 4)[l])
                for m in range(KT):
                    high(n0, n0.base, ("U", l, m), u_[:, m, :])
                hw((3, 5)[l])
                for t in range(NT):
                    act.wait_ge(tile_ready, n0.base + n0.at[("H", l, t)] + 1)
                    if t >= 2 or l:
                        act.wait_ge(leaky_ready, 4 * l + t - 1)
                    a.activation(slope[:, t % 2, :], bank(n0, ("H", l, t)), ACT.Copy, scale=0.01).then_inc(slope_ready, 1)
                    if l == 0:
                        act.wait_ge(leaky_ready, t + 1)
                        a.activation(hb_h[1][:, t, :], hv[:, t % 2, :], ACT.Copy).then_inc(hi_ready, 1)

            for j in range(NT):
                act.wait_ge(cnt_step, CNT * j + 2)
                a.activation(ctmp[3][:], ctmp[1][:], ACT.Ln).then_inc(cnt_act, 1)

            with act.Fori(0, BLOCKS) as i:
                b = i * PER + n1.base

                def hi(name, out, func=ACT.Copy):
                    high(n1, b, name, out, func)

                def hwi(j, freed):
                    high_weight(None, j % 3, j % 2, i * 3 + (W1 // 2 + j // 2), freed)

                def after(name):
                    return b + (n1.at[name] + 1)

                def exps(h):
                    for j in range(NT):
                        act.wait_ge(tile_taken, after(("s", h, j)))
                        a.activation(yp[:, j, :], yp[:, j, :], ACT.Exp, bias=nmin[:, j:j + 1], scale=-1.0,
                                     accum_out=rsum[:, j:j + 1]).then_inc(exp_ready, 1)

                def attend(h):
                    for m in range(NT):
                        hi(("PT", h, m), PT_h[:, m, :])
                    hi(("PV", h), oT_h[:, h, :])

                hwi(2, b)
                for t in range(NT):
                    if t:
                        hi(("v", t - 1), vm_h[:, t - 1, :])
                    hi(("Ta", t), yT_h[:, :, t * P:(t + 1) * P])
                hi(("v", NT - 1), vm_h[:, NT - 1, :])
                for h in range(HEADS):
                    hi(("q", h), qk_h[:, 0, :])
                    hi(("k", h), qk_h[:, 1, :])
                    if h == 0:
                        hwi(3, after(("v", NT - 1)))
                    if h:
                        attend(h - 1)
                    exps(h)
                hwi(4, after(("q", HEADS - 1)))
                attend(HEADS - 1)
                hwi(5, after(("k", HEADS - 1)))
                for t in range(NT):
                    hi(("Tb", t), yT_h[:, :, t * P:(t + 1) * P])
                hwi(6, after(("o", NT - 1)))
                for m in range(KT):
                    hi(("M", m), vm_h[:, m, :], ACT.Relu)
                hwi(7, after(("M", KT - 1)))

            hw(W3 + 1)
            for t in range(NT):
                high(n2, n2.base, ("T", t), y2T_h[:, :, t * P:(t + 1) * P])
            for t in range(NT):
                high(n2, n2.base, ("A", 0, t), cur_h[:, 0, t, :])
            hw(W3 + 2)
            for k in range(1, STEPS):
                for t in range(NT):
                    high(n2, n2.base, ("A", k, t), cur_h[:, k % 2, t, :], ACT.Identity, scale=rinv[:, t:t + 1])

            act.wait_ge(y_ready, 2 * NT)
            for r in range(2):
                a.activation(C_h[:, r, :, :], CT[r][:], ACT.Copy).then_inc(c_hi, 1)
            for t in range(NT):
                high(n3, n3.base, ("T", t), hT_h[0][:, :, t * P:(t + 1) * P])
            for l in range(2):
                act.wait_ge(tile_ready, n3.base + n3.at[("g", l)] + 1)
                a.activation(ge[:], ring[:, n3.bank(("g", l)), 0:2 * NT], ACT.Exp, scale=-1.0).then_inc(gate_exp, 1)
                act.wait_ge(gate_step, l + 1)
                for r in range(2):
                    for t in range(NT):
                        high(n3, n3.base, ("Z", l, r, t), Z_h[:, r, t, :], ACT.Identity,
                             scale=gate[:, 2 * t + r:2 * t + r + 1])
                    if l == 0:
                        hw(W3 + 3 + r)
                if l == 0:
                    for m in range(KT):
                        high(n3, n3.base, ("R", 0, m), hT_h[1][:, m, :], ACT.Relu)
                    hw(W3 + 5)

        @block.vector
        def _(dve):
            v = nc.vector

            def f(ap):
                return ap.bitcast(F32)

            def bank(T, name):
                return ring[:, T.bank(name), :]

            def ready(T, base, name):
                dve.wait_ge(tile_ready, base + (T.at[name] + 1))

            def taken(T, base, name):
                dve.wait_ge(tile_taken, base + (T.at[name] + 1))

            def low(T, base, name, hi_count, out, hi, func=None, scalar=None):
                dve.wait_ge(hi_ready, hi_count + 1)
                src = bank(T, name)
                if len(out.shape) == 3:
                    src = src.rearrange("p (a b) -> p a b", a=out.shape[1])
                if func is None:
                    v.tensor_tensor(out, src, f(hi), ALU.subtract).then_inc(tile_taken, 1)
                else:
                    v.scalar_tensor_tensor(out, src, scalar, f(hi), func, ALU.subtract).then_inc(tile_taken, 1)

            holds = [0]

            def hold():
                v.memset(pace[:, holds[0]:holds[0] + 1], 0.0)
                holds[0] += 1

            def norm_stats(src, t, n):
                v.bn_stats(stats[:, t, :], src).then_inc(ln_stats, 1)
                dve.wait_ge(ln_stats, n + 1)
                hold()
                v.bn_aggr(mv[:, t, :], stats[:, t, :]).then_inc(ln_mv, 1)
                dve.wait_ge(ln_mv, n + 1)
                v.tensor_scalar(ve[:, t:t + 1], mv[:, t, 1:2], EPS, None, ALU.add).then_inc(ln_var, 1)

            def normalise(out, src, t, n):
                dve.wait_ge(ln_rstd, n + 1)
                v.tensor_scalar(out, src, mv[:, t, 0:1], rstd[:, t:t + 1], ALU.subtract, ALU.mult).then_inc(ln_xn, 1)

            dve.wait_ge(const_ready, 2)
            v.tensor_scalar(selv[:, 1, :, :], selv[:, 0, :, :], 0.0, None, ALU.is_ge).then_inc(sel_step, 1)
            dve.wait_ge(sel_step, 1)
            v.scalar_tensor_tensor(sel[:].rearrange("p a b -> p (a b)"), selv[:, 0, :, :].rearrange("p a b -> p (a b)"), 1.0,
                                   selv[:, 1, :, :].rearrange("p a b -> p (a b)"), ALU.is_le, ALU.mult).then_inc(sel_step, 1)
            v.tensor_scalar(rowno[:], rowno[:], 1, None, ALU.bitwise_and).then_inc(sel_step, 1)
            dve.wait_ge(sel_step, 3)
            v.tensor_scalar(minus_odd[:], rowno[:], -1.0, None, ALU.mult).then_inc(sel_step, 1)
            dve.wait_ge(edges_loaded, 64)
            v.tensor_copy(efl[:], eint[:]).then_inc(table_ready, 1)
            dve.wait_ge(small_loaded, 16 * SMALL)
            v.tensor_copy(bias_rows[:], bias_raw[:]).then_inc(sel_step, 1)
            v.tensor_copy(gwh[:], gw[:]).then_inc(sel_step, 1)
            dve.wait_ge(sel_step, 6)
            v.scalar_tensor_tensor(bias_rows[:], f(bias_rows[:]), minus_odd[:], bias_raw[:], ALU.mult, ALU.add).then_inc(sel_step, 1)
            v.tensor_tensor(gwl[:], gw[:], f(gwh[:]), ALU.subtract).then_inc(sel_step, 1)

            v.tensor_scalar(noise[:], noise[:], freq[:], 1.0 / PERIOD, ALU.mult, ALU.mult).then_inc(emb_step, 1)
            dve.wait_ge(emb_step, 1)
            v.tensor_scalar(noise[:], noise[:], quarter[:], None, ALU.add).then_inc(emb_step, 1)
            dve.wait_ge(emb_step, 2)
            v.tensor_scalar(rnd[:], noise[:], MAGIC, MAGIC, ALU.add, ALU.subtract).then_inc(emb_step, 1)
            dve.wait_ge(emb_step, 3)
            v.tensor_tensor(noise[:], noise[:], rnd[:], ALU.subtract).then_inc(emb_step, 1)
            dve.wait_ge(whi_ready, 1)
            tab = bank(pre, "tab")
            v.tensor_copy(srcT[:], tab[:, 0:P])
            v.tensor_copy(dstT[:], tab[:, P:2 * P])
            v.tensor_scalar(isr[0][:], tab[:, 2 * P:3 * P], 0.0, None, ALU.is_equal)
            v.tensor_scalar(isr[1][:], tab[:, 2 * P:3 * P], 0.0, None, ALU.not_equal).then_inc(table_ready, 1)
            v.tensor_tensor(wloT[:], tab[:, 3 * P:4 * P], f(whiT[:]), ALU.subtract).then_inc(tile_taken, 1)
            ready(pre, pre.base, "z1")
            v.tensor_scalar(sil[1][:], bank(pre, "z1")[0:COND, :], fb1[:], None, ALU.add).then_inc(tile_taken, 1)
            dve.wait_ge(emb_act, 2)
            v.tensor_scalar(sil[0][:], sil[0][:], 1.0, None, ALU.add).then_inc(emb_step, 1)
            dve.wait_ge(emb_step, 5)
            v.reciprocal(sil[0][:], sil[0][:]).then_inc(emb_step, 1)
            dve.wait_ge(emb_step, 6)
            v.tensor_tensor(sil[0][:], sil[0][:], sil[1][:], ALU.mult).then_inc(emb_step, 1)
            ready(pre, pre.base, "z2")
            v.tensor_scalar(xn_c := macc[:, 0, 0:NODES], bank(pre, "z2"), cb[:], None, ALU.add).then_inc(tile_taken, 1)
            taken(pre, pre.base, "z2")
            v.tensor_copy(stk[:], xn_c).then_inc(emb_step, 1)
            dve.wait_ge(emb_step, 8)
            v.scalar_tensor_tensor(stk[:], f(stk[:]), minus_low[:], xn_c, ALU.mult, ALU.add).then_inc(emb_step, 1)

            def split_cond(n, count):
                dve.wait_ge(cond_loaded, count * 128 + 128)
                v.tensor_copy(cond[:, 2 * n:2 * n + 2, :], craw[:]).then_inc(cond_hi, 1)
                dve.wait_ge(cond_hi, count + 1)
                v.scalar_tensor_tensor(cond[:, 2 * n:2 * n + 2, :], f(cond[:, 2 * n:2 * n + 2, :]), minus_loww[:], craw[:],
                                       ALU.mult, ALU.add).then_inc(cond_ready, 1)

            split_cond(0, 0)
            split_cond(1, 1)

            dve.wait_ge(emb_step, 9)
            v.memset(macc[:], 0.0).then_inc(mixed, 1)
            v.engine_nop().then_inc(basis_used, 2)
            dve.wait_ge(mixed, 1)
            dve.wait_ge(table_ready, 2)
            dve.wait_ge(tile_taken, pre.base + 1)
            BODY = 8
            TURNS = ET // GRP // BODY

            def onehots(m, q, u):
                n = q * BODY + u
                dve.wait_ge(onehot_used, n + (m * (ET // GRP) + 1))
                for k in range(GRP):
                    e = bass.ds(n * GRP + k, 1)
                    s = u % 2
                    v.tensor_scalar(ohs[:, s, k, :], iota[:], srcT[:, e], None, ALU.is_equal)
                    cols = iota[:, m * P:(m + 1) * P]
                    for r, val in enumerate((f(whiT[:, e]), wloT[:, e], isr[0][:, e], isr[1][:, e])):
                        last = v.tensor_scalar(ohd[:, s, k, r, :], cols, dstT[:, e], val, ALU.is_equal, ALU.mult)
                last.then_inc(onehot_ready, 1)

            def mix(l, first, q, s, r):
                b = q * 2 + (first + s)
                if r == 0:
                    dve.wait_ge(basis_loaded[s], q * 16 + (BASES * l + first) // 2 * 16 + 16)
                dve.wait_ge(basis_used, b + (BASES * l + 2))
                ins = v.scalar_tensor_tensor(macc[:, r, :], basis[s][:].rearrange("p a b -> p (a b)"), att[:, l, r, bass.ds(b, 1)],
                                             macc[:, r, :], ALU.mult, ALU.add)
                if r == 1:
                    ins.then_inc(basis_used, 1)

            def turn(m, q, with_mix):
                for u in range(BODY):
                    onehots(m, q, u)
                    if with_mix and u % 2:
                        mix(m // 2, (m % 2) * 2 * TURNS, q, u // 4, (u // 2) % 2)

            for m in range(NT):
                bases = min(BASES - (m % 2) * 2 * TURNS, 2 * TURNS)
                with dve.Fori(0, bases // 2) as q:
                    turn(m, q, True)
                for q in range(bases // 2, TURNS):
                    turn(m, q, False)
                dve.wait_ge(pass_ready, m + 1)
                v.tensor_copy(CT[1][:, m, :], edge_ps[2])
                dve.wait_ge(pass_act, 2 * m + 1)
                v.tensor_tensor(Csum[:, m, :], edge_ps[2], CT[0][:, m, :], ALU.add).then_inc(pass_dve, 1)
                if m % 2:
                    l = m // 2
                    dve.wait_ge(basis_used, BASES * (l + 1) + 2)
                    v.engine_nop().then_inc(mixed, 1)
                    dve.wait_ge(mix_stored, 32 * (l + 1))
                    if l == 0:
                        v.memset(macc[:], 0.0).then_inc(mixed, 1)
                        dve.wait_ge(mixed, 3)

            dve.wait_ge(x_loaded, 16)
            for t in range(NT):
                norm_stats(x[:, t, :], t, t)
            for t in range(NT):
                normalise(xn0[:, t, :], x[:, t, :], t, t)
            ready(mid, mid.base, "deg")
            v.tensor_copy(dg[:, 0, :], bank(mid, "deg")[:, 0:2 * NT:2]).then_inc(tile_taken, 1)
            taken(mid, mid.base, "deg")
            v.tensor_scalar(dg[:, 1, :], dg[:, 0, :], 1e-37, None, ALU.max).then_inc(deg_step, 1)
            for t in range(NT):
                dve.wait_ge(h0_hi, t + 1)
                v.scalar_tensor_tensor(hb_l[0][:, t, :], xn0[:, t, :], 0.0, f(hb_h[0][:, t, :]), ALU.max, ALU.subtract).then_inc(h0_ready, 1)
            dve.wait_ge(deg_pool, 1)
            v.scalar_tensor_tensor(dg[:, 3, :], dg[:, 0, :], 0.0, dg[:, 2, :], ALU.is_gt, ALU.mult).then_inc(deg_step, 1)
            dve.wait_ge(deg_step, 2)
            for j in range(NT):
                v.tensor_scalar(diag[:, j, :], ident[:], dg[:, 3, j:j + 1], None, ALU.mult).then_inc(deg_step, 1)
            ready(mid, mid.base, "dinv")
            v.tensor_copy(D2[:], bank(mid, "dinv")).then_inc(tile_taken, 1)
            taken(mid, mid.base, "dinv")
            dve.wait_ge(pass_act, 2 * NT)
            for m in range(NT):
                v.scalar_tensor_tensor(Araw[:, m, :], Araw[:, m, :], dg[:, 3, m:m + 1], D2[:], ALU.mult, ALU.mult).then_inc(deg_step, 1)
            for m in range(NT):
                dve.wait_ge(deg_act, m + 1)
                v.tensor_tensor(An_l[:, m, :], Araw[:, m, :], f(An_h[:, m, :]), ALU.subtract).then_inc(deg_step, 1)

            for l in range(2):
                gb, ub = 1 - l, l
                for m in range(KT):
                    low(n0, n0.base, ("G", l, m), hi0[("G", l, m)], hb_l[gb][:, m, :], hb_h[gb][:, m, :])
                for m in range(KT):
                    low(n0, n0.base, ("U", l, m), hi0[("U", l, m)], hb_l[ub][:, m, :], hb_h[ub][:, m, :])
                for t in range(NT):
                    dve.wait_ge(slope_ready, 4 * l + t + 1)
                    v.tensor_tensor(hv[:, t % 2, :], bank(n0, ("H", l, t)), slope[:, t % 2, :], ALU.max).then_inc(leaky_ready, 1)
                    dve.wait_ge(leaky_ready, 4 * l + t + 1)
                    if l == 0:
                        dve.wait_ge(hi_ready, hi0[("H", 0, t)] + 1)
                        v.tensor_tensor(hb_l[1][:, t, :], hv[:, t % 2, :], f(hb_h[1][:, t, :]), ALU.subtract).then_inc(tile_taken, 1)
                    else:
                        v.tensor_tensor(x[:, t, :], x[:, t, :], hv[:, t % 2, :], ALU.add).then_inc(tile_taken, 1)

            step = [0]

            def counted(ins):
                step[0] += 1
                ins.then_inc(cnt_step, 1)
                return step[0]

            for j in range(NT):
                ready(cnt, cnt.base, ("C", j))
                if j:
                    dve.wait_ge(cnt_step, CNT * j)
                C = bank(cnt, ("C", j))
                counted(v.tensor_scalar(ctmp[0][:], C, 0.0, NOEDGE, ALU.is_equal, ALU.mult))
                counted(v.tensor_scalar(ctmp[1][:], C, 1.0, None, ALU.max))
                top_c = counted(v.reduce_max(rowsum[:, 1, j:j + 1], C, AX.X))
                v.tensor_tensor(ctmp[2][:], C, Csum[:, j, :], ALU.add).then_inc(tile_taken, 1)
                dve.wait_ge(cnt_step, top_c)
                counted(v.tensor_scalar(hasedge[:, j:j + 1], rowsum[:, 1, j:j + 1], 1.0, None, ALU.min))
                taken(cnt, cnt.base, ("C", j))
                one = counted(v.tensor_scalar(ctmp[2][:], ctmp[2][:], 1.0, None, ALU.min))
                dve.wait_ge(cnt_step, one)
                d = ctmp[2][:, j * P:(j + 1) * P]
                loop = counted(v.tensor_tensor(d, d, ident[:], ALU.add))
                dve.wait_ge(cnt_step, loop)
                total = counted(v.reduce_sum(rowsum[:, 0, j:j + 1], ctmp[2][:], AX.X))
                counted(v.tensor_copy(adj[:, j, :], ctmp[2][:]))
                dve.wait_ge(cnt_step, total)
                counted(v.reciprocal(rinv[:, j:j + 1], rowsum[:, 0, j:j + 1]))
                dve.wait_ge(cnt_act, j + 1)
                counted(v.scalar_tensor_tensor(mask[:, j, :], ctmp[3][:], 1.0 / SCALE, ctmp[0][:], ALU.mult, ALU.add))
                assert step[0] == CNT * (j + 1)
            dve.wait_ge(cnt_step, CNT * NT)
            for k in range(STEPS):
                v.tensor_scalar(rdw[:, k, :], rinv[:], dw[:, k + 1:k + 2], None, ALU.mult).then_inc(l2_step, 1)

            for t in range(NT):
                norm_stats(x[:, t, :], t, NT + t)
            for t in range(NT):
                normalise(xl[:, t, :], x[:, t, :], t, NT + t)
                dve.wait_ge(ln_xn, NT + t + 1)
                v.tensor_scalar(xl[:, t, :], xl[:, t, :], 0.0, None, ALU.max).then_inc(xl_ready, 1)
            dve.wait_ge(xl_ready, NT)

            with dve.Fori(0, BLOCKS) as i:
                b = i * PER + n1.base
                hb = i * PERH + HI1

                def lo(name, out, hi, **kw):
                    low(n1, b, name, hb + hi1[name], out, hi, **kw)

                def stats_of(s, t):
                    if s == "a":
                        dve.wait_ge(tile_taken, b + (n1.at[("X", t)] + 1 - PER))
                    norm_stats(xl[:, t, :], t, i * 8 + (8 + 4 * "ab".index(s) + t))

                def conditioned(s, t):
                    n = i * 8 + (8 + 4 * "ab".index(s) + t)
                    normalise(yp[:, t, :], xl[:, t, :], t, n)
                    dve.wait_ge(ln_xn, n + 1)
                    ready(n1, b, ("S" + s, t))
                    v.tensor_tensor(yp[:, t, :], yp[:, t, :], bank(n1, ("S" + s, t)), ALU.mult).then_inc(tile_taken, 1)
                    taken(n1, b, ("S" + s, t))
                    ready(n1, b, ("B" + s, t))
                    v.tensor_tensor(yp[:, t, :], yp[:, t, :], bank(n1, ("B" + s, t)), ALU.add).then_inc(tile_taken, 1)

                def transposed(s, t):
                    c = slice(t * P, (t + 1) * P)
                    lo(("T" + s, t), yT_l[:, :, c], yT_h[:, :, c])

                def value(t):
                    lo(("v", t), vm_l[:, t, :], vm_h[:, t, :])

                def residual(name, t):
                    ready(n1, b, (name, t))
                    v.tensor_tensor(xl[:, t, :], xl[:, t, :], bank(n1, (name, t)), ALU.add).then_inc(tile_taken, 1)

                def masked(h, j):
                    ready(n1, b, ("s", h, j))
                    hold()
                    v.tensor_tensor_reduce(out=yp[:, j, :], in0=bank(n1, ("s", h, j)), in1=mask[:, j, :], scale=-SCALE,
                                           scalar=3e38, op0=ALU.add, op1=ALU.min,
                                           accum_out=nmin[:, j:j + 1]).then_inc(tile_taken, 1)

                def probs(h, j):
                    n = i * 16 + (4 * h + j + 1)
                    dve.wait_ge(exp_ready, n)
                    v.reciprocal(rden[:, j:j + 1], rsum[:, j:j + 1]).then_inc(rden_ready, 1)
                    dve.wait_ge(rden_ready, n)
                    v.tensor_scalar(yp[:, j, :], yp[:, j, :], rden[:, j:j + 1], hasedge[:, j:j + 1], ALU.mult,
                                    ALU.mult).then_inc(probs_ready, 1)

                def attend(h):
                    for m in range(NT):
                        lo(("PT", h, m), PT_l[:, m, :], PT_h[:, m, :])
                    lo(("PV", h), oT_l[:, h, :], oT_h[:, h, :])

                stats_of("a", 0)
                stats_of("a", 1)
                conditioned("a", 0)
                stats_of("a", 2)
                conditioned("a", 1)
                transposed("a", 0)
                stats_of("a", 3)
                conditioned("a", 2)
                dve.wait_ge(braw_loaded, i * 96 + 96)
                v.tensor_copy(brow[:], braw[:]).then_inc(brow_hi, 1)
                dve.wait_ge(brow_hi, i + 1)
                v.scalar_tensor_tensor(brow[:], f(brow[:]), minus_odd[:], braw[:], ALU.mult, ALU.add).then_inc(brow_ready, 1)
                value(0)
                transposed("a", 1)
                conditioned("a", 3)
                value(1)
                transposed("a", 2)
                value(2)
                transposed("a", 3)
                value(3)
                for h in range(HEADS):
                    lo(("q", h), qk_l[:, 0, :], qk_h[:, 0, :])
                    if h:
                        probs(h - 1, NT - 1)
                    lo(("k", h), qk_l[:, 1, :], qk_h[:, 1, :])
                    if h:
                        attend(h - 1)
                    masked(h, 0)
                    for j in range(1, NT):
                        masked(h, j)
                        probs(h, j - 1)
                probs(HEADS - 1, NT - 1)
                attend(HEADS - 1)
                for t in range(NT):
                    residual("o", t)
                    taken(n1, b, ("o", t))
                    stats_of("b", t)
                    conditioned("b", t)
                    if t:
                        transposed("b", t - 1)
                transposed("b", NT - 1)
                split_cond(0, i * 2 + 2)
                for m in range(KT):
                    lo(("M", m), vm_l[:, m, :], vm_h[:, m, :], func=ALU.max, scalar=0.0)
                split_cond(1, i * 2 + 3)
                for t in range(NT):
                    residual("X", t)

            dve.wait_ge(tile_taken, n2.base)
            for t in range(NT):
                v.tensor_tensor(x[:, t, :], x[:, t, :], xl[:, t, :], ALU.add).then_inc(l2_step, 1)
            for t in range(NT):
                dve.wait_ge(l2_step, STEPS + t + 1)
                norm_stats(x[:, t, :], t, 40 + t)
            for t in range(NT):
                normalise(y2[:, t, :], x[:, t, :], t, 40 + t)
                dve.wait_ge(ln_xn, 40 + t + 1)
                v.tensor_scalar(y2[:, t, :], y2[:, t, :], 0.0, None, ALU.max).then_inc(y_ready, 1)
            v.tensor_copy(adj_r[:], adj[:]).then_inc(l2_step, 1)
            for t in range(NT):
                c = slice(t * P, (t + 1) * P)
                low(n2, n2.base, ("T", t), hi2[("T", t)], y2T_l[:, :, c], y2T_h[:, :, c])
            base = STEPS + NT + 1
            for t in range(NT):
                dve.wait_ge(hi_ready, hi2[("A", 0, t)] + 1)
                v.tensor_scalar(acc2[:, t, :], bank(n2, ("A", 0, t)), dw[:, 0:1], None, ALU.mult).then_inc(l2_step, 1)
                low(n2, n2.base, ("A", 0, t), hi2[("A", 0, t)], cur_l[:, 0, t, :], cur_h[:, 0, t, :])
            for k in range(1, STEPS + 1):
                for t in range(NT):
                    name = ("A", k, t)
                    if k < STEPS:
                        dve.wait_ge(hi_ready, hi2[name] + 1)
                    else:
                        ready(n2, n2.base, name)
                    dve.wait_ge(l2_step, base + 4 * (k - 1) + t + 1)
                    ins = v.scalar_tensor_tensor(acc2[:, t, :], bank(n2, name), rdw[:, k - 1, t:t + 1], acc2[:, t, :], ALU.mult, ALU.add)
                    if k < STEPS:
                        ins.then_inc(l2_step, 1)
                        low(n2, n2.base, name, hi2[name], cur_l[:, k % 2, t, :], cur_h[:, k % 2, t, :], func=ALU.mult,
                            scalar=rinv[:, t:t + 1])
                    else:
                        ins.then_inc(tile_taken, 1)
            for t in range(NT):
                taken(n2, n2.base, ("A", STEPS, t))
                v.scalar_tensor_tensor(x[:, t, :], acc2[:, t, :], 0.0, x[:, t, :], ALU.max, ALU.add).then_inc(l2_step, 1)

            base += 4 * STEPS
            for t in range(NT):
                dve.wait_ge(l2_step, base + t + 1)
                norm_stats(x[:, t, :], t, 44 + t)
            for t in range(NT):
                normalise(y3[:, t, :], x[:, t, :], t, 44 + t)
                dve.wait_ge(ln_xn, 44 + t + 1)
                v.tensor_scalar(y3[:, t, :], y3[:, t, :], 0.0, None, ALU.max).then_inc(y_ready, 1)
            for t in range(NT):
                c = slice(t * P, (t + 1) * P)
                low(n3, n3.base, ("T", t), hi3[("T", t)], hT_l[0][:, :, c], hT_h[0][:, :, c])
            for r in range(2):
                dve.wait_ge(c_hi, r + 1)
                v.tensor_tensor(C_l[:, r, :, :], CT[r][:], f(C_h[:, r, :, :]), ALU.subtract).then_inc(c_ready, 1)
            for l in range(2):
                dve.wait_ge(gate_exp, l + 1)
                v.tensor_scalar(gate[:], ge[:], 1.0, None, ALU.add).then_inc(tile_taken, 1)
                taken(n3, n3.base, ("g", l))
                v.reciprocal(gate[:], gate[:]).then_inc(gate_step, 1)
                dve.wait_ge(gate_step, l + 1)
                for r in range(2):
                    for t in range(NT):
                        name = ("Z", l, r, t)
                        low(n3, n3.base, name, hi3[name], Z_l[:, r, t, :], Z_h[:, r, t, :], func=ALU.mult,
                            scalar=gate[:, 2 * t + r:2 * t + r + 1])
                for t in range(NT):
                    name = ("R", l, t)
                    if l == 0:
                        low(n3, n3.base, name, hi3[name], hT_l[1][:, t, :], hT_h[1][:, t, :], func=ALU.max, scalar=0.0)
                    else:
                        ready(n3, n3.base, name)
                        v.tensor_tensor(x[:, t, :], x[:, t, :], bank(n3, name), ALU.add).then_inc(tile_taken, 1)

        @block.tensor
        def _(pe):
            te = nc.tensor

            def begin(T, base, name):
                j = T.at[name]
                if j >= RING or not isinstance(base, int):
                    pe.wait_ge(tile_taken, base + (j - RING + 1))
                elif j == 0:
                    pe.wait_ge(tile_taken, base)
                return ring[:, T.bank(name), :]

            def taken(T, base, name):
                pe.wait_ge(tile_taken, base + (T.at[name] + 1))

            def multiply(out, pairs):
                for n, (l, r) in enumerate(pairs):
                    last = te.matmul(out, l, r, start=n == 0, stop=n == len(pairs) - 1)
                return last

            def three(lh, ll, rh, rl):
                return [(lh, rh), (lh, rl), (ll, rh)]

            def cols(ap, k, m):
                return ap[:, k, m * P:(m + 1) * P]

            def bias_to_rows(j, rows_ap):
                return (sel[:, j, :], rows_ap[:])

            def bias_to_columns(j, rows_ap, m):
                return (rows_ap[:, m * P:(m + 1) * P], sel[:, j:j + 1, :].broadcast_to([P, NT, P]))

            def transposes(out, ins):
                for n, ap in enumerate(ins):
                    last = te.transpose(out[:, n * P:(n + 1) * P], ap, ident[:])
                return last

            pe.wait_ge(const_ready, 2)
            pe.wait_ge(edges_loaded, 64)
            pe.wait_ge(table_ready, 1)
            out = ring[:, pre.bank("tab"), :]
            transposes(out, [efl[:, 0, :], efl[:, 1, :], efl[:, 2, :], ewt[:]]).then_inc(tile_ready, 1)
            pe.wait_ge(small_loaded, 16 * SMALL)
            pe.wait_ge(emb_act, 1)
            te.matmul(ring[0:COND, pre.bank("z1"), :], fw1[:], rnd[:], start=True, stop=True).then_inc(tile_ready, 1)
            pe.wait_ge(emb_step, 7)
            te.matmul(ring[:, pre.bank("z2"), :], fw2[:], sil[0][:], start=True, stop=True).then_inc(tile_ready, 1)

            zeros = zero_l[:].unsqueeze(1).broadcast_to([P, NODES // P, P])
            BODY = 8
            TURNS = ET // GRP // BODY
            for m in range(NT):
                if m:
                    pe.wait_ge(pass_act, 2 * m)
                    pe.wait_ge(pass_dve, m)
                for n, ps in enumerate(edge_ps):
                    last = te.matmul(ps, zero_l[:], zeros, start=True, stop=False)
                if m == 0:
                    last.then_inc(onehot_used, 2)
                with pe.Fori(0, TURNS) as q:
                    for u in range(BODY):
                        pe.wait_ge(onehot_ready, q * BODY + (m * (ET // GRP) + u + 1))
                        for k in range(GRP):
                            s = u % 2
                            for r, ps in enumerate((edge_ps[0], edge_ps[0], edge_ps[1], edge_ps[2])):
                                last = te.matmul(ps, ohd[:, s, k, r, :], ohs[:, s, k, :], start=False, stop=False)
                        last.then_inc(onehot_used, 1)
                for ps in edge_ps:
                    last = te.matmul(ps, zero_l[:], zeros, start=False, stop=True)
                last.then_inc(pass_ready, 1)

            pe.wait_ge(pass_act, 2 * NT)
            pe.wait_ge(pass_dve, NT)
            out = begin(mid, mid.base, "deg")
            for j in range(NT):
                last = multiply(out[:, 2 * j:2 * j + 2], [(cols(Araw, m, j), ones[:, 0:2]) for m in range(NT)])
            last.then_inc(tile_ready, 1)
            pe.wait_ge(deg_step, 2 + NT)
            out = begin(mid, mid.base, "dinv")
            for j in range(NT):
                last = te.matmul(out[:, j * P:(j + 1) * P], ones[:], diag[:, j, :], start=True, stop=True)
            last.then_inc(tile_ready, 1)

            pe.wait_ge(sel_step, 8)
            pe.wait_ge(deg_step, 2 + 3 * NT)
            pe.wait_ge(h0_ready, NT)
            for l in range(2):
                B = n0.base
                hh, hl, gh, gl, uh, ul = hb_h[l], hb_l[l], hb_h[1 - l], hb_l[1 - l], hb_h[l], hb_l[l]
                if l:
                    taken(n0, B, ("H", 0, NT - 1))
                for m in range(KT):
                    out = begin(n0, B, ("G", l, m))
                    multiply(out, [p for t in range(NT) for p in three(cols(hh, t, m), cols(hl, t, m), An_h[:, t, :], An_l[:, t, :])]
                             ).then_inc(tile_ready, 1)
                s = slot(2 * l)
                pe.wait_ge(weight_lo, 2 * l + 1)
                taken(n0, B, ("G", l, KT - 1))
                for m in range(KT):
                    out = begin(n0, B, ("U", l, m))
                    multiply(out, [bias_to_columns(2 * l, bias_rows, m)]
                             + [p for k in range(KT) for p in three(cols(wh[s], k, m), cols(wl[s], k, m), gh[:, k, :], gl[:, k, :])]
                             ).then_inc(tile_ready, 1)
                s = slot(2 * l + 1)
                pe.wait_ge(weight_lo, 2 * l + 2)
                taken(n0, B, ("U", l, KT - 1))
                for t in range(NT):
                    out = begin(n0, B, ("H", l, t))
                    multiply(out, [bias_to_rows(2 * l + 1, bias_rows)]
                             + [p for k in range(KT) for p in three(cols(uh, k, t), cols(ul, k, t), wh[s][:, k, :], wl[s][:, k, :])]
                             ).then_inc(tile_ready, 1)

            for j in range(NT):
                out = begin(cnt, cnt.base, ("C", j))
                transposes(out, [cols(Csum, m, j) for m in range(NT)]).then_inc(tile_ready, 1)

            pe.wait_ge(tile_taken, n1.base)
            pe.wait_ge(emb_step, 9)
            with pe.Fori(0, BLOCKS) as i:
                b = i * PER + n1.base

                def weight(j):
                    pe.wait_ge(weight_lo, i * 6 + (W1 + j + 1))
                    return wh[j % 3], wl[j % 3]

                def done(name):
                    taken(n1, b, name)

                def tile(name, pairs):
                    multiply(begin(n1, b, name), pairs).then_inc(tile_ready, 1)

                def condition(s, t):
                    n = "ab".index(s)
                    if t == 0:
                        pe.wait_ge(cond_ready, i * 2 + (n + 1))
                    tile(("S" + s, t), [(stk[:, t * P:(t + 1) * P], cond[:, 2 * n, :])])
                    tile(("B" + s, t), [(stk[:, t * P:(t + 1) * P], cond[:, 2 * n + 1, :])])

                def transpose_rows(s, t):
                    done(("B" + s, t))
                    out = begin(n1, b, ("T" + s, t))
                    transposes(out, [cols(yp, t, k) for k in range(KT)]).then_inc(tile_ready, 1)

                def rows_product(name, t, lh, ll, w, bias):
                    tile((name, t), [bias_to_rows(bias, brow)] + [p for k in range(KT) for p in
                         three(cols(lh, k, t), cols(ll, k, t), w[0][:, k, :], w[1][:, k, :])])

                def columns_product(name, m, w, rh, rl, bias):
                    tile((name, m), [bias_to_columns(bias, brow, m)] + [p for k in range(KT) for p in
                         three(cols(w[0], k, m), cols(w[1], k, m), rh[:, k, :], rl[:, k, :])])

                def value(t, w):
                    done(("Ta", t))
                    rows_product("v", t, yT_h, yT_l, w, 0)

                def attend(h):
                    pe.wait_ge(probs_ready, i * 16 + (4 * h + 4))
                    for m in range(NT):
                        out = begin(n1, b, ("PT", h, m))
                        transposes(out, [cols(yp, j, m) for j in range(NT)]).then_inc(tile_ready, 1)
                    done(("PT", h, NT - 1))
                    tile(("PV", h), [p for m in range(NT) for p in
                                     three(cols(vm_h, m, h), cols(vm_l, m, h), PT_h[:, m, :], PT_l[:, m, :])])

                condition("a", 0)
                condition("a", 1)
                transpose_rows("a", 0)
                condition("a", 2)
                w = weight(0)
                pe.wait_ge(brow_ready, i + 1)
                value(0, w)
                transpose_rows("a", 1)
                condition("a", 3)
                value(1, w)
                transpose_rows("a", 2)
                value(2, w)
                transpose_rows("a", 3)
                value(3, w)
                wq, wk = weight(1), weight(2)
                for h in range(HEADS):
                    columns_product("q", h, wq, yT_h, yT_l, 1)
                    columns_product("k", h, wk, yT_h, yT_l, 2)
                    if h:
                        attend(h - 1)
                    done(("k", h))
                    for j in range(NT):
                        tile(("s", h, j), three(qk_h[:, 0, j * P:(j + 1) * P], qk_l[:, 0, j * P:(j + 1) * P], qk_h[:, 1, :], qk_l[:, 1, :]))
                attend(HEADS - 1)
                w = weight(3)
                done(("PV", HEADS - 1))
                for t in range(NT):
                    rows_product("o", t, oT_h, oT_l, w, 3)
                    condition("b", t)
                    if t:
                        transpose_rows("b", t - 1)
                transpose_rows("b", NT - 1)
                w = weight(4)
                done(("Tb", NT - 1))
                for m in range(KT):
                    columns_product("M", m, w, yT_h, yT_l, 4)
                w = weight(5)
                done(("M", KT - 1))
                for t in range(NT):
                    rows_product("X", t, vm_h, vm_l, w, 5)

            B = n2.base
            for t in range(NT):
                pe.wait_ge(y_ready, t + 1)
                transposes(begin(n2, B, ("T", t)), [cols(y2, t, k) for k in range(KT)]).then_inc(tile_ready, 1)
            pe.wait_ge(weight_lo, W2 + 1)
            s = slot(W2)
            for t in range(NT):
                taken(n2, B, ("T", t))
                multiply(begin(n2, B, ("A", 0, t)), [bias_to_rows(4, bias_rows)] + [p for k in range(KT) for p in
                         three(cols(y2T_h, k, t), cols(y2T_l, k, t), wh[s][:, k, :], wl[s][:, k, :])]).then_inc(tile_ready, 1)
            pe.wait_ge(l2_step, STEPS + NT + 1)
            for k in range(1, STEPS + 1):
                c = (k - 1) % 2
                taken(n2, B, ("A", k - 1, NT - 1))
                for t in range(NT):
                    multiply(begin(n2, B, ("A", k, t)), [p for m in range(NT) for p in
                             ((cols(adj_r, m, t), cur_h[:, c, m, :]), (cols(adj_r, m, t), cur_l[:, c, m, :]))]).then_inc(tile_ready, 1)

            B = n3.base
            for t in range(NT):
                pe.wait_ge(y_ready, NT + t + 1)
                transposes(begin(n3, B, ("T", t)), [cols(y3, t, k) for k in range(KT)]).then_inc(tile_ready, 1)
            for l in range(2):
                h, hl = hT_h[l], hT_l[l]
                taken(n3, B, ("T", NT - 1) if l == 0 else ("R", 0, KT - 1))
                out = begin(n3, B, ("g", l))
                for t in range(NT):
                    last = multiply(out[:, 2 * t:2 * t + 2], [p for k in range(KT) for p in
                                    three(cols(h, k, t), cols(hl, k, t), gwh[:, l, k, :], gwl[:, l, k, :])])
                last.then_inc(tile_ready, 1)
                for r in range(2):
                    w = W3 + 3 * l + r
                    pe.wait_ge(weight_lo, w + 1)
                    for t in range(NT):
                        multiply(begin(n3, B, ("Z", l, r, t)), [p for k in range(KT) for p in
                                 three(cols(h, k, t), cols(hl, k, t), wh[slot(w)][:, k, :], wl[slot(w)][:, k, :])]).then_inc(tile_ready, 1)
                w = W3 + 3 * l + 2
                pe.wait_ge(weight_lo, w + 1)
                wrh, wrl = wh[slot(w)], wl[slot(w)]
                pe.wait_ge(c_ready, 2)
                taken(n3, B, ("Z", l, 1, NT - 1))
                for m in range(NT):
                    if l == 0:
                        pairs = [bias_to_columns(5, bias_rows, m)]
                        pairs += [p for k in range(KT) for p in three(cols(wrh, k, m), cols(wrl, k, m), h[:, k, :], hl[:, k, :])]
                        pairs += [p for r in range(2) for t in range(NT) for p in
                                  three(Z_h[:, r, t, m * P:(m + 1) * P], Z_l[:, r, t, m * P:(m + 1) * P], C_h[:, r, t, :], C_l[:, r, t, :])]
                    else:
                        pairs = [bias_to_rows(6, bias_rows)]
                        pairs += [p for k in range(KT) for p in three(cols(h, k, m), cols(hl, k, m), wrh[:, k, :], wrl[:, k, :])]
                        pairs += [p for r in range(2) for t in range(NT) for p in
                                  three(C_h[:, r, t, m * P:(m + 1) * P], C_l[:, r, t, m * P:(m + 1) * P], Z_h[:, r, t, :], Z_l[:, r, t, :])]
                    multiply(begin(n3, B, ("R", l, m)), pairs).then_inc(tile_ready, 1)


SMALL = 8 + 7 + 1 + 2 + 6 + 1
CNT = 10


_L0 = ["W_gcn", "b_gcn", "W_mlp", "b_mlp"]
_L1 = ["f_w1", "f_b1", "f_w2", "f_b2", "s1_w", "s1_b", "b1_w", "b1_b", "wq", "bq", "wk", "bk", "wv", "bv", "wo", "bo",
       "s2_w", "s2_b", "b2_w", "b2_b", "m_w1", "m_b1", "m_w2", "m_b2"]
_L2 = ["W", "b", "diffusion_weights"]
_L3 = [f"{n}{l}" for l in (1, 2) for n in ("basis", "att", "gate_w", "root", "bias")]
_INS = (["x", "src", "dst", "edge_type_2", "edge_weight", "node_vec1"] + [f"L0_gnn_{n}" for n in _L0]
        + [f"L1_gnn_{n}" for n in _L1] + [f"L2_gnn_{n}" for n in _L2] + [f"L3_gnn_{n}" for n in _L3])


def kernel(**inputs):
    import numpy as _np
    import concourse.bacc as _bacc
    from concourse import mybir as _mybir
    from concourse.bass_utils import run_bass_kernel_spmd as _run

    nc = _bacc.Bacc("TRN2", target_bir_lowering=False, num_devices=1)
    arrays, d = {}, {}
    for name in _INS:
        a = _np.ascontiguousarray(inputs[name])
        arrays[f"in_{name}"] = a
        d[name] = nc.dram_tensor(f"in_{name}", a.shape, _mybir.dt.from_np(a.dtype), kind="ExternalInput").ap()
    out = nc.dram_tensor("out", (NODES, D), _mybir.dt.float32, kind="ExternalOutput").ap()
    mix_d = nc.dram_tensor("mix_scratch", (2, 2, P, KT * D), _mybir.dt.float32).ap()
    l0 = {n: d[f"L0_gnn_{n}"] for n in _L0}
    l1 = {n: d[f"L1_gnn_{n}"] for n in _L1}
    l2 = {"W": d["L2_gnn_W"], "b": d["L2_gnn_b"], "dw": d["L2_gnn_diffusion_weights"]}
    l3 = {n: [d[f"L3_gnn_{n}{l}"] for l in (1, 2)] for n in ("basis", "att", "gate_w", "root", "bias")}
    program(nc, d["x"], d["src"], d["dst"], d["edge_type_2"], d["edge_weight"], d["node_vec1"], l0, l1, l2, l3, out, mix_d)
    r = _run(nc, [arrays], core_ids=[0])
    return r.results[0]["out"]
```

```python
from contextlib import ExitStack

import concourse.bass as bass
from concourse import mybir

ALU = mybir.AluOpType
ACT = mybir.ActivationFunctionType
AX = mybir.AxisListType
F32 = mybir.dt.float32
F32R = mybir.dt.float32r
I32 = mybir.dt.int32
I16 = mybir.dt.int16
U8 = mybir.dt.uint8

P = 128
NODES = 512
D = 512
NT = NODES // P
KT = D // P
EDGES = 16384
ET = EDGES // P
BODY = 8
TURNS = ET // BODY
SLOTS = 4
HEADS = 4
DH = D // HEADS
BLOCKS = 4
FREQS = 32
PERIOD = 16
COND = 16
BASES = 30
BSLOTS = 3
STEPS = 3
RING = 7
EPS = 1e-5
SCALE = DH ** -0.5
NOEDGE = -1e30
MAGIC = 1.5 * 2 ** 23
TURN = 6.283185


class Tiles:

    def __init__(self, names, base, banks=RING):
        self.at = {n: j for j, n in enumerate(names)}
        self.base, self.n, self.banks = base, len(names), banks
        self.end = base + len(names)

    def bank(self, name):
        return self.at[name] % self.banks


def l1_order():
    o = []
    ln = lambda s, t: [("S" + s, t), ("B" + s, t)]
    o += ln("a", 0) + ln("a", 1) + [("Ta", 0)] + ln("a", 2) + [("v", 0), ("Ta", 1)] + ln("a", 3)
    o += [("v", 1), ("Ta", 2), ("v", 2), ("Ta", 3), ("v", 3)]
    for h in range(HEADS):
        o += [("q", h), ("k", h)]
        if h:
            o += [("PT", h - 1, m) for m in range(NT)] + [("PV", h - 1)]
        o += [("s", h, j) for j in range(NT)]
    o += [("PT", HEADS - 1, m) for m in range(NT)] + [("PV", HEADS - 1)]
    o += [("o", 0)] + ln("b", 0) + [("o", 1)] + ln("b", 1) + [("Tb", 0), ("o", 2)] + ln("b", 2)
    o += [("Tb", 1), ("o", 3)] + ln("b", 3) + [("Tb", 2), ("Tb", 3)]
    o += [("M", m) for m in range(KT)] + [("X", t) for t in range(NT)]
    return o


def program(nc, x_d, src_d, dst_d, type_d, w_d, noise_d, l0, l1, l2, l3, out_d, mix_d, ct_d):
    top = ExitStack()
    with top:
        def sb(name, shape, dt=F32, ctx=top):
            return ctx.enter_context(nc.sbuf_tensor(name, shape, dt))

        def sem(name):
            return top.enter_context(nc.semaphore(name))

        pre = Tiles(["tab", "flag", "z1", "z2"], 0)
        mid = Tiles(["deg", "dinv"], pre.end)
        n0 = Tiles([(s, l, t) for l in range(2) for s in ("G", "U", "H") for t in range(4)], mid.end)
        cnt = Tiles([("C", j) for j in range(NT)], n0.end)
        order1 = l1_order()
        n1 = Tiles(order1, cnt.end)
        assert n1.n % RING == 0
        PER = n1.n
        n2 = Tiles([("T", t) for t in range(4)] + [("A", k, t) for k in range(STEPS + 1) for t in range(4)],
                   n1.base + BLOCKS * PER)
        n3 = Tiles([("T", t) for t in range(4)]
                   + [n for l in range(2) for n in [("g", l)] + [("Z", l, r, t) for r in range(2) for t in range(4)]
                      + [("R", l, t) for t in range(4)]], n2.end)

        def highs(names, base):
            return {n: base + j for j, n in enumerate(names)}, base + len(names)

        hi0, e = highs([n for n in n0.at if n[0] != "H" or n[1] == 0], 0)
        HI1 = e
        names1 = [n for n in order1 if n[0] in ("Ta", "v", "q", "k", "PT", "PV", "Tb", "M")]
        hi1 = {n: j for j, n in enumerate(names1)}
        PERH = len(names1)
        hi2, e = highs([n for n in n2.at if n[0] == "T" or n[1] < STEPS], HI1 + BLOCKS * PERH)
        hi3, e = highs([n for n in n3.at if n[0] in ("T", "Z") or (n[0] == "R" and n[1] == 0)], e)

        x = sb("x", [P, NT, D])
        mask = sb("mask", [P, NT, NODES])
        adj = sb("adj", [P, NT, NODES], U8)
        ident = sb("ident", [P, P])
        ones = sb("ones", [P, P])
        sel = sb("sel", [P, 7, P], F32R)
        stk = sb("stk", [P, NODES], F32R)
        bias_rows = sb("bias_rows", [P, D], F32R)
        rowno = sb("rowno", [P, 1], I32)
        minus_odd = sb("minus_odd", [P, 1])
        minus_low = sb("minus_low", [P, 1])
        minus_loww = sb("minus_loww", [P, 1])
        half = sb("half", [P, NT])
        hasedge = sb("hasedge", [P, NT])
        rinv = sb("rinv", [P, NT])
        stats = sb("stats", [P, NT, 6])
        mv = sb("mv", [P, NT, 2])
        ve = sb("ve", [P, NT])
        rstd = sb("rstd", [P, NT])
        pace = sb("pace", [P, 64])
        nmin = sb("nmin", [P, NT])
        rsum = sb("rsum", [P, NT])
        rden = sb("rden", [P, NT])
        dw = sb("dw", [P, STEPS + 1])
        rdw = sb("rdw", [P, STEPS, NT])
        gw = sb("gw", [P, 2, KT, 2])
        gwh = sb("gwh", [P, 2, KT, 2], F32R)
        gwl = sb("gwl", [P, 2, KT, 2], F32R)
        ge = sb("ge", [P, 2 * NT])
        gate = sb("gate", [P, 2 * NT])
        att = sb("att", [P, 2, 2, BASES])
        bas = sb("bas", [P, BSLOTS, D])
        macc = sb("macc", [P, 2, D])
        wraw = [sb(f"wraw{s}", [P, KT, D]) for s in range(2)]
        wh = [sb(f"wh{s}", [P, KT, D], F32R) for s in range(3)]
        wl = [sb(f"wl{s}", [P, KT, D], F32R) for s in range(3)]

        cg = ExitStack()
        craw = sb("craw", [P, 2, D], ctx=cg)
        cond = sb("cond", [P, 4, D], F32R, ctx=cg)
        braw = sb("braw", [P, D], ctx=cg)
        brow = sb("brow", [P, D], F32R, ctx=cg)
        ec = ExitStack()
        Araw = sb("Araw", [P, NT, NODES], ctx=ec)
        Csum = sb("Csum", [P, NT, NODES], ctx=ec)
        CT = [sb(f"CT{r}", [P, NT, NODES], I16, ctx=ec) for r in range(2)]
        ec2 = ExitStack()
        eint = sb("eint", [P, 3, P], I32, ctx=ec2)
        ewt = sb("ewt", [P, P], ctx=ec2)
        efl = sb("efl", [P, 3, P], ctx=ec2)
        srcT = sb("srcT", [P, ET], ctx=ec2)
        dstT = sb("dstT", [P, ET], ctx=ec2)
        whiT = sb("whiT", [P, ET], F32R, ctx=ec2)
        wloT = sb("wloT", [P, ET], ctx=ec2)
        isr1 = sb("isr1", [P, ET], ctx=ec2)
        iota = sb("iota", [P, NODES], ctx=ec2)
        zero_l = sb("zero_l", [P, P], F32R, ctx=ec2)
        ohs = sb("ohs", [P, SLOTS, NODES], F32R, ctx=ec2)
        ohd = sb("ohd", [P, SLOTS, 4, P], F32R, ctx=ec2)
        eblk = sb("eblk", [P, P], I32, ctx=ec2)
        hit = sb("hit", [P, NT, P], ctx=ec2)
        tile_hit = sb("tile_hit", [P, NT], ctx=ec2)
        turn_of = sb("turn_of", [P, 3, TURNS], ctx=ec2)
        turn_hit = sb("turn_hit", [P, NT, TURNS], ctx=ec2)
        pow2 = sb("pow2", [P, NT, TURNS], ctx=ec2)
        bits_f = sb("bits_f", [P, NT], ctx=ec2)
        turn_bits = sb("turn_bits", [P, NT], I32, ctx=ec2)
        bias_raw = sb("bias_raw", [P, D], ctx=ec2)
        selv = sb("selv", [P, 2, 7, P], ctx=ec2)
        noise = sb("noise", [2 * FREQS, NODES], ctx=ec2)
        rnd = sb("rnd", [2 * FREQS, NODES], ctx=ec2)
        freq = sb("freq", [2 * FREQS, 1], ctx=ec2)
        quarter = sb("quarter", [2 * FREQS, 1], ctx=ec2)
        fw1 = sb("fw1", [2 * FREQS, COND], ctx=ec2)
        fb1 = sb("fb1", [COND, 1], ctx=ec2)
        fw2 = sb("fw2", [COND, P], ctx=ec2)
        cb = sb("cb", [P, 1], ctx=ec2)
        sil = [sb(f"sil{i}", [COND, NODES], ctx=ec2) for i in range(2)]
        ec2.close()
        An_h = sb("An_h", [P, NT, NODES], F32R, ctx=ec)
        An_l = sb("An_l", [P, NT, NODES], F32R, ctx=ec)
        hb_h = [sb(f"hb_h{i}", [P, NT, D], F32R, ctx=ec) for i in range(2)]
        hb_l = [sb(f"hb_l{i}", [P, NT, D], F32R, ctx=ec) for i in range(2)]
        D2 = sb("D2", [P, NODES], ctx=ec)
        xn0 = mask
        slope = sb("slope", [P, 2, D], ctx=ec)
        hv = sb("hv", [P, 2, D], ctx=ec)
        dg = sb("dg", [P, 4, NT], ctx=ec)
        diag = sb("diag", [P, NT, P], ctx=ec)
        ec.close()
        c1 = ExitStack()
        xl = sb("xl", [P, NT, D], ctx=c1)
        yp = sb("yp", [P, NT, D], ctx=c1)
        yT_h = sb("yT_h", [P, KT, NODES], F32R, ctx=c1)
        yT_l = sb("yT_l", [P, KT, NODES], F32R, ctx=c1)
        vm_h = sb("vm_h", [P, NT, D], F32R, ctx=c1)
        vm_l = sb("vm_l", [P, NT, D], F32R, ctx=c1)
        qk_h = sb("qk_h", [P, 2, NODES], F32R, ctx=c1)
        qk_l = sb("qk_l", [P, 2, NODES], F32R, ctx=c1)
        PT_h = sb("PT_h", [P, NT, NODES], F32R, ctx=c1)
        PT_l = sb("PT_l", [P, NT, NODES], F32R, ctx=c1)
        oT_h = sb("oT_h", [P, HEADS, NODES], F32R, ctx=c1)
        oT_l = sb("oT_l", [P, HEADS, NODES], F32R, ctx=c1)
        c1.close()
        cc = ExitStack()
        Cskip = sb("Cskip", [P, 3 * NT, NODES], ctx=cc)
        ctmp = [sb(f"ctmp{i}", [P, NODES], ctx=cc) for i in range(4)]
        rowsum = sb("rowsum", [P, 2, NT], ctx=cc)
        cc.close()
        cg.close()
        c2 = ExitStack()
        y2 = sb("y2", [P, NT, D], ctx=c2)
        y2T_h = sb("y2T_h", [P, KT, NODES], F32R, ctx=c2)
        y2T_l = sb("y2T_l", [P, KT, NODES], F32R, ctx=c2)
        adj_r = sb("adj_r", [P, NT, NODES], F32R, ctx=c2)
        cur_h = sb("cur_h", [P, 2, NT, D], F32R, ctx=c2)
        cur_l = sb("cur_l", [P, 2, NT, D], F32R, ctx=c2)
        acc2 = sb("acc2", [P, NT, D], ctx=c2)
        c2.close()
        c3 = ExitStack()
        Z_h = sb("Z_h", [P, 2, NT, D], F32R, ctx=c3)
        Z_l = sb("Z_l", [P, 2, NT, D], F32R, ctx=c3)
        C_h = sb("C_h", [P, 2, NT, NODES], F32R, ctx=c3)
        C_l = sb("C_l", [P, 2, NT, NODES], F32R, ctx=c3)
        hT_h = [sb("hT_h0", [P, KT, NODES], F32R, ctx=c3)]
        hT_l = [sb("hT_l0", [P, KT, NODES], F32R, ctx=c3)]
        c3y = ExitStack()
        y3 = sb("y3", [P, NT, D], ctx=c3y)
        c3y.close()
        hT_h.append(sb("hT_h1", [P, KT, NODES], F32R, ctx=c3))
        hT_l.append(sb("hT_l1", [P, KT, NODES], F32R, ctx=c3))
        Cr = [sb(f"Cr{r}", [P, NT, NODES], I16, ctx=c3) for r in range(2)]
        c3.close()

        ring = top.enter_context(nc.psum_tensor("ring", [P, RING, 512], F32))
        edge_ps = [[ring[:, 4 - 3 * (m % 2) + j, :] for j in range(3)] for m in range(NT)]

        const_ready = sem("const_ready")
        const_step = sem("const_step")
        sel_step = sem("sel_step")
        small_loaded = sem("small_loaded")
        x_loaded = sem("x_loaded")
        edges_loaded = sem("edges_loaded")
        tile_ready = sem("tile_ready")
        tile_taken = sem("tile_taken")
        hi_ready = sem("hi_ready")
        table_ready = sem("table_ready")
        whi_ready = sem("whi_ready")
        flags_ready = sem("flags_ready")
        dst_ready = sem("dst_ready")
        onehot_ready = sem("onehot_ready")
        scaled_ready = sem("scaled_ready")
        onehot_used = sem("onehot_used")
        pass_ready = sem("pass_ready")
        pass_act = sem("pass_act")
        pass_dve = sem("pass_dve")
        ct_stored = sem("ct_stored")
        ct_loaded = sem("ct_loaded")
        basis_loaded = [sem(f"basis_loaded{s}") for s in range(BSLOTS)]
        basis_used = sem("basis_used")
        mix_clear = sem("mix_clear")
        mix_stored = sem("mix_stored")
        emb_step = sem("emb_step")
        emb_act = sem("emb_act")
        deg_step = sem("deg_step")
        deg_act = sem("deg_act")
        deg_pool = sem("deg_pool")
        cnt_step = sem("cnt_step")
        cnt_act = sem("cnt_act")
        weight_loaded = [sem(f"weight_loaded{s}") for s in range(2)]
        weight_hi = sem("weight_hi")
        weight_lo = sem("weight_lo")
        ln_stats = sem("ln_stats")
        ln_mv = sem("ln_mv")
        ln_var = sem("ln_var")
        ln_rstd = sem("ln_rstd")
        ln_xn = sem("ln_xn")
        h0_hi = sem("h0_hi")
        h0_ready = sem("h0_ready")
        slope_ready = sem("slope_ready")
        leaky_ready = sem("leaky_ready")
        xl_ready = sem("xl_ready")
        cond_clear = sem("cond_clear")
        cond_loaded = sem("cond_loaded")
        cond_hi = sem("cond_hi")
        cond_ready = sem("cond_ready")
        braw_loaded = sem("braw_loaded")
        brow_hi = sem("brow_hi")
        brow_ready = sem("brow_ready")
        exp_ready = sem("exp_ready")
        rden_ready = sem("rden_ready")
        probs_ready = sem("probs_ready")
        y_ready = sem("y_ready")
        l2_step = sem("l2_step")
        c_hi = sem("c_hi")
        c_ready = sem("c_ready")
        gate_exp = sem("gate_exp")
        gate_step = sem("gate_step")
        out_stored = sem("out_stored")

        block = top.enter_context(nc.Block())

        def rows(ap):
            return ap.rearrange("(t p) n -> p t n", p=P)

        W1 = 4
        W2 = W1 + 6 * BLOCKS
        W3 = W2 + 1
        slot = lambda w: (w + 2) % 3

        def last_use(w):
            if w < W1:
                return n0.base + n0.at[(("U", "H")[w % 2], w // 2, 3)]
            if w < W2:
                i, j = divmod(w - W1, 6)
                return n1.base + i * PER + n1.at[(("v", "q", "k", "o", "M", "X")[j], 3)]
            if w == W2:
                return n2.base + n2.at[("A", 0, 3)]
            l, j = divmod(w - W3, 3)
            return n3.base + n3.at[("Z", l, j, 3) if j < 2 else ("R", l, 3)]

        def block_weight(i, j):
            return l1[("wv", "wq", "wk", "wo", "m_w1", "m_w2")[j]][bass.ds(i, 1)].rearrange("a (t p) n -> p (a t) n", p=P)

        def weight_source(w):
            if w < W1:
                return rows(l0[("W_gcn", "W_mlp")[w % 2]][w // 2])
            if w < W2:
                return block_weight(*divmod(w - W1, 6))
            if w == W2:
                return rows(l2["W"])
            l, j = divmod(w - W3, 3)
            return mix_d[l, j].rearrange("p (k n) -> p k n", k=KT) if j < 2 else rows(l3["root"][l])

        scales = [None, isr1[:], wloT[:], whiT[:].bitcast(F32)]
        scaled_by_act = lambda u: 4 - u % 2

        @block.sync
        def _(sp):
            for t, d in enumerate((src_d, dst_d, type_d)):
                sp.dma_start(eint[:, t, :], d.rearrange("(t p) -> t p", p=P)).then_inc(edges_loaded, 16)
            sp.dma_start(ewt[:], w_d.rearrange("(t p) -> t p", p=P)).then_inc(edges_loaded, 16)
            sp.dma_start(x[:], rows(x_d)).then_inc(x_loaded, 16)

            sp.wait_ge(const_ready, 1)
            n_small = [0]

            def small(dst, src):
                sp.dma_start(dst, src, allow_slow_non_contiguous=True).then_inc(small_loaded, 16)
                n_small[0] += 1

            for l in range(2):
                for r in range(2):
                    small(att[:, l, r, :], l3["att"][l][r:r + 1, :].broadcast_to([P, BASES]))
                    small(gw[:, l, :, r], l3["gate_w"][l][r, :, 0].rearrange("(k p) -> p k", p=P))
            vecs = [l0["b_gcn"][0:1], l0["b_mlp"][0:1], l0["b_gcn"][1:2], l0["b_mlp"][1:2]]
            vecs += [b.rearrange("(a d) -> a d", a=1) for b in (l2["b"], l3["bias"][0], l3["bias"][1])]
            for j, v in enumerate(vecs):
                small(bias_raw[2 * j:2 * j + 2, :], v.broadcast_to([2, D]))
            small(noise[:], noise_d.rearrange("n a -> a n").broadcast_to([2 * FREQS, NODES]))
            small(fw1[:], l1["f_w1"])
            small(fb1[:], l1["f_b1"].rearrange("(c a) -> c a", a=1))
            for g in range(3):
                small(fw2[:, 32 * g:32 * g + COND], l1["f_w2"])
                small(cb[32 * g:32 * g + COND, :], l1["f_b2"].rearrange("(c a) -> c a", a=1))
            small(dw[:], l2["dw"].rearrange("(a d) -> a d", a=1).broadcast_to([P, STEPS + 1]))
            assert n_small[0] == SMALL

            def load_cond(b, n, ready):
                if ready is not None:
                    sp.wait_ge(cond_ready, ready)
                for k in range(2):
                    w_, b_ = l1[("s", "b")[k] + f"{n + 1}_w"], l1[("s", "b")[k] + f"{n + 1}_b"]
                    for g in range(3):
                        sp.dma_start(craw[32 * g:32 * g + COND, k, :],
                                     w_[bass.ds(b, 1)].rearrange("a c d -> (a c) d")).then_inc(cond_loaded, 16)
                    sp.dma_start(craw[96:98, k, :], b_[bass.ds(b, 1)].broadcast_to([2, D])).then_inc(cond_loaded, 16)

            sp.wait_ge(cond_clear, 1)
            load_cond(0, 0, None)
            load_cond(0, 1, 1)

            def bases(c, g):
                l, k = (c // KT, c % KT) if isinstance(c, int) else (1, c - KT)
                for s in range(BSLOTS):
                    sp.wait_ge(basis_used, c * BASES + (g * BSLOTS + (s + 1)))
                    src = l3["basis"][l][bass.ds(g * BSLOTS + s, 1), bass.ds(k * P, P), :]
                    sp.dma_start(bas[:, s, :], src.rearrange("a k n -> (a k) n")).then_inc(basis_loaded[s], 16)

            def store_mix(c):
                l, k = (c // KT, c % KT) if isinstance(c, int) else (1, c - KT)
                sp.wait_ge(basis_used, c * BASES + (BASES + BSLOTS))
                sp.dma_start(mix_d[l].rearrange("r p n -> p r n")[:, :, bass.ds(k * D, D)], macc[:]).then_inc(mix_stored, 16)

            GROUPS = BASES // BSLOTS
            bases(0, 0)
            for c in range(KT):
                with sp.Fori(1, GROUPS) as g:
                    bases(c, g)
                bases(c + 1, 0)
                store_mix(c)
                if c == 1:
                    sp.wait_ge(pass_act, 2 * NT)
                    sp.wait_ge(pass_dve, NT)
                    for r in range(2):
                        sp.dma_start(ct_d[r], CT[r][:]).then_inc(ct_stored, 16)

            def load_biases(i):
                for j, name in enumerate(("bv", "bq", "bk", "bo", "m_b1", "m_b2")):
                    sp.dma_start(braw[2 * j:2 * j + 2, :], l1[name][bass.ds(i, 1)].broadcast_to([2, D])
                                 ).then_inc(braw_loaded, 16)

            def block_loads(i, nxt, last):
                c = i + KT
                load_cond(nxt, 0, i * 2 + 2)
                with sp.Fori(1, EARLY // 2) as g:
                    bases(c, g)
                if not last:
                    sp.wait_ge(brow_ready, i + 1)
                    load_biases(nxt)
                with sp.Fori(EARLY // 2, EARLY) as g:
                    bases(c, g)
                load_cond(nxt, 1, i * 2 + 3)
                with sp.Fori(EARLY, GROUPS) as g:
                    bases(c, g)
                if not last:
                    bases(c + 1, 0)
                store_mix(c)

            load_biases(0)
            with sp.Fori(0, BLOCKS - 1) as i:
                block_loads(i, i + 1, False)
            block_loads(BLOCKS - 1, BLOCKS - 1, True)
            sp.wait_ge(tile_taken, n2.base)
            for r in range(2):
                sp.dma_start(Cr[r][:], ct_d[r]).then_inc(ct_loaded, 16)
            for t in range(NT):
                sp.wait_ge(tile_taken, n3.base + n3.at[("R", 1, t)] + 1)
                sp.dma_start(out_d[t * P:(t + 1) * P, :], x[:, t, :]).then_inc(out_stored, 16)
            sp.wait_ge(out_stored, 16 * NT)

        @block.gpsimd
        def _(pool):
            g = nc.gpsimd
            for clear in (bias_raw, fw2, cb, craw, braw, ones, half, zero_l, minus_low, minus_loww, ident, quarter):
                v = clear[:].bitcast(F32) if clear is zero_l else clear[:]
                last = g.memset(v, 1.0 if clear is ones else -0.5 if clear is half else 0.0)
            last.then_inc(const_step, 1)
            pool.wait_ge(const_step, 1)
            g.memset(cb[96:99, :], 1.0).then_inc(const_ready, 1)
            pool.wait_ge(const_ready, 1)
            g.affine_select(out=craw[:, 0, :], in_=craw[:, 0, :], compare_op=ALU.not_equal, fill=1.0, base=-98,
                            pattern=[[0, D]], channel_multiplier=1).then_inc(cond_clear, 1)
            pool.wait_ge(cond_clear, 1)
            g.memset(quarter[FREQS:2 * FREQS, :], 0.25).then_inc(const_step, 1)
            pool.wait_ge(const_step, 2)
            g.memset(minus_low[64:96, :], -1.0).then_inc(const_step, 1)
            pool.wait_ge(const_step, 3)
            g.memset(minus_loww[32:64, :], -1.0).then_inc(const_step, 1)
            pool.wait_ge(const_step, 4)
            g.affine_select(out=minus_loww[:], in_=minus_loww[:], compare_op=ALU.not_equal, fill=-1.0, base=-97,
                            pattern=[[0, 1]], channel_multiplier=1)
            g.affine_select(out=ident[:], in_=ident[:], compare_op=ALU.not_equal, fill=1.0, base=0,
                            pattern=[[-1, P]], channel_multiplier=1)
            g.iota(iota[:], [[1, NODES]], base=0, channel_multiplier=0, allow_small_or_imprecise_dtypes=True)
            g.iota(selv[:, 0, :, :], [[-2, 7], [0, P]], base=0, channel_multiplier=1, allow_small_or_imprecise_dtypes=True)
            g.iota(rowno[:], [[0, 1]], base=0, channel_multiplier=1)
            g.iota(turn_of[:, 0, :], [[-BODY, TURNS]], base=0, channel_multiplier=1, allow_small_or_imprecise_dtypes=True)
            for q in range(TURNS):
                g.memset(pow2[:, :, q], float(2 ** q))
            g.iota(freq[0:FREQS, :], [[0, 1]], base=1, channel_multiplier=1, allow_small_or_imprecise_dtypes=True
                   ).then_inc(const_step, 1)
            pool.wait_ge(const_step, 5)
            g.iota(freq[FREQS:2 * FREQS, :], [[0, 1]], base=1, channel_multiplier=1, allow_small_or_imprecise_dtypes=True
                   ).then_inc(const_ready, 1)

            def low_weight(w, s, r):
                pool.wait_ge(weight_hi, w + 1)
                g.tensor_tensor(wl[s][:], wraw[r][:], wh[s][:].bitcast(F32), ALU.subtract).then_inc(weight_lo, 1)

            def inverse_root(n, t):
                pool.wait_ge(ln_var, n + 1)
                g.tensor_tensor(rstd[:, t:t + 1], ve[:, t:t + 1], half[:, 0:1], ALU.pow).then_inc(ln_rstd, 1)

            for w in range(2):
                low_weight(w, slot(w), w % 2)
            for t in range(NT):
                inverse_root(t, t)
            pool.wait_ge(deg_step, 1)
            g.tensor_tensor(dg[:, 2, :], dg[:, 1, :], half[:], ALU.pow).then_inc(deg_pool, 1)
            for w in range(2, W1 + 2):
                low_weight(w, slot(w), w % 2)
            for t in range(NT):
                inverse_root(NT + t, t)
            with pool.Fori(0, BLOCKS) as i:
                for t in range(NT):
                    inverse_root(i * 8 + (8 + t), t)
                for j in (2, 3, 4):
                    low_weight(i * 6 + (W1 + j), j % 3, j % 2)
                for t in range(NT):
                    inverse_root(i * 8 + (12 + t), t)
                for j in (5, 6, 7):
                    low_weight(i * 6 + (W1 + j), j % 3, j % 2)
            low_weight(W3 + 1, slot(W3 + 1), (W3 + 1) % 2)
            for t in range(NT):
                inverse_root(40 + t, t)
            low_weight(W3 + 2, slot(W3 + 2), (W3 + 2) % 2)
            for t in range(NT):
                inverse_root(44 + t, t)
            for w in range(W3 + 3, W3 + 6):
                low_weight(w, slot(w), w % 2)

        @block.scalar
        def _(act):
            a = nc.scalar

            def high_weight(w, s, r, half_w, freed, following):
                if following is not None:
                    if not (isinstance(w, int) and w == 0):
                        act.wait_ge(weight_lo, w)
                    act.dma_start(wraw[1 - r][:], following).then_inc(weight_loaded[1 - r], 16)
                act.wait_ge(weight_loaded[r], half_w * 16 + 16)
                if freed is not None:
                    act.wait_ge(tile_ready, freed)
                a.activation(wh[s][:], wraw[r][:], ACT.Copy).then_inc(weight_hi, 1)

            def hw(w):
                if w + 1 == W3 or w + 1 == W3 + 3:
                    act.wait_ge(mix_stored, 16 * KT * (1 if w + 1 == W3 else 2))
                high_weight(w, slot(w), w % 2, w // 2, last_use(w - 3) + 1 if w >= 3 else None,
                            weight_source(w + 1) if w + 1 < W3 + 6 else None)

            def bank(T, name):
                return ring[:, T.bank(name), :]

            def high(T, base, name, out, func=ACT.Copy, **kw):
                act.wait_ge(tile_ready, base + (T.at[name] + 1))
                src = bank(T, name)
                if len(out.shape) == 3:
                    src = src.rearrange("p (a b) -> p a b", a=out.shape[1])
                a.activation(out, src, func, **kw).then_inc(hi_ready, 1)

            act.dma_start(wraw[0][:], weight_source(0)).then_inc(weight_loaded[0], 16)
            act.wait_ge(emb_step, 4)
            a.activation(rnd[:], noise[:], ACT.Sin, scale=TURN).then_inc(emb_act, 1)
            act.wait_ge(tile_ready, pre.base + pre.at["tab"] + 1)
            a.activation(whiT[:], ring[:, pre.bank("tab"), 3 * P:4 * P], ACT.Copy).then_inc(whi_ready, 1)
            act.wait_ge(tile_taken, pre.base + pre.at["z1"] + 1)
            a.activation(sil[0][:], sil[1][:], ACT.Exp, scale=-1.0).then_inc(emb_act, 1)
            hw(0)
            hw(1)
            act.wait_ge(flags_ready, 1)
            for m in range(NT):
                bits = act.value_load(turn_bits[0:1, m:m + 1], min_val=0, max_val=2 ** TURNS - 1)
                with act.Fori(0, TURNS) as q:
                    with act.If(((bits >> q) & 1) > 0):
                        for u in range(BODY):
                            n = q * BODY + (m * ET + u)
                            act.wait_ge(dst_ready, n + 1)
                            s, e = u % SLOTS, bass.ds(q * BODY + u, 1)
                            for r in range(1, scaled_by_act(u)):
                                last = a.activation(ohd[:, s, r, :], ohd[:, s, 0, :].bitcast(F32), ACT.Copy,
                                                    scale=scales[r][:, e])
                            last.then_inc(scaled_ready, 1)
                    with act.Else():
                        act.drain().then_inc(scaled_ready, BODY)
                act.wait_ge(pass_ready, m + 1)
                a.activation(CT[1][:, m, :], edge_ps[m][2], ACT.Copy).then_inc(pass_act, 1)
                a.activation(Araw[:, m, :], edge_ps[m][0], ACT.Copy).then_inc(pass_act, 1)

            for t in range(NT):
                act.wait_ge(ln_xn, t + 1)
                a.activation(hb_h[0][:, t, :], xn0[:, t, :], ACT.Relu).then_inc(h0_hi, 1)
            for m in range(NT):
                act.wait_ge(deg_step, 7 + m)
                a.activation(An_h[:, m, :], Araw[:, m, :], ACT.Copy).then_inc(deg_act, 1)
            for l in range(2):
                g_, u_ = hb_h[1 - l], hb_h[l]
                for m in range(KT):
                    high(n0, n0.base, ("G", l, m), g_[:, m, :])
                hw((2, 4)[l])
                for m in range(KT):
                    high(n0, n0.base, ("U", l, m), u_[:, m, :])
                hw((3, 5)[l])
                for t in range(NT):
                    act.wait_ge(tile_ready, n0.base + n0.at[("H", l, t)] + 1)
                    if t >= 2 or l:
                        act.wait_ge(leaky_ready, 4 * l + t - 1)
                    a.activation(slope[:, t % 2, :], bank(n0, ("H", l, t)), ACT.Copy, scale=0.01).then_inc(slope_ready, 1)
                    if l == 0:
                        act.wait_ge(leaky_ready, t + 1)
                        a.activation(hb_h[1][:, t, :], hv[:, t % 2, :], ACT.Copy).then_inc(hi_ready, 1)

            for j in range(NT):
                act.wait_ge(cnt_step, CNT * j + 2)
                a.activation(ctmp[3][:], ctmp[1][:], ACT.Ln).then_inc(cnt_act, 1)

            def block_highs(i, last):
                b = i * PER + n1.base

                def hi(name, out, func=ACT.Copy):
                    high(n1, b, name, out, func)

                def hwi(j, freed):
                    if last:
                        hw(W1 + 6 * i + j)
                    else:
                        high_weight(i * 6 + (W1 + j), j % 3, j % 2, i * 3 + (W1 // 2 + j // 2), freed,
                                    block_weight(i + (j + 1) // 6, (j + 1) % 6))

                def after(name):
                    return b + (n1.at[name] + 1)

                def exps(h):
                    for j in range(NT):
                        act.wait_ge(tile_taken, after(("s", h, j)))
                        a.activation(yp[:, j, :], yp[:, j, :], ACT.Exp, bias=nmin[:, j:j + 1], scale=-1.0,
                                     accum_out=rsum[:, j:j + 1]).then_inc(exp_ready, 1)

                def attend(h):
                    for m in range(NT):
                        hi(("PT", h, m), PT_h[:, m, :])
                    hi(("PV", h), oT_h[:, h, :])

                hwi(2, b)
                for t in range(NT):
                    if t:
                        hi(("v", t - 1), vm_h[:, t - 1, :])
                    hi(("Ta", t), yT_h[:, :, t * P:(t + 1) * P])
                hi(("v", NT - 1), vm_h[:, NT - 1, :])
                for h in range(HEADS):
                    hi(("q", h), qk_h[:, 0, :])
                    hi(("k", h), qk_h[:, 1, :])
                    if h == 0:
                        hwi(3, after(("v", NT - 1)))
                    if h:
                        attend(h - 1)
                    exps(h)
                hwi(4, after(("q", HEADS - 1)))
                attend(HEADS - 1)
                hwi(5, after(("k", HEADS - 1)))
                for t in range(NT):
                    hi(("Tb", t), yT_h[:, :, t * P:(t + 1) * P])
                hwi(6, after(("o", NT - 1)))
                for m in range(KT):
                    hi(("M", m), vm_h[:, m, :], ACT.Relu)
                hwi(7, after(("M", KT - 1)))

            with act.Fori(0, BLOCKS - 1) as i:
                block_highs(i, False)
            block_highs(BLOCKS - 1, True)

            hw(W3 + 1)
            for t in range(NT):
                high(n2, n2.base, ("T", t), y2T_h[:, :, t * P:(t + 1) * P])
            for t in range(NT):
                high(n2, n2.base, ("A", 0, t), cur_h[:, 0, t, :])
            hw(W3 + 2)
            for k in range(1, STEPS):
                for t in range(NT):
                    high(n2, n2.base, ("A", k, t), cur_h[:, k % 2, t, :], ACT.Identity, scale=rinv[:, t:t + 1])

            act.wait_ge(y_ready, 2 * NT)
            act.wait_ge(ct_loaded, 32)
            for r in range(2):
                a.activation(C_h[:, r, :, :], Cr[r][:], ACT.Copy).then_inc(c_hi, 1)
            for t in range(NT):
                high(n3, n3.base, ("T", t), hT_h[0][:, :, t * P:(t + 1) * P])
            for l in range(2):
                act.wait_ge(tile_ready, n3.base + n3.at[("g", l)] + 1)
                a.activation(ge[:], ring[:, n3.bank(("g", l)), 0:2 * NT], ACT.Exp, scale=-1.0).then_inc(gate_exp, 1)
                act.wait_ge(gate_step, l + 1)
                for r in range(2):
                    for t in range(NT):
                        high(n3, n3.base, ("Z", l, r, t), Z_h[:, r, t, :], ACT.Identity,
                             scale=gate[:, 2 * t + r:2 * t + r + 1])
                    if l == 0:
                        hw(W3 + 3 + r)
                if l == 0:
                    for m in range(KT):
                        high(n3, n3.base, ("R", 0, m), hT_h[1][:, m, :], ACT.Relu)
                    hw(W3 + 5)

        @block.vector
        def _(dve):
            v = nc.vector

            def f(ap):
                return ap.bitcast(F32)

            def bank(T, name):
                return ring[:, T.bank(name), :]

            def ready(T, base, name):
                dve.wait_ge(tile_ready, base + (T.at[name] + 1))

            def taken(T, base, name):
                dve.wait_ge(tile_taken, base + (T.at[name] + 1))

            def low(T, base, name, hi_count, out, hi, func=None, scalar=None):
                dve.wait_ge(hi_ready, hi_count + 1)
                src = bank(T, name)
                if len(out.shape) == 3:
                    src = src.rearrange("p (a b) -> p a b", a=out.shape[1])
                if func is None:
                    v.tensor_tensor(out, src, f(hi), ALU.subtract).then_inc(tile_taken, 1)
                else:
                    v.scalar_tensor_tensor(out, src, scalar, f(hi), func, ALU.subtract).then_inc(tile_taken, 1)

            holds = [0]

            def hold():
                v.memset(pace[:, holds[0]:holds[0] + 1], 0.0)
                holds[0] += 1

            def norm_stats(src, t, n):
                v.bn_stats(stats[:, t, :], src).then_inc(ln_stats, 1)
                dve.wait_ge(ln_stats, n + 1)
                hold()
                v.bn_aggr(mv[:, t, :], stats[:, t, :]).then_inc(ln_mv, 1)
                dve.wait_ge(ln_mv, n + 1)
                v.tensor_scalar(ve[:, t:t + 1], mv[:, t, 1:2], EPS, None, ALU.add).then_inc(ln_var, 1)

            def normalise(out, src, t, n):
                dve.wait_ge(ln_rstd, n + 1)
                v.tensor_scalar(out, src, mv[:, t, 0:1], rstd[:, t:t + 1], ALU.subtract, ALU.mult).then_inc(ln_xn, 1)

            dve.wait_ge(const_ready, 2)
            v.tensor_scalar(selv[:, 1, :, :], selv[:, 0, :, :], 0.0, None, ALU.is_ge).then_inc(sel_step, 1)
            dve.wait_ge(sel_step, 1)
            v.scalar_tensor_tensor(sel[:].rearrange("p a b -> p (a b)"), selv[:, 0, :, :].rearrange("p a b -> p (a b)"), 1.0,
                                   selv[:, 1, :, :].rearrange("p a b -> p (a b)"), ALU.is_le, ALU.mult).then_inc(sel_step, 1)
            v.tensor_scalar(rowno[:], rowno[:], 1, None, ALU.bitwise_and).then_inc(sel_step, 1)
            dve.wait_ge(sel_step, 3)
            v.tensor_scalar(minus_odd[:], rowno[:], -1.0, None, ALU.mult).then_inc(sel_step, 1)
            dve.wait_ge(edges_loaded, 64)
            v.tensor_copy(efl[:], eint[:]).then_inc(table_ready, 1)
            v.tensor_scalar(eblk[:], eint[:, 1, :], P.bit_length() - 1, None, ALU.arith_shift_right).then_inc(table_ready, 1)
            v.tensor_scalar(turn_of[:, 1, :], turn_of[:, 0, :], 0.0, None, ALU.is_ge).then_inc(table_ready, 1)
            dve.wait_ge(table_ready, 3)
            for m in range(NT):
                last = v.tensor_scalar(hit[:, m, :], eblk[:], float(m), None, ALU.is_equal)
            last.then_inc(table_ready, 1)
            v.scalar_tensor_tensor(turn_of[:, 2, :], turn_of[:, 0, :], BODY - 1.0, turn_of[:, 1, :], ALU.is_le, ALU.mult
                                   ).then_inc(table_ready, 1)
            dve.wait_ge(table_ready, 5)
            v.reduce_max(tile_hit[:], hit[:], AX.X).then_inc(table_ready, 1)
            dve.wait_ge(table_ready, 6)
            v.tensor_tensor(turn_hit[:], tile_hit[:].unsqueeze(2).broadcast_to([P, NT, TURNS]),
                            turn_of[:, 2, :].unsqueeze(1).broadcast_to([P, NT, TURNS]), ALU.mult).then_inc(table_ready, 1)
            dve.wait_ge(small_loaded, 16 * SMALL)
            v.tensor_copy(bias_rows[:], bias_raw[:]).then_inc(sel_step, 1)
            v.tensor_copy(gwh[:], gw[:]).then_inc(sel_step, 1)
            dve.wait_ge(sel_step, 6)
            v.scalar_tensor_tensor(bias_rows[:], f(bias_rows[:]), minus_odd[:], bias_raw[:], ALU.mult, ALU.add).then_inc(sel_step, 1)
            v.tensor_tensor(gwl[:], gw[:], f(gwh[:]), ALU.subtract).then_inc(sel_step, 1)

            v.tensor_scalar(noise[:], noise[:], freq[:], 1.0 / PERIOD, ALU.mult, ALU.mult).then_inc(emb_step, 1)
            dve.wait_ge(emb_step, 1)
            v.tensor_scalar(noise[:], noise[:], quarter[:], None, ALU.add).then_inc(emb_step, 1)
            dve.wait_ge(emb_step, 2)
            v.tensor_scalar(rnd[:], noise[:], MAGIC, MAGIC, ALU.add, ALU.subtract).then_inc(emb_step, 1)
            dve.wait_ge(emb_step, 3)
            v.tensor_tensor(noise[:], noise[:], rnd[:], ALU.subtract).then_inc(emb_step, 1)
            dve.wait_ge(whi_ready, 1)
            tab = bank(pre, "tab")
            v.tensor_copy(srcT[:], tab[:, 0:P])
            v.tensor_copy(dstT[:], tab[:, P:2 * P])
            v.tensor_scalar(isr1[:], tab[:, 2 * P:3 * P], 0.0, None, ALU.not_equal).then_inc(table_ready, 1)
            v.tensor_tensor(wloT[:], tab[:, 3 * P:4 * P], f(whiT[:]), ALU.subtract).then_inc(tile_taken, 1)
            ready(pre, pre.base, "flag")
            v.scalar_tensor_tensor(turn_hit[:].rearrange("p m q -> p (m q)"), bank(pre, "flag")[:, 0:NT * TURNS], 1.0,
                                   pow2[:].rearrange("p m q -> p (m q)"), ALU.min, ALU.mult).then_inc(tile_taken, 1)
            taken(pre, pre.base, "flag")
            v.reduce_sum(bits_f[:], turn_hit[:], AX.X).then_inc(table_ready, 1)
            dve.wait_ge(table_ready, 9)
            v.tensor_copy(turn_bits[:], bits_f[:]).then_inc(flags_ready, 1)
            ready(pre, pre.base, "z1")
            v.tensor_scalar(sil[1][:], bank(pre, "z1")[0:COND, :], fb1[:], None, ALU.add).then_inc(tile_taken, 1)
            dve.wait_ge(emb_act, 2)
            v.tensor_scalar(sil[0][:], sil[0][:], 1.0, None, ALU.add).then_inc(emb_step, 1)
            dve.wait_ge(emb_step, 5)
            v.reciprocal(sil[0][:], sil[0][:]).then_inc(emb_step, 1)
            dve.wait_ge(emb_step, 6)
            v.tensor_tensor(sil[0][:], sil[0][:], sil[1][:], ALU.mult).then_inc(emb_step, 1)
            ready(pre, pre.base, "z2")
            v.tensor_scalar(xn_c := macc[:, 0, 0:NODES], bank(pre, "z2"), cb[:], None, ALU.add).then_inc(tile_taken, 1)
            taken(pre, pre.base, "z2")
            v.tensor_copy(stk[:], xn_c).then_inc(emb_step, 1)
            dve.wait_ge(emb_step, 8)
            v.scalar_tensor_tensor(stk[:], f(stk[:]), minus_low[:], xn_c, ALU.mult, ALU.add).then_inc(emb_step, 1)

            def split_cond(n, count):
                dve.wait_ge(cond_loaded, count * 128 + 128)
                v.tensor_copy(cond[:, 2 * n:2 * n + 2, :], craw[:]).then_inc(cond_hi, 1)
                dve.wait_ge(cond_hi, count + 1)
                v.scalar_tensor_tensor(cond[:, 2 * n:2 * n + 2, :], f(cond[:, 2 * n:2 * n + 2, :]), minus_loww[:], craw[:],
                                       ALU.mult, ALU.add).then_inc(cond_ready, 1)

            split_cond(0, 0)
            split_cond(1, 1)

            dve.wait_ge(emb_step, 9)
            v.engine_nop().then_inc(basis_used, BSLOTS)

            def clear_mix(c):
                if not (isinstance(c, int) and c == 0):
                    dve.wait_ge(mix_stored, c * 16)
                v.memset(macc[:], 0.0).then_inc(mix_clear, 1)

            def mix_at(c, g, s):
                n = c * BASES + g * BSLOTS + s
                l = c // KT if isinstance(c, int) else 1
                dve.wait_ge(basis_loaded[s], c * (16 * BASES // BSLOTS) + (g * 16 + 16))
                if isinstance(g, int) and g == 0 and s == 0:
                    dve.wait_ge(mix_clear, c + 1)
                dve.wait_ge(basis_used, n + BSLOTS)
                e = bass.ds(g * BSLOTS + s, 1)
                for r in range(2):
                    last = v.scalar_tensor_tensor(macc[:, r, :], bas[:, s, :], att[:, l, r, e], macc[:, r, :], ALU.mult, ALU.add)
                last.then_inc(basis_used, 1)

            def turn(m, q, bits):
                with dve.If(((bits >> q) & 1) > 0):
                    for u in range(BODY):
                        n = q * BODY + (m * ET + u)
                        s, e = u % SLOTS, bass.ds(q * BODY + u, 1)
                        dve.wait_ge(onehot_used, n + 1)
                        cols = iota[:, m * P:(m + 1) * P]
                        v.tensor_scalar(ohd[:, s, 0, :], cols, dstT[:, e], None, ALU.is_equal).then_inc(dst_ready, 1)
                        for r in range(scaled_by_act(u), 4):
                            v.tensor_scalar(ohd[:, s, r, :], cols, dstT[:, e], scales[r][:, e], ALU.is_equal, ALU.mult)
                        v.tensor_scalar(ohs[:, s, :], iota[:], srcT[:, e], None, ALU.is_equal).then_inc(onehot_ready, 1)
                with dve.Else():
                    dve.drain().then_inc(dst_ready, BODY)
                    dve.drain().then_inc(onehot_ready, BODY)

            dve.wait_ge(flags_ready, 1)
            dve.wait_ge(table_ready, 9)
            dve.wait_ge(tile_taken, pre.base + 1)
            MT = BASES // 2
            for m in range(NT):
                if m % 2 == 0:
                    clear_mix(m // 2)
                    dve.wait_ge(mix_clear, m // 2 + 1)
                bits = dve.value_load(turn_bits[0:1, m:m + 1], min_val=0, max_val=2 ** TURNS - 1)
                with dve.Fori(0, MT // BSLOTS) as g:
                    for s in range(BSLOTS):
                        mix_at(m // 2, g + (m % 2) * (MT // BSLOTS), s)
                        turn(m, g * BSLOTS + s, bits)
                for q in range(MT, TURNS):
                    turn(m, q, bits)
                dve.wait_ge(pass_ready, m + 1)
                v.tensor_copy(Csum[:, m, :], edge_ps[m][1])
                dve.wait_ge(pass_act, 2 * m + 1)
                v.tensor_tensor(CT[0][:, m, :], edge_ps[m][1], CT[1][:, m, :], ALU.subtract).then_inc(pass_dve, 1)

            mixes = [(c, g, s) for c in (2, 3) for g in range(BASES // BSLOTS) for s in range(BSLOTS)]

            def mix_some(count):
                for c, g, s in mixes[:count]:
                    if g == s == 0:
                        clear_mix(c)
                    mix_at(c, g, s)
                del mixes[:count]

            dve.wait_ge(x_loaded, 16)
            for t in range(NT):
                norm_stats(x[:, t, :], t, t)
            for t in range(NT):
                normalise(xn0[:, t, :], x[:, t, :], t, t)
            ready(mid, mid.base, "deg")
            v.tensor_copy(dg[:, 0, :], bank(mid, "deg")[:, 0:2 * NT:2]).then_inc(tile_taken, 1)
            taken(mid, mid.base, "deg")
            v.tensor_scalar(dg[:, 1, :], dg[:, 0, :], 1e-37, None, ALU.max).then_inc(deg_step, 1)
            for t in range(NT):
                dve.wait_ge(h0_hi, t + 1)
                v.scalar_tensor_tensor(hb_l[0][:, t, :], xn0[:, t, :], 0.0, f(hb_h[0][:, t, :]), ALU.max, ALU.subtract).then_inc(h0_ready, 1)
            dve.wait_ge(deg_pool, 1)
            v.scalar_tensor_tensor(dg[:, 3, :], dg[:, 0, :], 0.0, dg[:, 2, :], ALU.is_gt, ALU.mult).then_inc(deg_step, 1)
            dve.wait_ge(deg_step, 2)
            for j in range(NT):
                v.tensor_scalar(diag[:, j, :], ident[:], dg[:, 3, j:j + 1], None, ALU.mult).then_inc(deg_step, 1)
            ready(mid, mid.base, "dinv")
            v.tensor_copy(D2[:], bank(mid, "dinv")).then_inc(tile_taken, 1)
            taken(mid, mid.base, "dinv")
            dve.wait_ge(pass_act, 2 * NT)
            for m in range(NT):
                v.scalar_tensor_tensor(Araw[:, m, :], Araw[:, m, :], dg[:, 3, m:m + 1], D2[:], ALU.mult, ALU.mult).then_inc(deg_step, 1)
            for m in range(NT):
                dve.wait_ge(deg_act, m + 1)
                v.tensor_tensor(An_l[:, m, :], Araw[:, m, :], f(An_h[:, m, :]), ALU.subtract).then_inc(deg_step, 1)

            for l in range(2):
                gb, ub = 1 - l, l
                for m in range(KT):
                    low(n0, n0.base, ("G", l, m), hi0[("G", l, m)], hb_l[gb][:, m, :], hb_h[gb][:, m, :])
                    mix_some(2)
                for m in range(KT):
                    low(n0, n0.base, ("U", l, m), hi0[("U", l, m)], hb_l[ub][:, m, :], hb_h[ub][:, m, :])
                    mix_some(2)
                for t in range(NT):
                    dve.wait_ge(slope_ready, 4 * l + t + 1)
                    v.tensor_tensor(hv[:, t % 2, :], bank(n0, ("H", l, t)), slope[:, t % 2, :], ALU.max).then_inc(leaky_ready, 1)
                    dve.wait_ge(leaky_ready, 4 * l + t + 1)
                    if l == 0:
                        dve.wait_ge(hi_ready, hi0[("H", 0, t)] + 1)
                        v.tensor_tensor(hb_l[1][:, t, :], hv[:, t % 2, :], f(hb_h[1][:, t, :]), ALU.subtract).then_inc(tile_taken, 1)
                    else:
                        v.tensor_tensor(x[:, t, :], x[:, t, :], hv[:, t % 2, :], ALU.add).then_inc(tile_taken, 1)
                    mix_some(2)

            step = [0]

            def counted(ins):
                step[0] += 1
                ins.then_inc(cnt_step, 1)
                return step[0]

            for j in range(NT):
                ready(cnt, cnt.base, ("C", j))
                if j:
                    dve.wait_ge(cnt_step, CNT * j)
                C = bank(cnt, ("C", j))
                counted(v.tensor_scalar(ctmp[0][:], C, 0.0, NOEDGE, ALU.is_equal, ALU.mult))
                counted(v.tensor_scalar(ctmp[1][:], C, 1.0, None, ALU.max))
                top_c = counted(v.reduce_max(rowsum[:, 1, j:j + 1], C, AX.X))
                v.tensor_tensor(ctmp[2][:], C, Csum[:, j, :], ALU.add).then_inc(tile_taken, 1)
                dve.wait_ge(cnt_step, top_c)
                counted(v.tensor_scalar(hasedge[:, j:j + 1], rowsum[:, 1, j:j + 1], 1.0, None, ALU.min))
                taken(cnt, cnt.base, ("C", j))
                one = counted(v.tensor_scalar(ctmp[2][:], ctmp[2][:], 1.0, None, ALU.min))
                dve.wait_ge(cnt_step, one)
                d = ctmp[2][:, j * P:(j + 1) * P]
                loop = counted(v.tensor_tensor(d, d, ident[:], ALU.add))
                dve.wait_ge(cnt_step, loop)
                total = counted(v.reduce_sum(rowsum[:, 0, j:j + 1], ctmp[2][:], AX.X))
                counted(v.tensor_copy(adj[:, j, :], ctmp[2][:]))
                dve.wait_ge(cnt_step, total)
                counted(v.reciprocal(rinv[:, j:j + 1], rowsum[:, 0, j:j + 1]))
                dve.wait_ge(cnt_act, j + 1)
                counted(v.scalar_tensor_tensor(mask[:, j, :], ctmp[3][:], 1.0 / SCALE, ctmp[0][:], ALU.mult, ALU.add))
                assert step[0] == CNT * (j + 1)
                mix_some(3)
            assert not mixes
            dve.wait_ge(cnt_step, CNT * NT)
            for k in range(STEPS):
                v.tensor_scalar(rdw[:, k, :], rinv[:], dw[:, k + 1:k + 2], None, ALU.mult).then_inc(l2_step, 1)

            for t in range(NT):
                norm_stats(x[:, t, :], t, NT + t)
            for t in range(NT):
                normalise(xl[:, t, :], x[:, t, :], t, NT + t)
                dve.wait_ge(ln_xn, NT + t + 1)
                v.tensor_scalar(xl[:, t, :], xl[:, t, :], 0.0, None, ALU.max).then_inc(xl_ready, 1)
            dve.wait_ge(xl_ready, NT)
            dve.wait_ge(ct_stored, 32)

            with dve.Fori(0, BLOCKS) as i:
                b = i * PER + n1.base
                hb = i * PERH + HI1

                def lo(name, out, hi, **kw):
                    low(n1, b, name, hb + hi1[name], out, hi, **kw)

                def stats_of(s, t):
                    if s == "a":
                        dve.wait_ge(tile_taken, b + (n1.at[("X", t)] + 1 - PER))
                    norm_stats(xl[:, t, :], t, i * 8 + (8 + 4 * "ab".index(s) + t))

                def conditioned(s, t):
                    n = i * 8 + (8 + 4 * "ab".index(s) + t)
                    normalise(yp[:, t, :], xl[:, t, :], t, n)
                    dve.wait_ge(ln_xn, n + 1)
                    ready(n1, b, ("S" + s, t))
                    v.tensor_tensor(yp[:, t, :], yp[:, t, :], bank(n1, ("S" + s, t)), ALU.mult).then_inc(tile_taken, 1)
                    taken(n1, b, ("S" + s, t))
                    ready(n1, b, ("B" + s, t))
                    v.tensor_tensor(yp[:, t, :], yp[:, t, :], bank(n1, ("B" + s, t)), ALU.add).then_inc(tile_taken, 1)

                def transposed(s, t):
                    c = slice(t * P, (t + 1) * P)
                    lo(("T" + s, t), yT_l[:, :, c], yT_h[:, :, c])

                def value(t):
                    lo(("v", t), vm_l[:, t, :], vm_h[:, t, :])

                def residual(name, t):
                    ready(n1, b, (name, t))
                    v.tensor_tensor(xl[:, t, :], xl[:, t, :], bank(n1, (name, t)), ALU.add).then_inc(tile_taken, 1)

                def masked(h, j):
                    ready(n1, b, ("s", h, j))
                    hold()
                    v.tensor_tensor_reduce(out=yp[:, j, :], in0=bank(n1, ("s", h, j)), in1=mask[:, j, :], scale=-SCALE,
                                           scalar=3e38, op0=ALU.add, op1=ALU.min,
                                           accum_out=nmin[:, j:j + 1]).then_inc(tile_taken, 1)

                def probs(h, j):
                    n = i * 16 + (4 * h + j + 1)
                    dve.wait_ge(exp_ready, n)
                    v.reciprocal(rden[:, j:j + 1], rsum[:, j:j + 1]).then_inc(rden_ready, 1)
                    dve.wait_ge(rden_ready, n)
                    v.tensor_scalar(yp[:, j, :], yp[:, j, :], rden[:, j:j + 1], hasedge[:, j:j + 1], ALU.mult,
                                    ALU.mult).then_inc(probs_ready, 1)

                def attend(h):
                    for m in range(NT):
                        lo(("PT", h, m), PT_l[:, m, :], PT_h[:, m, :])
                    lo(("PV", h), oT_l[:, h, :], oT_h[:, h, :])

                order = [(g, s) for g in range(BASES // BSLOTS) for s in range(BSLOTS)]

                def mix_some(count):
                    for g, s in order[:count]:
                        mix_at(i + KT, g, s)
                    del order[:count]

                clear_mix(i + KT)
                stats_of("a", 0)
                stats_of("a", 1)
                conditioned("a", 0)
                stats_of("a", 2)
                conditioned("a", 1)
                transposed("a", 0)
                stats_of("a", 3)
                conditioned("a", 2)
                dve.wait_ge(braw_loaded, i * 96 + 96)
                v.tensor_copy(brow[:], braw[:]).then_inc(brow_hi, 1)
                dve.wait_ge(brow_hi, i + 1)
                v.scalar_tensor_tensor(brow[:], f(brow[:]), minus_odd[:], braw[:], ALU.mult, ALU.add).then_inc(brow_ready, 1)
                value(0)
                transposed("a", 1)
                conditioned("a", 3)
                value(1)
                mix_some(1)
                transposed("a", 2)
                value(2)
                mix_some(1)
                transposed("a", 3)
                value(3)
                mix_some(2)
                for h in range(HEADS):
                    lo(("q", h), qk_l[:, 0, :], qk_h[:, 0, :])
                    mix_some(1)
                    if h:
                        probs(h - 1, NT - 1)
                    lo(("k", h), qk_l[:, 1, :], qk_h[:, 1, :])
                    mix_some(2)
                    if h:
                        attend(h - 1)
                        mix_some(2)
                    masked(h, 0)
                    for j in range(1, NT):
                        masked(h, j)
                        probs(h, j - 1)
                probs(HEADS - 1, NT - 1)
                attend(HEADS - 1)
                mix_some(2)
                assert len(order) == (BASES // BSLOTS - EARLY) * BSLOTS
                for t in range(NT):
                    residual("o", t)
                    taken(n1, b, ("o", t))
                    stats_of("b", t)
                    conditioned("b", t)
                    if t:
                        transposed("b", t - 1)
                transposed("b", NT - 1)
                split_cond(0, i * 2 + 2)
                for m in range(KT):
                    lo(("M", m), vm_l[:, m, :], vm_h[:, m, :], func=ALU.max, scalar=0.0)
                    mix_some(1)
                split_cond(1, i * 2 + 3)
                mix_some(2)
                for t in range(NT):
                    residual("X", t)

            dve.wait_ge(tile_taken, n2.base)
            for t in range(NT):
                v.tensor_tensor(x[:, t, :], x[:, t, :], xl[:, t, :], ALU.add).then_inc(l2_step, 1)
            for t in range(NT):
                dve.wait_ge(l2_step, STEPS + t + 1)
                norm_stats(x[:, t, :], t, 40 + t)
            for t in range(NT):
                normalise(y2[:, t, :], x[:, t, :], t, 40 + t)
                dve.wait_ge(ln_xn, 40 + t + 1)
                v.tensor_scalar(y2[:, t, :], y2[:, t, :], 0.0, None, ALU.max).then_inc(y_ready, 1)
            v.tensor_copy(adj_r[:], adj[:]).then_inc(l2_step, 1)
            for t in range(NT):
                c = slice(t * P, (t + 1) * P)
                low(n2, n2.base, ("T", t), hi2[("T", t)], y2T_l[:, :, c], y2T_h[:, :, c])
            base = STEPS + NT + 1
            for t in range(NT):
                dve.wait_ge(hi_ready, hi2[("A", 0, t)] + 1)
                v.tensor_scalar(acc2[:, t, :], bank(n2, ("A", 0, t)), dw[:, 0:1], None, ALU.mult).then_inc(l2_step, 1)
                low(n2, n2.base, ("A", 0, t), hi2[("A", 0, t)], cur_l[:, 0, t, :], cur_h[:, 0, t, :])
            for k in range(1, STEPS + 1):
                for t in range(NT):
                    name = ("A", k, t)
                    if k < STEPS:
                        dve.wait_ge(hi_ready, hi2[name] + 1)
                    else:
                        ready(n2, n2.base, name)
                    dve.wait_ge(l2_step, base + 4 * (k - 1) + t + 1)
                    ins = v.scalar_tensor_tensor(acc2[:, t, :], bank(n2, name), rdw[:, k - 1, t:t + 1], acc2[:, t, :], ALU.mult, ALU.add)
                    if k < STEPS:
                        ins.then_inc(l2_step, 1)
                        low(n2, n2.base, name, hi2[name], cur_l[:, k % 2, t, :], cur_h[:, k % 2, t, :], func=ALU.mult,
                            scalar=rinv[:, t:t + 1])
                    else:
                        ins.then_inc(tile_taken, 1)
            for t in range(NT):
                taken(n2, n2.base, ("A", STEPS, t))
                v.scalar_tensor_tensor(x[:, t, :], acc2[:, t, :], 0.0, x[:, t, :], ALU.max, ALU.add).then_inc(l2_step, 1)

            base += 4 * STEPS
            for t in range(NT):
                dve.wait_ge(l2_step, base + t + 1)
                norm_stats(x[:, t, :], t, 44 + t)
            for t in range(NT):
                normalise(y3[:, t, :], x[:, t, :], t, 44 + t)
                dve.wait_ge(ln_xn, 44 + t + 1)
                v.tensor_scalar(y3[:, t, :], y3[:, t, :], 0.0, None, ALU.max).then_inc(y_ready, 1)
            for t in range(NT):
                c = slice(t * P, (t + 1) * P)
                low(n3, n3.base, ("T", t), hi3[("T", t)], hT_l[0][:, :, c], hT_h[0][:, :, c])
            for r in range(2):
                dve.wait_ge(c_hi, r + 1)
                v.tensor_tensor(C_l[:, r, :, :], Cr[r][:], f(C_h[:, r, :, :]), ALU.subtract).then_inc(c_ready, 1)
            for l in range(2):
                dve.wait_ge(gate_exp, l + 1)
                v.tensor_scalar(gate[:], ge[:], 1.0, None, ALU.add).then_inc(tile_taken, 1)
                taken(n3, n3.base, ("g", l))
                v.reciprocal(gate[:], gate[:]).then_inc(gate_step, 1)
                dve.wait_ge(gate_step, l + 1)
                for r in range(2):
                    for t in range(NT):
                        name = ("Z", l, r, t)
                        low(n3, n3.base, name, hi3[name], Z_l[:, r, t, :], Z_h[:, r, t, :], func=ALU.mult,
                            scalar=gate[:, 2 * t + r:2 * t + r + 1])
                for t in range(NT):
                    name = ("R", l, t)
                    if l == 0:
                        low(n3, n3.base, name, hi3[name], hT_l[1][:, t, :], hT_h[1][:, t, :], func=ALU.max, scalar=0.0)
                    else:
                        ready(n3, n3.base, name)
                        v.tensor_tensor(x[:, t, :], x[:, t, :], bank(n3, name), ALU.add).then_inc(tile_taken, 1)

        @block.tensor
        def _(pe):
            te = nc.tensor

            def begin(T, base, name):
                j = T.at[name]
                if j >= RING or not isinstance(base, int):
                    pe.wait_ge(tile_taken, base + (j - RING + 1))
                elif j == 0:
                    pe.wait_ge(tile_taken, base)
                return ring[:, T.bank(name), :]

            def taken(T, base, name):
                pe.wait_ge(tile_taken, base + (T.at[name] + 1))

            def multiply(out, pairs):
                for n, (l, r) in enumerate(pairs):
                    last = te.matmul(out, l, r, start=n == 0, stop=n == len(pairs) - 1)
                return last

            def three(lh, ll, rh, rl):
                return [(lh, rh), (lh, rl), (ll, rh)]

            def cols(ap, k, m):
                return ap[:, k, m * P:(m + 1) * P]

            def bias_to_rows(j, rows_ap):
                return (sel[:, j, :], rows_ap[:])

            def bias_to_columns(j, rows_ap, m):
                return (rows_ap[:, m * P:(m + 1) * P], sel[:, j:j + 1, :].broadcast_to([P, NT, P]))

            def transposes(out, ins):
                for n, ap in enumerate(ins):
                    last = te.transpose(out[:, n * P:(n + 1) * P], ap, ident[:])
                return last

            pe.wait_ge(const_ready, 2)
            pe.wait_ge(edges_loaded, 64)
            pe.wait_ge(table_ready, 1)
            out = ring[:, pre.bank("tab"), :]
            transposes(out, [efl[:, 0, :], efl[:, 1, :], efl[:, 2, :], ewt[:]]).then_inc(tile_ready, 1)
            pe.wait_ge(table_ready, 7)
            te.matmul(ring[:, pre.bank("flag"), 0:NT * TURNS], ones[:], turn_hit[:].rearrange("p m q -> p (m q)"),
                      start=True, stop=True).then_inc(tile_ready, 1)
            pe.wait_ge(small_loaded, 16 * SMALL)
            pe.wait_ge(emb_act, 1)
            te.matmul(ring[0:COND, pre.bank("z1"), :], fw1[:], rnd[:], start=True, stop=True).then_inc(tile_ready, 1)
            pe.wait_ge(emb_step, 7)
            te.matmul(ring[:, pre.bank("z2"), :], fw2[:], sil[0][:], start=True, stop=True).then_inc(tile_ready, 1)

            zeros = zero_l[:].unsqueeze(1).broadcast_to([P, NODES // P, P])
            pe.wait_ge(flags_ready, 1)
            for m in range(NT):
                if m == 1:
                    pe.wait_ge(tile_taken, pre.end)
                if m >= 2:
                    pe.wait_ge(pass_act, 2 * m - 2)
                    pe.wait_ge(pass_dve, m - 1)
                bits = pe.value_load(turn_bits[0:1, m:m + 1], min_val=0, max_val=2 ** TURNS - 1)
                ps_w, ps_c, ps_c1 = edge_ps[m]
                for ps in edge_ps[m]:
                    last = te.matmul(ps, zero_l[:], zeros, start=True, stop=False)
                if m == 0:
                    last.then_inc(onehot_used, SLOTS)
                with pe.Fori(0, TURNS) as q:
                    with pe.If(((bits >> q) & 1) > 0):
                        for u in range(BODY):
                            n = q * BODY + (m * ET + u)
                            s = u % SLOTS
                            pe.wait_ge(onehot_ready, n + 1)
                            te.matmul(ps_c, ohd[:, s, 0, :], ohs[:, s, :], start=False, stop=False)
                            pe.wait_ge(scaled_ready, n + 1)
                            for r, ps in ((1, ps_c1), (2, ps_w), (3, ps_w)):
                                last = te.matmul(ps, ohd[:, s, r, :], ohs[:, s, :], start=False, stop=False)
                            last.then_inc(onehot_used, 1)
                    with pe.Else():
                        pe.drain().then_inc(onehot_used, BODY)
                for ps in edge_ps[m]:
                    last = te.matmul(ps, zero_l[:], zeros, start=False, stop=True)
                last.then_inc(pass_ready, 1)

            pe.wait_ge(pass_act, 2 * NT)
            pe.wait_ge(pass_dve, NT)
            out = begin(mid, mid.base, "deg")
            for j in range(NT):
                last = multiply(out[:, 2 * j:2 * j + 2], [(cols(Araw, m, j), ones[:, 0:2]) for m in range(NT)])
            last.then_inc(tile_ready, 1)
            pe.wait_ge(deg_step, 2 + NT)
            out = begin(mid, mid.base, "dinv")
            for j in range(NT):
                last = te.matmul(out[:, j * P:(j + 1) * P], ones[:], diag[:, j, :], start=True, stop=True)
            last.then_inc(tile_ready, 1)

            pe.wait_ge(sel_step, 8)
            pe.wait_ge(deg_step, 2 + 3 * NT)
            pe.wait_ge(h0_ready, NT)
            for l in range(2):
                B = n0.base
                hh, hl, gh, gl, uh, ul = hb_h[l], hb_l[l], hb_h[1 - l], hb_l[1 - l], hb_h[l], hb_l[l]
                if l:
                    taken(n0, B, ("H", 0, NT - 1))
                for m in range(KT):
                    out = begin(n0, B, ("G", l, m))
                    multiply(out, [p for t in range(NT) for p in three(cols(hh, t, m), cols(hl, t, m), An_h[:, t, :], An_l[:, t, :])]
                             ).then_inc(tile_ready, 1)
                s = slot(2 * l)
                pe.wait_ge(weight_lo, 2 * l + 1)
                taken(n0, B, ("G", l, KT - 1))
                for m in range(KT):
                    out = begin(n0, B, ("U", l, m))
                    multiply(out, [bias_to_columns(2 * l, bias_rows, m)]
                             + [p for k in range(KT) for p in three(cols(wh[s], k, m), cols(wl[s], k, m), gh[:, k, :], gl[:, k, :])]
                             ).then_inc(tile_ready, 1)
                s = slot(2 * l + 1)
                pe.wait_ge(weight_lo, 2 * l + 2)
                taken(n0, B, ("U", l, KT - 1))
                for t in range(NT):
                    out = begin(n0, B, ("H", l, t))
                    multiply(out, [bias_to_rows(2 * l + 1, bias_rows)]
                             + [p for k in range(KT) for p in three(cols(uh, k, t), cols(ul, k, t), wh[s][:, k, :], wl[s][:, k, :])]
                             ).then_inc(tile_ready, 1)

            for j in range(NT):
                out = begin(cnt, cnt.base, ("C", j))
                transposes(out, [cols(Csum, m, j) for m in range(NT)]).then_inc(tile_ready, 1)

            pe.wait_ge(tile_taken, n1.base)
            pe.wait_ge(emb_step, 9)
            with pe.Fori(0, BLOCKS) as i:
                b = i * PER + n1.base

                def weight(j):
                    pe.wait_ge(weight_lo, i * 6 + (W1 + j + 1))
                    return wh[j % 3], wl[j % 3]

                def done(name):
                    taken(n1, b, name)

                def tile(name, pairs):
                    multiply(begin(n1, b, name), pairs).then_inc(tile_ready, 1)

                def condition(s, t):
                    n = "ab".index(s)
                    if t == 0:
                        pe.wait_ge(cond_ready, i * 2 + (n + 1))
                    tile(("S" + s, t), [(stk[:, t * P:(t + 1) * P], cond[:, 2 * n, :])])
                    tile(("B" + s, t), [(stk[:, t * P:(t + 1) * P], cond[:, 2 * n + 1, :])])

                def transpose_rows(s, t):
                    done(("B" + s, t))
                    out = begin(n1, b, ("T" + s, t))
                    transposes(out, [cols(yp, t, k) for k in range(KT)]).then_inc(tile_ready, 1)

                def rows_product(name, t, lh, ll, w, bias):
                    tile((name, t), [bias_to_rows(bias, brow)] + [p for k in range(KT) for p in
                         three(cols(lh, k, t), cols(ll, k, t), w[0][:, k, :], w[1][:, k, :])])

                def columns_product(name, m, w, rh, rl, bias):
                    tile((name, m), [bias_to_columns(bias, brow, m)] + [p for k in range(KT) for p in
                         three(cols(w[0], k, m), cols(w[1], k, m), rh[:, k, :], rl[:, k, :])])

                def value(t, w):
                    done(("Ta", t))
                    rows_product("v", t, yT_h, yT_l, w, 0)

                def attend(h):
                    pe.wait_ge(probs_ready, i * 16 + (4 * h + 4))
                    for m in range(NT):
                        out = begin(n1, b, ("PT", h, m))
                        transposes(out, [cols(yp, j, m) for j in range(NT)]).then_inc(tile_ready, 1)
                    done(("PT", h, NT - 1))
                    tile(("PV", h), [p for m in range(NT) for p in
                                     three(cols(vm_h, m, h), cols(vm_l, m, h), PT_h[:, m, :], PT_l[:, m, :])])

                condition("a", 0)
                condition("a", 1)
                transpose_rows("a", 0)
                condition("a", 2)
                w = weight(0)
                pe.wait_ge(brow_ready, i + 1)
                value(0, w)
                transpose_rows("a", 1)
                condition("a", 3)
                value(1, w)
                transpose_rows("a", 2)
                value(2, w)
                transpose_rows("a", 3)
                value(3, w)
                wq, wk = weight(1), weight(2)
                for h in range(HEADS):
                    columns_product("q", h, wq, yT_h, yT_l, 1)
                    columns_product("k", h, wk, yT_h, yT_l, 2)
                    if h:
                        attend(h - 1)
                    done(("k", h))
                    for j in range(NT):
                        tile(("s", h, j), three(qk_h[:, 0, j * P:(j + 1) * P], qk_l[:, 0, j * P:(j + 1) * P], qk_h[:, 1, :], qk_l[:, 1, :]))
                attend(HEADS - 1)
                w = weight(3)
                done(("PV", HEADS - 1))
                for t in range(NT):
                    rows_product("o", t, oT_h, oT_l, w, 3)
                    condition("b", t)
                    if t:
                        transpose_rows("b", t - 1)
                transpose_rows("b", NT - 1)
                w = weight(4)
                done(("Tb", NT - 1))
                for m in range(KT):
                    columns_product("M", m, w, yT_h, yT_l, 4)
                w = weight(5)
                done(("M", KT - 1))
                for t in range(NT):
                    rows_product("X", t, vm_h, vm_l, w, 5)

            B = n2.base
            for t in range(NT):
                pe.wait_ge(y_ready, t + 1)
                transposes(begin(n2, B, ("T", t)), [cols(y2, t, k) for k in range(KT)]).then_inc(tile_ready, 1)
            pe.wait_ge(weight_lo, W2 + 1)
            s = slot(W2)
            for t in range(NT):
                taken(n2, B, ("T", t))
                multiply(begin(n2, B, ("A", 0, t)), [bias_to_rows(4, bias_rows)] + [p for k in range(KT) for p in
                         three(cols(y2T_h, k, t), cols(y2T_l, k, t), wh[s][:, k, :], wl[s][:, k, :])]).then_inc(tile_ready, 1)
            pe.wait_ge(l2_step, STEPS + NT + 1)
            for k in range(1, STEPS + 1):
                c = (k - 1) % 2
                taken(n2, B, ("A", k - 1, NT - 1))
                for t in range(NT):
                    multiply(begin(n2, B, ("A", k, t)), [p for m in range(NT) for p in
                             ((cols(adj_r, m, t), cur_h[:, c, m, :]), (cols(adj_r, m, t), cur_l[:, c, m, :]))]).then_inc(tile_ready, 1)

            B = n3.base
            for t in range(NT):
                pe.wait_ge(y_ready, NT + t + 1)
                transposes(begin(n3, B, ("T", t)), [cols(y3, t, k) for k in range(KT)]).then_inc(tile_ready, 1)
            for l in range(2):
                h, hl = hT_h[l], hT_l[l]
                taken(n3, B, ("T", NT - 1) if l == 0 else ("R", 0, KT - 1))
                out = begin(n3, B, ("g", l))
                for t in range(NT):
                    last = multiply(out[:, 2 * t:2 * t + 2], [p for k in range(KT) for p in
                                    three(cols(h, k, t), cols(hl, k, t), gwh[:, l, k, :], gwl[:, l, k, :])])
                last.then_inc(tile_ready, 1)
                for r in range(2):
                    w = W3 + 3 * l + r
                    pe.wait_ge(weight_lo, w + 1)
                    for t in range(NT):
                        multiply(begin(n3, B, ("Z", l, r, t)), [p for k in range(KT) for p in
                                 three(cols(h, k, t), cols(hl, k, t), wh[slot(w)][:, k, :], wl[slot(w)][:, k, :])]).then_inc(tile_ready, 1)
                w = W3 + 3 * l + 2
                pe.wait_ge(weight_lo, w + 1)
                wrh, wrl = wh[slot(w)], wl[slot(w)]
                pe.wait_ge(c_ready, 2)
                taken(n3, B, ("Z", l, 1, NT - 1))
                for m in range(NT):
                    if l == 0:
                        pairs = [bias_to_columns(5, bias_rows, m)]
                        pairs += [p for k in range(KT) for p in three(cols(wrh, k, m), cols(wrl, k, m), h[:, k, :], hl[:, k, :])]
                        pairs += [p for r in range(2) for t in range(NT) for p in
                                  three(Z_h[:, r, t, m * P:(m + 1) * P], Z_l[:, r, t, m * P:(m + 1) * P], C_h[:, r, t, :], C_l[:, r, t, :])]
                    else:
                        pairs = [bias_to_rows(6, bias_rows)]
                        pairs += [p for k in range(KT) for p in three(cols(h, k, m), cols(hl, k, m), wrh[:, k, :], wrl[:, k, :])]
                        pairs += [p for r in range(2) for t in range(NT) for p in
                                  three(C_h[:, r, t, m * P:(m + 1) * P], C_l[:, r, t, m * P:(m + 1) * P], Z_h[:, r, t, :], Z_l[:, r, t, :])]
                    multiply(begin(n3, B, ("R", l, m)), pairs).then_inc(tile_ready, 1)


SMALL = 8 + 7 + 1 + 2 + 6 + 1
CNT = 10
EARLY = 8


_L0 = ["W_gcn", "b_gcn", "W_mlp", "b_mlp"]
_L1 = ["f_w1", "f_b1", "f_w2", "f_b2", "s1_w", "s1_b", "b1_w", "b1_b", "wq", "bq", "wk", "bk", "wv", "bv", "wo", "bo",
       "s2_w", "s2_b", "b2_w", "b2_b", "m_w1", "m_b1", "m_w2", "m_b2"]
_L2 = ["W", "b", "diffusion_weights"]
_L3 = [f"{n}{l}" for l in (1, 2) for n in ("basis", "att", "gate_w", "root", "bias")]
_INS = (["x", "src", "dst", "edge_type_2", "edge_weight", "node_vec1"] + [f"L0_gnn_{n}" for n in _L0]
        + [f"L1_gnn_{n}" for n in _L1] + [f"L2_gnn_{n}" for n in _L2] + [f"L3_gnn_{n}" for n in _L3])


def kernel(**inputs):
    import numpy as _np
    import concourse.bacc as _bacc
    from concourse import mybir as _mybir
    from concourse.bass_utils import run_bass_kernel_spmd as _run

    nc = _bacc.Bacc("TRN2", target_bir_lowering=False, num_devices=1)
    arrays, d = {}, {}
    for name in _INS:
        a = _np.ascontiguousarray(inputs[name])
        arrays[f"in_{name}"] = a
        d[name] = nc.dram_tensor(f"in_{name}", a.shape, _mybir.dt.from_np(a.dtype), kind="ExternalInput").ap()
    out = nc.dram_tensor("out", (NODES, D), _mybir.dt.float32, kind="ExternalOutput").ap()
    mix_d = nc.dram_tensor("mix_scratch", (2, 2, P, KT * D), _mybir.dt.float32).ap()
    ct_d = nc.dram_tensor("count_scratch", (2, P, NT, NODES), _mybir.dt.int16).ap()
    l0 = {n: d[f"L0_gnn_{n}"] for n in _L0}
    l1 = {n: d[f"L1_gnn_{n}"] for n in _L1}
    l2 = {"W": d["L2_gnn_W"], "b": d["L2_gnn_b"], "dw": d["L2_gnn_diffusion_weights"]}
    l3 = {n: [d[f"L3_gnn_{n}{l}"] for l in (1, 2)] for n in ("basis", "att", "gate_w", "root", "bias")}
    program(nc, d["x"], d["src"], d["dst"], d["edge_type_2"], d["edge_weight"], d["node_vec1"], l0, l1, l2, l3, out, mix_d, ct_d)
    r = _run(nc, [arrays], core_ids=[0])
    return r.results[0]["out"]
```

```python
from contextlib import ExitStack

import concourse.bass as bass
from concourse import mybir

ALU = mybir.AluOpType
ACT = mybir.ActivationFunctionType
AX = mybir.AxisListType
F32 = mybir.dt.float32
F32R = mybir.dt.float32r
I32 = mybir.dt.int32
I16 = mybir.dt.int16
U8 = mybir.dt.uint8

P = 128
NODES = 512
D = 512
NT = NODES // P
KT = D // P
EDGES = 16384
ET = EDGES // P
BODY = 8
SPAN = 4
TURNS = ET // BODY
SLOTS = 4
HEADS = 4
DH = D // HEADS
BLOCKS = 4
FREQS = 32
PERIOD = 16
COND = 16
BASES = 30
BSLOTS = 3
PIECES = ((0, 0), (0, 1), (1, 3))
QUADS = 4
SHIFTS = 16
PAIR = 2
UNITS = SHIFTS // PAIR
SET_ROWS = QUADS * SHIFTS
SETS0 = (D - 2 * P) // SET_ROWS
SETS1 = (D - P) // SET_ROWS
SETS = SETS0 + SETS1
EARLY_SETS = 5
STEPS = 3
RING = 7
EPS = 1e-5
SCALE = DH ** -0.5
NOEDGE = -1e30
MAGIC = 1.5 * 2 ** 23
TURN = 6.283185


class Tiles:

    def __init__(self, names, base, banks=None):
        self.at = {n: j for j, n in enumerate(names)}
        self.base, self.n, self.banks = base, len(names), banks
        self.end = base + len(names)

    def bank(self, name):
        return self.banks[name] if self.banks else self.at[name] % RING


def l1_order():
    ln = lambda s, t: [("S" + s, t), ("B" + s, t)]
    scores = lambda h: [("s", h, j) for j in range(NT)]
    PT = lambda h: [("PT", h, m) for m in range(NT)]
    o = ln("a", 0) + ln("a", 1) + [("Ta", 0)] + ln("a", 2) + [("Ta", 1), ("v", 0)] + ln("a", 3)
    o += [("Ta", 2), ("v", 1), ("Ta", 3)]
    o += [("q", 0), ("k", 0), ("v", 2)] + scores(0) + [("q", 1), ("k", 1)]
    for h in range(1, HEADS):
        o += PT(h - 1) + ([("v", 3)] if h == 1 else []) + scores(h) + [("PV", h - 1)]
        if h + 1 < HEADS:
            o += [("q", h + 1), ("k", h + 1)]
    o += PT(HEADS - 1) + [("PV", HEADS - 1)]
    o += [("o", 0), ("o", 1)] + ln("b", 0) + ln("b", 1) + [("o", 2), ("Tb", 0), ("Tb", 1)] + ln("b", 2)
    o += [("o", 3)] + ln("b", 3) + [("Tb", 2), ("Tb", 3)]
    o += [("M", m) for m in range(KT)] + [("X", t) for t in range(NT)]
    return o


def program(nc, x_d, src_d, dst_d, type_d, w_d, noise_d, l0, l1, l2, l3, out_d, mix_d, ct_d, x_s):
    top = ExitStack()
    with top:
        def sb(name, shape, dt=F32, ctx=top):
            return ctx.enter_context(nc.sbuf_tensor(name, shape, dt))

        def sem(name):
            return top.enter_context(nc.semaphore(name))

        pre = Tiles(["tab", "flag", "z1", "z2"], 0, {"tab": 0, "flag": 1, "z1": 0, "z2": 0})
        mid = Tiles(["deg", "dinv"], pre.end)
        n0 = Tiles([(s, l, t) for l in range(2) for s in ("G", "U", "H") for t in range(4)], mid.end)
        cnt = Tiles([("C", j) for j in range(NT)], n0.end)
        order1 = l1_order()
        n1 = Tiles(order1, cnt.end)
        assert n1.n % RING == 0
        PER = n1.n
        n2 = Tiles([("T", t) for t in range(4)] + [("A", k, t) for k in range(STEPS + 1) for t in range(4)],
                   n1.base + BLOCKS * PER)
        n3 = Tiles([("T", t) for t in range(4)]
                   + [n for l in range(2) for n in [("g", l)] + [("Z", l, r, t) for r in range(2) for t in range(4)]
                      + [("R", l, t) for t in range(4)]], n2.end)

        def highs(names, base):
            return {n: base + j for j, n in enumerate(names)}, base + len(names)

        hi0, e = highs([n for n in n0.at if n[0] != "H" or n[1] == 0], 0)
        HI1 = e
        names1 = [n for n in order1 if n[0] in ("Ta", "v", "q", "k", "PT", "PV", "Tb", "M")]
        hi1 = {n: j for j, n in enumerate(names1)}
        PERH = len(names1)
        hi2, e = highs([n for n in n2.at if n[0] == "T" or n[1] < STEPS], HI1 + BLOCKS * PERH)
        hi3, e = highs([n for n in n3.at if n[0] in ("T", "Z") or (n[0] == "R" and n[1] == 0)], e)

        x = sb("x", [P, NT, D])
        mask = sb("mask", [P, NT, NODES])
        adj = sb("adj", [P, NT, NODES], U8)
        ident = sb("ident", [P, P])
        ones = sb("ones", [P, P])
        sel = sb("sel", [P, 7, P], F32R)
        stk = sb("stk", [P, NODES], F32R)
        bias_rows = sb("bias_rows", [P, D], F32R)
        rowno = sb("rowno", [P, 1], I32)
        minus_odd = sb("minus_odd", [P, 1])
        minus_low = sb("minus_low", [P, 1])
        minus_loww = sb("minus_loww", [P, 1])
        half = sb("half", [P, NT])
        hasedge = sb("hasedge", [P, NT])
        rinv = sb("rinv", [P, NT])
        stats = sb("stats", [P, NT, 6])
        mv = sb("mv", [P, NT, 2])
        ve = sb("ve", [P, NT])
        rstd = sb("rstd", [P, NT])
        pace = sb("pace", [P, 64])
        nmin = sb("nmin", [P, 2, NT])
        rsum = sb("rsum", [P, 2, NT])
        rden = sb("rden", [P, 2, NT])
        dw = sb("dw", [P, STEPS + 1])
        rdw = sb("rdw", [P, STEPS, NT])
        gw = sb("gw", [P, 2, KT, 2])
        gwh = sb("gwh", [P, 2, KT, 2], F32R)
        gwl = sb("gwl", [P, 2, KT, 2], F32R)
        ge = sb("ge", [P, 2 * NT])
        gate = sb("gate", [P, 2 * NT])
        att = sb("att", [P, 2, 2 * BASES])
        att_shift = sb("att_shift", [P, 2, SHIFTS - 1 + P])
        mixing = ExitStack()
        quad = sb("quad", [P, 2, PAIR, D], ctx=mixing)
        mixed = sb("mixed", [P, D], ctx=mixing)
        mixing.close()
        bas1 = sb("bas1", [P, BSLOTS, D])
        macc1 = sb("macc1", [P, 2, D])
        wraw = [sb(f"wraw{s}", [P, KT, D]) for s in range(2)]
        wh = [sb(f"wh{s}", [P, KT, D], F32R) for s in range(3)]
        wl = [sb(f"wl{s}", [P, KT, D], F32R) for s in range(3)]

        cg = ExitStack()
        craw = sb("craw", [P, 2, D], ctx=cg)
        cond = sb("cond", [P, 4, D], F32R, ctx=cg)
        braw = sb("braw", [P, D], ctx=cg)
        brow = sb("brow", [P, D], F32R, ctx=cg)
        ec = ExitStack()
        Araw = sb("Araw", [P, NT, NODES], ctx=ec)
        Csum = sb("Csum", [P, NT, NODES], ctx=ec)
        CT = [sb(f"CT{r}", [P, NT, NODES], I16, ctx=ec) for r in range(2)]
        ec2 = ExitStack()
        eint = sb("eint", [P, 3, P], I32, ctx=ec2)
        ewt = sb("ewt", [P, P], ctx=ec2)
        efl = sb("efl", [P, 3, P], ctx=ec2)
        srcT = sb("srcT", [P, ET], ctx=ec2)
        dstT = sb("dstT", [P, ET], ctx=ec2)
        whiT = sb("whiT", [P, ET], F32R, ctx=ec2)
        wloT = sb("wloT", [P, ET], ctx=ec2)
        isr1 = sb("isr1", [P, ET], ctx=ec2)
        iota = sb("iota", [P, NODES], ctx=ec2)
        zero_l = sb("zero_l", [P, P], F32R, ctx=ec2)
        ohs = sb("ohs", [P, SLOTS, NODES], F32R, ctx=ec2)
        ohd = sb("ohd", [P, SLOTS, 4, P], F32R, ctx=ec2)
        eblk = sb("eblk", [P, P], I32, ctx=ec2)
        hit = sb("hit", [P, NT, P], ctx=ec2)
        tile_hit = sb("tile_hit", [P, NT], ctx=ec2)
        turn_of = sb("turn_of", [P, 3, TURNS], ctx=ec2)
        turn_hit = sb("turn_hit", [P, NT, TURNS], ctx=ec2)
        pow2 = sb("pow2", [P, NT, TURNS], ctx=ec2)
        bits_f = sb("bits_f", [P, NT], ctx=ec2)
        turn_bits = sb("turn_bits", [P, NT], I32, ctx=ec2)
        bias_raw = sb("bias_raw", [P, D], ctx=ec2)
        selv = sb("selv", [P, 2, 7, P], ctx=ec2)
        noise = sb("noise", [2 * FREQS, NODES], ctx=ec2)
        rnd = sb("rnd", [2 * FREQS, NODES], ctx=ec2)
        freq = sb("freq", [2 * FREQS, 1], ctx=ec2)
        quarter = sb("quarter", [2 * FREQS, 1], ctx=ec2)
        fw1 = sb("fw1", [2 * FREQS, COND], ctx=ec2)
        fb1 = sb("fb1", [COND, 1], ctx=ec2)
        fw2 = sb("fw2", [COND, P], ctx=ec2)
        cb = sb("cb", [P, 1], ctx=ec2)
        sil = [sb(f"sil{i}", [COND, NODES], ctx=ec2) for i in range(2)]
        ec2.close()
        An_h = sb("An_h", [P, NT, NODES], F32R, ctx=ec)
        An_l = sb("An_l", [P, NT, NODES], F32R, ctx=ec)
        hb_h = [sb(f"hb_h{i}", [P, NT, D], F32R, ctx=ec) for i in range(2)]
        hb_l = [sb(f"hb_l{i}", [P, NT, D], F32R, ctx=ec) for i in range(2)]
        D2 = sb("D2", [P, NODES], ctx=ec)
        xn0 = mask
        slope, hv = mask[:, 0:2, :], mask[:, 2:4, :]
        dg = sb("dg", [P, 4, NT], ctx=ec)
        diag = sb("diag", [P, NT, P], ctx=ec)
        bas = sb("bas", [P, BSLOTS, D], ctx=ec)
        macc = sb("macc", [P, 2, D], ctx=ec)
        ec.close()
        c1 = ExitStack()
        xl = sb("xl", [P, NT, D], ctx=c1)
        yp = sb("yp", [P, NT, D], ctx=c1)
        probs_of = [yp, x]
        yT_h = sb("yT_h", [P, KT, NODES], F32R, ctx=c1)
        yT_l = sb("yT_l", [P, KT, NODES], F32R, ctx=c1)
        vm_h = sb("vm_h", [P, NT, D], F32R, ctx=c1)
        vm_l = sb("vm_l", [P, NT, D], F32R, ctx=c1)
        qk_h = sb("qk_h", [P, 2, NODES], F32R, ctx=c1)
        qk_l = sb("qk_l", [P, 2, NODES], F32R, ctx=c1)
        PT_h = sb("PT_h", [P, NT, NODES], F32R, ctx=c1)
        PT_l = sb("PT_l", [P, NT, NODES], F32R, ctx=c1)
        oT_h = sb("oT_h", [P, HEADS, NODES], F32R, ctx=c1)
        oT_l = sb("oT_l", [P, HEADS, NODES], F32R, ctx=c1)
        c1.close()
        cc = ExitStack()
        Cskip = sb("Cskip", [P, 3 * NT, NODES], ctx=cc)
        ctmp = [sb(f"ctmp{i}", [P, NODES], ctx=cc) for i in range(3)]
        both = sb("both", [P, NT, NODES], ctx=cc)
        rowsum = sb("rowsum", [P, 2, NT], ctx=cc)
        cc.close()
        cg.close()
        c2 = ExitStack()
        y2 = sb("y2", [P, NT, D], ctx=c2)
        y2T_h = sb("y2T_h", [P, KT, NODES], F32R, ctx=c2)
        y2T_l = sb("y2T_l", [P, KT, NODES], F32R, ctx=c2)
        adj_r = sb("adj_r", [P, NT, NODES], F32R, ctx=c2)
        cur_h = sb("cur_h", [P, 2, NT, D], F32R, ctx=c2)
        cur_l = sb("cur_l", [P, 2, NT, D], F32R, ctx=c2)
        acc2 = sb("acc2", [P, NT, D], ctx=c2)
        c2.close()
        c3 = ExitStack()
        Z_h = sb("Z_h", [P, 2, NT, D], F32R, ctx=c3)
        Z_l = sb("Z_l", [P, 2, NT, D], F32R, ctx=c3)
        C_h = sb("C_h", [P, 2, NT, NODES], F32R, ctx=c3)
        C_l = sb("C_l", [P, 2, NT, NODES], F32R, ctx=c3)
        hT_h = [sb("hT_h0", [P, KT, NODES], F32R, ctx=c3)]
        hT_l = [sb("hT_l0", [P, KT, NODES], F32R, ctx=c3)]
        c3y = ExitStack()
        y3 = sb("y3", [P, NT, D], ctx=c3y)
        c3y.close()
        hT_h.append(sb("hT_h1", [P, KT, NODES], F32R, ctx=c3))
        hT_l.append(sb("hT_l1", [P, KT, NODES], F32R, ctx=c3))
        Cr = [sb(f"Cr{r}", [P, NT, NODES], I16, ctx=c3) for r in range(2)]
        c3.close()

        ring = top.enter_context(nc.psum_tensor("ring", [P, RING, 512], F32))
        mix_ps = top.enter_context(nc.psum_tensor("mix_ps", [P, D], F32))
        edge_ps = [[ring[:, 4 - 3 * (m % 2) + j, :] for j in range(3)] for m in range(NT)]

        const_ready = sem("const_ready")
        const_step = sem("const_step")
        sel_step = sem("sel_step")
        small_loaded = sem("small_loaded")
        x_loaded = sem("x_loaded")
        x_stored = sem("x_stored")
        edges_loaded = sem("edges_loaded")
        tile_ready = sem("tile_ready")
        tile_taken = sem("tile_taken")
        hi_ready = sem("hi_ready")
        table_ready = sem("table_ready")
        whi_ready = sem("whi_ready")
        flags_ready = sem("flags_ready")
        dst_ready = sem("dst_ready")
        onehot_ready = sem("onehot_ready")
        scaled_ready = sem("scaled_ready")
        onehot_used = sem("onehot_used")
        pass_ready = sem("pass_ready")
        pass_act = sem("pass_act")
        pass_dve = sem("pass_dve")
        ct_stored = sem("ct_stored")
        ct_loaded = sem("ct_loaded")
        basis_loaded = [sem(f"basis_loaded{s}") for s in range(BSLOTS)]
        basis_used = sem("basis_used")
        mix_stored = sem("mix_stored")
        quad_loaded = [sem(f"quad_loaded{s}") for s in range(2)]
        quad_used = sem("quad_used")
        set_taken = sem("set_taken")
        set_stored = sem("set_stored")
        emb_step = sem("emb_step")
        emb_act = sem("emb_act")
        deg_step = sem("deg_step")
        deg_act = sem("deg_act")
        deg_pool = sem("deg_pool")
        cnt_step = sem("cnt_step")
        cnt_act = sem("cnt_act")
        adj_step = sem("adj_step")
        row_sums = sem("row_sums")
        weight_loaded = [sem(f"weight_loaded{s}") for s in range(2)]
        weight_hi = sem("weight_hi")
        weight_lo = sem("weight_lo")
        ln_stats = sem("ln_stats")
        ln_mv = sem("ln_mv")
        ln_var = sem("ln_var")
        ln_rstd = sem("ln_rstd")
        ln_xn = sem("ln_xn")
        h0_hi = sem("h0_hi")
        h0_ready = sem("h0_ready")
        slope_ready = sem("slope_ready")
        leaky_ready = sem("leaky_ready")
        xl_ready = sem("xl_ready")
        cond_clear = sem("cond_clear")
        cond_loaded = sem("cond_loaded")
        cond_hi = sem("cond_hi")
        cond_ready = sem("cond_ready")
        braw_loaded = sem("braw_loaded")
        brow_hi = sem("brow_hi")
        brow_ready = sem("brow_ready")
        exp_ready = sem("exp_ready")
        rden_ready = sem("rden_ready")
        probs_ready = sem("probs_ready")
        y_ready = sem("y_ready")
        l2_step = sem("l2_step")
        c_hi = sem("c_hi")
        c_ready = sem("c_ready")
        gate_exp = sem("gate_exp")
        gate_step = sem("gate_step")
        out_stored = sem("out_stored")

        block = top.enter_context(nc.Block())

        def rows(ap):
            return ap.rearrange("(t p) n -> p t n", p=P)

        W1 = 4
        W2 = W1 + 6 * BLOCKS
        W3 = W2 + 1
        slot = lambda w: (w + 2) % 3

        def last_use(w):
            if w < W1:
                return n0.base + n0.at[(("U", "H")[w % 2], w // 2, 3)]
            if w < W2:
                i, j = divmod(w - W1, 6)
                return n1.base + i * PER + n1.at[(("v", "q", "k", "o", "M", "X")[j], 3)]
            if w == W2:
                return n2.base + n2.at[("A", 0, 3)]
            l, j = divmod(w - W3, 3)
            return n3.base + n3.at[("Z", l, j, 3) if j < 2 else ("R", l, 3)]

        def block_weight(i, j):
            return l1[("wv", "wq", "wk", "wo", "m_w1", "m_w2")[j]][bass.ds(i, 1)].rearrange("a (t p) n -> p (a t) n", p=P)

        def weight_source(w):
            if w < W1:
                return rows(l0[("W_gcn", "W_mlp")[w % 2]][w // 2])
            if w < W2:
                return block_weight(*divmod(w - W1, 6))
            if w == W2:
                return rows(l2["W"])
            l, j = divmod(w - W3, 3)
            return rows(mix_d[l, j]) if j < 2 else rows(l3["root"][l])

        scales = [None, isr1[:], wloT[:], whiT[:].bitcast(F32)]
        scaled_by_act = lambda u: 4 - u % 2

        @block.sync
        def _(sp):
            for t, d in enumerate((src_d, dst_d, type_d)):
                sp.dma_start(eint[:, t, :], d.rearrange("(t p) -> t p", p=P)).then_inc(edges_loaded, 16)
            sp.dma_start(ewt[:], w_d.rearrange("(t p) -> t p", p=P)).then_inc(edges_loaded, 16)
            sp.dma_start(x[:], rows(x_d)).then_inc(x_loaded, 16)

            sp.wait_ge(const_ready, 1)
            n_small = [0]

            def small(dst, src):
                sp.dma_start(dst, src, allow_slow_non_contiguous=True).then_inc(small_loaded, 16)
                n_small[0] += 1

            for l in range(2):
                small(att[:, l, :], l3["att"][l].rearrange("(a r) b -> a (r b)", a=1).broadcast_to([P, 2 * BASES]))
                for i in range(QUADS):
                    c = SHIFTS - 1 + i * SHIFTS
                    small(att_shift[i * BASES:(i + 1) * BASES, l, c:c + SET_ROWS + 1:SET_ROWS], l3["att"][l].rearrange("r b -> b r"))
            for l in range(2):
                for r in range(2):
                    small(gw[:, l, :, r], l3["gate_w"][l][r, :, 0].rearrange("(k p) -> p k", p=P))
            vecs = [l0["b_gcn"][0:1], l0["b_mlp"][0:1], l0["b_gcn"][1:2], l0["b_mlp"][1:2]]
            vecs += [b.rearrange("(a d) -> a d", a=1) for b in (l2["b"], l3["bias"][0], l3["bias"][1])]
            for j, v in enumerate(vecs):
                small(bias_raw[2 * j:2 * j + 2, :], v.broadcast_to([2, D]))
            small(noise[:], noise_d.rearrange("n a -> a n").broadcast_to([2 * FREQS, NODES]))
            small(fw1[:], l1["f_w1"])
            small(fb1[:], l1["f_b1"].rearrange("(c a) -> c a", a=1))
            for g in range(3):
                small(fw2[:, 32 * g:32 * g + COND], l1["f_w2"])
                small(cb[32 * g:32 * g + COND, :], l1["f_b2"].rearrange("(c a) -> c a", a=1))
            small(dw[:], l2["dw"].rearrange("(a d) -> a d", a=1).broadcast_to([P, STEPS + 1]))
            assert n_small[0] == SMALL

            def load_cond(b, n, ready):
                if ready is not None:
                    sp.wait_ge(cond_ready, ready)
                for k in range(2):
                    w_, b_ = l1[("s", "b")[k] + f"{n + 1}_w"], l1[("s", "b")[k] + f"{n + 1}_b"]
                    for g in range(3):
                        sp.dma_start(craw[32 * g:32 * g + COND, k, :],
                                     w_[bass.ds(b, 1)].rearrange("a c d -> (a c) d")).then_inc(cond_loaded, 16)
                    sp.dma_start(craw[96:98, k, :], b_[bass.ds(b, 1)].broadcast_to([2, D])).then_inc(cond_loaded, 16)

            sp.wait_ge(cond_clear, 1)
            load_cond(0, 0, None)

            def first_row(t):
                if isinstance(t, int) and t < SETS0:
                    return 2 * P + t * SHIFTS, SETS0 * SHIFTS
                return (t - SETS0) * SHIFTS, SETS1 * SHIFTS

            def layer(t):
                return 0 if isinstance(t, int) and t < SETS0 else 1

            def load_unit(t, q, s):
                if not (isinstance(q, int) and isinstance(t, int) and t == q == 0):
                    sp.wait_ge(quad_used, t * UNITS + (q * 2 + (s - 1)))
                first, apart = first_row(t)
                for i in range(QUADS):
                    src = l3["basis"][layer(t)][:, bass.ds(first + (q * (2 * PAIR) + (s * PAIR + i * apart)), PAIR), :]
                    sp.dma_start(quad[i * BASES:(i + 1) * BASES, s, :, :], src).then_inc(quad_loaded[s], 16)

            def load_pair(t, q):
                for s in range(2):
                    load_unit(t, q, s)

            def store_set(t):
                sp.wait_ge(set_taken, t + 1)
                for r in range(2):
                    for i in range(QUADS):
                        part, (first, apart) = (r * QUADS + i) * SHIFTS, first_row(t)
                        sp.dma_start(mix_d[layer(t), r, bass.ds(first + i * apart, SHIFTS), :], mixed[part:part + SHIFTS, :]
                                     ).then_inc(set_stored, 16)

            def bases(c, g):
                l, k = PIECES[c]
                for s in range(BSLOTS):
                    sp.wait_ge(basis_used, g * BSLOTS + (c * BASES + (s + 1)))
                    src = l3["basis"][l][bass.ds(g * BSLOTS + s, 1), k * P:(k + 1) * P, :]
                    sp.dma_start((bas, bas, bas1)[c][:, s, :], src.rearrange("a k n -> (a k) n")).then_inc(basis_loaded[s], 16)

            def store_mix(c):
                l, k = PIECES[c]
                sp.wait_ge(basis_used, c * BASES + (BASES + BSLOTS))
                sp.dma_start(mix_d[l, :, k * P:(k + 1) * P, :].rearrange("r p n -> p r n"), (macc, macc, macc1)[c][:]
                             ).then_inc(mix_stored, 16)

            GROUPS = BASES // BSLOTS
            groups = [(c, g) for c in range(2) for g in range(GROUPS)]

            def next_groups(count):
                for c, g in groups[:count]:
                    if c and g == 0:
                        store_mix(c - 1)
                    bases(c, g)
                del groups[:count]

            pairs = [(t, q) for t in range(1, EARLY_SETS) for q in range(UNITS // 2)]

            def next_pair():
                load_pair(*pairs.pop(0))

            load_pair(0, 0)
            next_groups(1)
            load_pair(0, 1)
            load_pair(0, 2)
            next_groups(1)
            load_pair(0, 3)
            next_pair()
            next_groups(1)
            store_set(0)
            next_pair()
            next_pair()
            next_groups(1)
            next_pair()
            next_groups(sum(GROUPS_MID))
            load_cond(0, 1, 1)
            sp.wait_ge(pass_act, 2 * NT)
            sp.wait_ge(pass_dve, NT)
            for r in range(2):
                sp.dma_start(ct_d[r], CT[r][:]).then_inc(ct_stored, 16)
            store_set(1)
            next_pair()
            for k, count in enumerate(GROUPS_0):
                if k == 3:
                    store_set(2)
                next_pair()
                next_groups(count)
            def load_biases(i):
                for j, name in enumerate(("bv", "bq", "bk", "bo", "m_b1", "m_b2")):
                    sp.dma_start(braw[2 * j:2 * j + 2, :], l1[name][bass.ds(i, 1)].broadcast_to([2, D])
                                 ).then_inc(braw_loaded, 16)

            def block_loads(i, nxt, last):
                t = i + EARLY_SETS
                load_cond(nxt, 0, i * 2 + 2)
                load_pair(t, 1)
                if not last:
                    sp.wait_ge(brow_ready, i + 1)
                    load_biases(nxt)
                load_pair(t, 2)
                load_cond(nxt, 1, i * 2 + 3)
                load_pair(t, 3)
                if last:
                    sp.wait_ge(tile_taken, n1.base + i * PER + n1.at[("PT", HEADS - 1, NT - 1)] + 1)
                    sp.dma_start(x[:], rows(x_s)).then_inc(x_loaded, 16)
                if not last:
                    load_pair(t + 1, 0)
                store_set(t)

            load_biases(0)
            sp.wait_ge(tile_taken, n0.end)
            sp.dma_start(rows(x_s), x[:]).then_inc(x_stored, 16)
            next_pair()
            next_pair()
            store_set(3)
            while pairs:
                next_groups(1)
                next_pair()
            next_groups(len(groups))
            store_mix(1)
            load_pair(EARLY_SETS, 0)
            store_set(EARLY_SETS - 1)
            with sp.Fori(0, BLOCKS - 1) as i:
                block_loads(i, i + 1, False)
            block_loads(BLOCKS - 1, BLOCKS - 1, True)
            sp.wait_ge(tile_taken, n2.base)
            for q in range(UNITS // 2):
                load_pair(SETS - 1, q)
            for r in range(2):
                sp.dma_start(Cr[r][:], ct_d[r]).then_inc(ct_loaded, 16)
            store_set(SETS - 1)
            sp.wait_ge(set_stored, 16 * 2 * QUADS * SETS)
            with sp.Fori(0, GROUPS) as k:
                bases(2, k)
            store_mix(2)
            for t in range(NT):
                sp.wait_ge(tile_taken, n3.base + n3.at[("R", 1, t)] + 1)
                sp.dma_start(out_d[t * P:(t + 1) * P, :], x[:, t, :]).then_inc(out_stored, 16)
            sp.wait_ge(out_stored, 16 * NT)

        @block.gpsimd
        def _(pool):
            g = nc.gpsimd
            for clear in (att_shift, bias_raw, fw2, cb, craw, braw, ones, half, zero_l, minus_low, minus_loww, ident, quarter):
                v = clear[:].bitcast(F32) if clear is zero_l else clear[:]
                last = g.memset(v, 1.0 if clear is ones else -0.5 if clear is half else 0.0)
            last.then_inc(const_step, 1)
            pool.wait_ge(const_step, 1)
            g.memset(cb[96:99, :], 1.0).then_inc(const_ready, 1)
            pool.wait_ge(const_ready, 1)
            g.affine_select(out=craw[:, 0, :], in_=craw[:, 0, :], compare_op=ALU.not_equal, fill=1.0, base=-98,
                            pattern=[[0, D]], channel_multiplier=1).then_inc(cond_clear, 1)
            pool.wait_ge(cond_clear, 1)
            g.memset(quarter[FREQS:2 * FREQS, :], 0.25).then_inc(const_step, 1)
            pool.wait_ge(const_step, 2)
            g.memset(minus_low[64:96, :], -1.0).then_inc(const_step, 1)
            pool.wait_ge(const_step, 3)
            g.memset(minus_loww[32:64, :], -1.0).then_inc(const_step, 1)
            pool.wait_ge(const_step, 4)
            g.affine_select(out=minus_loww[:], in_=minus_loww[:], compare_op=ALU.not_equal, fill=-1.0, base=-97,
                            pattern=[[0, 1]], channel_multiplier=1)
            g.affine_select(out=ident[:], in_=ident[:], compare_op=ALU.not_equal, fill=1.0, base=0,
                            pattern=[[-1, P]], channel_multiplier=1)
            g.iota(iota[:], [[1, NODES]], base=0, channel_multiplier=0, allow_small_or_imprecise_dtypes=True)
            g.iota(selv[:, 0, :, :], [[-2, 7], [0, P]], base=0, channel_multiplier=1, allow_small_or_imprecise_dtypes=True)
            g.iota(rowno[:], [[0, 1]], base=0, channel_multiplier=1)
            g.iota(turn_of[:, 0, :], [[-BODY, TURNS]], base=0, channel_multiplier=1, allow_small_or_imprecise_dtypes=True)
            for q in range(TURNS):
                g.memset(pow2[:, :, q], float(2 ** q))
            g.iota(freq[0:FREQS, :], [[0, 1]], base=1, channel_multiplier=1, allow_small_or_imprecise_dtypes=True
                   ).then_inc(const_step, 1)
            pool.wait_ge(const_step, 5)
            g.iota(freq[FREQS:2 * FREQS, :], [[0, 1]], base=1, channel_multiplier=1, allow_small_or_imprecise_dtypes=True
                   ).then_inc(const_ready, 1)

            def low_weight(w, s, r):
                pool.wait_ge(weight_hi, w + 1)
                g.tensor_tensor(wl[s][:], wraw[r][:], wh[s][:].bitcast(F32), ALU.subtract).then_inc(weight_lo, 1)

            def inverse_root(n, t):
                pool.wait_ge(ln_var, n + 1)
                g.tensor_tensor(rstd[:, t:t + 1], ve[:, t:t + 1], half[:, 0:1], ALU.pow).then_inc(ln_rstd, 1)

            for w in range(2):
                low_weight(w, slot(w), w % 2)
            for t in range(NT):
                inverse_root(t, t)
            pool.wait_ge(deg_step, 1)
            g.tensor_tensor(dg[:, 2, :], dg[:, 1, :], half[:], ALU.pow).then_inc(deg_pool, 1)
            for w in range(2, W1 + 2):
                low_weight(w, slot(w), w % 2)
            for j in range(NT):
                pool.wait_ge(tile_taken, cnt.base + cnt.at[("C", j)] + 1)
                g.tensor_scalar(both[:, j, :], both[:, j, :], 1.0, None, ALU.min).then_inc(adj_step, 1)
                pool.wait_ge(adj_step, 2 * j + 1)
                d = both[:, j, j * P:(j + 1) * P]
                g.tensor_tensor(d, d, ident[:], ALU.add).then_inc(adj_step, 1)
            for t in range(NT):
                inverse_root(NT + t, t)
            for t in range(NT):
                inverse_root(2 * NT + t, t)
            def block_lows(i, last):
                for j in (2, 3, 4):
                    low_weight(i * 6 + (W1 + j), j % 3, j % 2)
                for t in range(NT):
                    inverse_root(i * 8 + (12 + t), t)
                for j in (5, 6):
                    low_weight(i * 6 + (W1 + j), j % 3, j % 2)
                for t in range(NT):
                    inverse_root(i * 8 + (16 + t), t)
                if not last:
                    low_weight(i * 6 + (W1 + 7), 7 % 3, 7 % 2)

            with pool.Fori(0, BLOCKS - 1) as i:
                block_lows(i, False)
            block_lows(BLOCKS - 1, True)
            for t in range(NT):
                inverse_root(44 + t, t)
            for w in (W3, W3 + 1):
                low_weight(w, slot(w), w % 2)
            for t in range(NT):
                inverse_root(48 + t, t)
            for w in range(W3 + 2, W3 + 6):
                low_weight(w, slot(w), w % 2)

        @block.scalar
        def _(act):
            a = nc.scalar

            def high_weight(w, s, r, half_w, freed, following):
                if following is not None:
                    if not (isinstance(w, int) and w == 0):
                        act.wait_ge(weight_lo, w)
                    act.dma_start(wraw[1 - r][:], following).then_inc(weight_loaded[1 - r], 16)
                act.wait_ge(weight_loaded[r], half_w * 16 + 16)
                if freed is not None:
                    act.wait_ge(tile_ready, freed)
                a.activation(wh[s][:], wraw[r][:], ACT.Copy).then_inc(weight_hi, 1)

            def hw(w):
                late = (W3, W3 + 3)
                high_weight(w, slot(w), w % 2, w // 2, last_use(w - 3) + 1 if w >= 3 else None,
                            weight_source(w + 1) if w + 1 < W3 + 6 and w + 1 not in late else None)

            def load_mixed(w):
                l = (w - W3) // 3
                act.wait_ge(mix_stored, 16 * (2 + l))
                act.wait_ge(set_stored, 16 * 2 * QUADS * (SETS0, SETS)[l])
                act.wait_ge(weight_lo, w - 1)
                act.dma_start(wraw[w % 2][:], weight_source(w)).then_inc(weight_loaded[w % 2], 16)

            def take_set(t):
                if not (isinstance(t, int) and t == 0):
                    act.wait_ge(set_stored, t * (16 * 2 * QUADS))
                act.wait_ge(quad_used, t * UNITS + UNITS)
                a.activation(mixed[:], mix_ps[:], ACT.Copy).then_inc(set_taken, 1)

            def bank(T, name):
                return ring[:, T.bank(name), :]

            def high(T, base, name, out, func=ACT.Copy, **kw):
                act.wait_ge(tile_ready, base + (T.at[name] + 1))
                src = bank(T, name)
                if len(out.shape) == 3:
                    src = src.rearrange("p (a b) -> p a b", a=out.shape[1])
                a.activation(out, src, func, **kw).then_inc(hi_ready, 1)

            act.dma_start(wraw[0][:], weight_source(0)).then_inc(weight_loaded[0], 16)
            act.wait_ge(tile_ready, pre.base + pre.at["tab"] + 1)
            a.activation(whiT[:], ring[:, pre.bank("tab"), 3 * P:4 * P], ACT.Copy).then_inc(whi_ready, 1)
            hw(0)
            hw(1)
            act.wait_ge(flags_ready, 1)

            def turn(m, q, bits):
                with act.If(((bits >> q) & 1) > 0):
                    for u in range(BODY):
                        n = q * BODY + (m * ET + u)
                        act.wait_ge(dst_ready, n + 1)
                        s, e = u % SLOTS, bass.ds(q * BODY + u, 1)
                        for r in range(1, scaled_by_act(u)):
                            last = a.activation(ohd[:, s, r, :], ohd[:, s, 0, :].bitcast(F32), ACT.Copy,
                                                scale=scales[r][:, e])
                        last.then_inc(scaled_ready, 1)
                with act.Else():
                    act.drain().then_inc(scaled_ready, BODY)

            for m in range(NT):
                bits = act.value_load(turn_bits[0:1, m:m + 1], min_val=0, max_val=2 ** TURNS - 1)
                with act.Fori(0, TURNS // SPAN) as g:
                    with act.If(((bits >> (g * SPAN)) & (2 ** SPAN - 1)) > 0):
                        with act.Fori(0, SPAN) as q:
                            turn(m, g * SPAN + q, bits)
                    with act.Else():
                        act.drain().then_inc(scaled_ready, SPAN * BODY)
                act.wait_ge(pass_ready, m + 1)
                a.activation(CT[1][:, m, :], edge_ps[m][2], ACT.Copy).then_inc(pass_act, 1)
                a.activation(Araw[:, m, :], edge_ps[m][0], ACT.Copy).then_inc(pass_act, 1)
                if m == 0:
                    act.wait_ge(emb_step, 4)
                    a.activation(rnd[:], noise[:], ACT.Sin, scale=TURN).then_inc(emb_act, 1)
                if m == 1:
                    act.wait_ge(tile_taken, pre.base + pre.at["z1"] + 1)
                    a.activation(sil[0][:], sil[1][:], ACT.Exp, scale=-1.0).then_inc(emb_act, 1)
                if m % 2:
                    take_set(m // 2)

            for t in range(NT):
                act.wait_ge(ln_xn, t + 1)
                a.activation(hb_h[0][:, t, :], xn0[:, t, :], ACT.Relu).then_inc(h0_hi, 1)
            for m in range(NT):
                act.wait_ge(deg_step, 7 + m)
                a.activation(An_h[:, m, :], Araw[:, m, :], ACT.Copy).then_inc(deg_act, 1)
            for l in range(2):
                g_, u_ = hb_h[1 - l], hb_h[l]
                if l == 1:
                    take_set(2)
                for m in range(KT):
                    high(n0, n0.base, ("G", l, m), g_[:, m, :])
                hw((2, 4)[l])
                for m in range(KT):
                    high(n0, n0.base, ("U", l, m), u_[:, m, :])
                hw((3, 5)[l])
                for t in range(NT):
                    act.wait_ge(tile_ready, n0.base + n0.at[("H", l, t)] + 1)
                    if t >= 2 or l:
                        act.wait_ge(leaky_ready, 4 * l + t - 1)
                    a.activation(slope[:, t % 2, :], bank(n0, ("H", l, t)), ACT.Copy, scale=0.01).then_inc(slope_ready, 1)
                    if l == 0:
                        act.wait_ge(leaky_ready, t + 1)
                        a.activation(hb_h[1][:, t, :], hv[:, t % 2, :], ACT.Copy).then_inc(hi_ready, 1)

            for j in range(NT):
                act.wait_ge(cnt_step, CNT * j + 2)
                a.activation(ctmp[2][:], ctmp[1][:], ACT.Ln).then_inc(cnt_act, 1)
            take_set(3)
            for j in range(NT):
                act.wait_ge(adj_step, 2 * j + 2)
                a.activation(adj[:, j, :], both[:, j, :], ACT.Copy, accum_out=rowsum[:, 0, j:j + 1]).then_inc(row_sums, 1)
            take_set(EARLY_SETS - 1)

            act.wait_ge(mix_stored, 16 * 2)
            def block_highs(i, last):
                b = i * PER + n1.base

                def hi(name, out, func=ACT.Copy):
                    high(n1, b, name, out, func)

                def hwi(j, freed):
                    if last:
                        hw(W1 + 6 * i + j)
                    else:
                        high_weight(i * 6 + (W1 + j), j % 3, j % 2, i * 3 + (W1 // 2 + j // 2), freed,
                                    block_weight(i + (j + 1) // 6, (j + 1) % 6))

                def after(name):
                    return b + (n1.at[name] + 1)

                def exps(h):
                    pr = probs_of[h % 2]
                    for j in range(NT):
                        act.wait_ge(tile_taken, after(("s", h, j)))
                        a.activation(pr[:, j, :], pr[:, j, :], ACT.Exp, bias=nmin[:, h % 2, j:j + 1], scale=-1.0,
                                     accum_out=rsum[:, h % 2, j:j + 1]).then_inc(exp_ready, 1)

                def norm_rows(s, t):
                    hi(("T" + s, t), yT_h[:, :, t * P:(t + 1) * P])

                def value(t):
                    hi(("v", t), vm_h[:, t, :])

                def query(h):
                    hi(("q", h), qk_h[:, 0, :])

                def key(h):
                    hi(("k", h), qk_h[:, 1, :])

                def query_key(h):
                    query(h)
                    key(h)

                def probs_T(h):
                    for m in range(NT):
                        hi(("PT", h, m), PT_h[:, m, :])

                def mean_value(h):
                    hi(("PV", h), oT_h[:, h, :])

                def scale_probs(h):
                    act.wait_ge(rden_ready, i * (2 * HEADS) + (2 * h + 2))
                    pr = probs_of[h % 2]
                    for j in range(NT):
                        a.activation(pr[:, j, :], pr[:, j, :], ACT.Copy, scale=rden[:, h % 2, j:j + 1]).then_inc(probs_ready, 1)

                norm_rows("a", 0)
                norm_rows("a", 1)
                value(0)
                hwi(2, b)
                norm_rows("a", 2)
                value(1)
                norm_rows("a", 3)
                query_key(0)
                value(2)
                exps(0)
                scale_probs(0)
                query_key(1)
                for h in range(1, HEADS):
                    probs_T(h - 1)
                    if h == 1:
                        value(3)
                    exps(h)
                    mean_value(h - 1)
                    scale_probs(h)
                    if h + 1 < HEADS:
                        query(h + 1)
                        if h == 1:
                            hwi(3, after(("v", NT - 1)))
                        key(h + 1)
                hwi(4, after(("q", HEADS - 1)))
                probs_T(HEADS - 1)
                mean_value(HEADS - 1)
                hwi(5, after(("k", HEADS - 1)))
                for t in range(NT):
                    norm_rows("b", t)
                hwi(6, after(("o", NT - 1)))
                for m in range(KT):
                    hi(("M", m), vm_h[:, m, :], ACT.Relu)
                take_set(i + EARLY_SETS)
                if not last:
                    hwi(7, after(("M", KT - 1)))

            with act.Fori(0, BLOCKS - 1) as i:
                block_highs(i, False)
            block_highs(BLOCKS - 1, True)

            load_mixed(W3)
            for t in range(NT):
                high(n2, n2.base, ("T", t), y2T_h[:, :, t * P:(t + 1) * P])
            for t in range(NT):
                high(n2, n2.base, ("A", 0, t), cur_h[:, 0, t, :])
            for k in range(1, STEPS):
                hw(W3 + k - 1)
                for t in range(NT):
                    high(n2, n2.base, ("A", k, t), cur_h[:, k % 2, t, :], ACT.Identity, scale=rinv[:, t:t + 1])
            hw(W3 + 2)
            take_set(SETS - 1)

            act.wait_ge(y_ready, 2 * NT)
            act.wait_ge(ct_loaded, 32)
            for r in range(2):
                a.activation(C_h[:, r, :, :], Cr[r][:], ACT.Copy).then_inc(c_hi, 1)
            for t in range(NT):
                high(n3, n3.base, ("T", t), hT_h[0][:, :, t * P:(t + 1) * P])
            for l in range(2):
                act.wait_ge(tile_ready, n3.base + n3.at[("g", l)] + 1)
                a.activation(ge[:], ring[:, n3.bank(("g", l)), 0:2 * NT], ACT.Exp, scale=-1.0).then_inc(gate_exp, 1)
                act.wait_ge(gate_step, l + 1)
                for r in range(2):
                    for t in range(NT):
                        high(n3, n3.base, ("Z", l, r, t), Z_h[:, r, t, :], ACT.Identity,
                             scale=gate[:, 2 * t + r:2 * t + r + 1])
                if l == 0:
                    load_mixed(W3 + 3)
                    hw(W3 + 3)
                    for m in range(KT):
                        high(n3, n3.base, ("R", 0, m), hT_h[1][:, m, :], ACT.Relu)
                        if m == 0:
                            hw(W3 + 4)
                    hw(W3 + 5)

        @block.vector
        def _(dve):
            v = nc.vector

            def f(ap):
                return ap.bitcast(F32)

            def bank(T, name):
                return ring[:, T.bank(name), :]

            def ready(T, base, name):
                dve.wait_ge(tile_ready, base + (T.at[name] + 1))

            def taken(T, base, name):
                dve.wait_ge(tile_taken, base + (T.at[name] + 1))

            def low(T, base, name, hi_count, out, hi, func=None, scalar=None):
                dve.wait_ge(hi_ready, hi_count + 1)
                src = bank(T, name)
                if len(out.shape) == 3:
                    src = src.rearrange("p (a b) -> p a b", a=out.shape[1])
                if func is None:
                    v.tensor_tensor(out, src, f(hi), ALU.subtract).then_inc(tile_taken, 1)
                else:
                    v.scalar_tensor_tensor(out, src, scalar, f(hi), func, ALU.subtract).then_inc(tile_taken, 1)

            holds = [0]

            def hold():
                v.memset(pace[:, holds[0]:holds[0] + 1], 0.0)
                holds[0] += 1

            def norm_stats(src, t, n):
                v.bn_stats(stats[:, t, :], src).then_inc(ln_stats, 1)
                dve.wait_ge(ln_stats, n + 1)
                hold()
                v.bn_aggr(mv[:, t, :], stats[:, t, :]).then_inc(ln_mv, 1)
                dve.wait_ge(ln_mv, n + 1)
                v.tensor_scalar(ve[:, t:t + 1], mv[:, t, 1:2], EPS, None, ALU.add).then_inc(ln_var, 1)

            def normalise(out, src, t, n):
                dve.wait_ge(ln_rstd, n + 1)
                v.tensor_scalar(out, src, mv[:, t, 0:1], rstd[:, t:t + 1], ALU.subtract, ALU.mult).then_inc(ln_xn, 1)

            dve.wait_ge(edges_loaded, 64)
            v.tensor_copy(efl[:], eint[:]).then_inc(table_ready, 1)
            v.tensor_scalar(eblk[:], eint[:, 1, :], P.bit_length() - 1, None, ALU.arith_shift_right).then_inc(table_ready, 1)
            dve.wait_ge(const_ready, 2)
            v.tensor_scalar(turn_of[:, 1, :], turn_of[:, 0, :], 0.0, None, ALU.is_ge).then_inc(table_ready, 1)
            dve.wait_ge(table_ready, 3)
            for m in range(NT):
                last = v.tensor_scalar(hit[:, m, :], eblk[:], float(m), None, ALU.is_equal)
            last.then_inc(table_ready, 1)
            v.scalar_tensor_tensor(turn_of[:, 2, :], turn_of[:, 0, :], BODY - 1.0, turn_of[:, 1, :], ALU.is_le, ALU.mult
                                   ).then_inc(table_ready, 1)
            dve.wait_ge(table_ready, 5)
            v.reduce_max(tile_hit[:], hit[:], AX.X).then_inc(table_ready, 1)
            dve.wait_ge(table_ready, 6)
            v.tensor_tensor(turn_hit[:], tile_hit[:].unsqueeze(2).broadcast_to([P, NT, TURNS]),
                            turn_of[:, 2, :].unsqueeze(1).broadcast_to([P, NT, TURNS]), ALU.mult).then_inc(table_ready, 1)
            dve.wait_ge(whi_ready, 1)
            tab = bank(pre, "tab")
            v.tensor_copy(srcT[:], tab[:, 0:P])
            v.tensor_copy(dstT[:], tab[:, P:2 * P])
            v.tensor_scalar(isr1[:], tab[:, 2 * P:3 * P], 0.0, None, ALU.not_equal).then_inc(table_ready, 1)
            v.tensor_tensor(wloT[:], tab[:, 3 * P:4 * P], f(whiT[:]), ALU.subtract).then_inc(tile_taken, 1)
            ready(pre, pre.base, "flag")
            v.scalar_tensor_tensor(turn_hit[:].rearrange("p m q -> p (m q)"), bank(pre, "flag")[:, 0:NT * TURNS], 1.0,
                                   pow2[:].rearrange("p m q -> p (m q)"), ALU.min, ALU.mult).then_inc(tile_taken, 1)
            taken(pre, pre.base, "flag")
            v.reduce_sum(bits_f[:], turn_hit[:], AX.X).then_inc(table_ready, 1)
            dve.wait_ge(table_ready, 9)
            v.tensor_copy(turn_bits[:], bits_f[:]).then_inc(flags_ready, 1)

            def selectors_and_angles():
                v.tensor_scalar(selv[:, 1, :, :], selv[:, 0, :, :], 0.0, None, ALU.is_ge).then_inc(sel_step, 1)
                dve.wait_ge(sel_step, 1)
                v.scalar_tensor_tensor(sel[:].rearrange("p a b -> p (a b)"), selv[:, 0, :, :].rearrange("p a b -> p (a b)"), 1.0,
                                       selv[:, 1, :, :].rearrange("p a b -> p (a b)"), ALU.is_le, ALU.mult).then_inc(sel_step, 1)
                v.tensor_scalar(rowno[:], rowno[:], 1, None, ALU.bitwise_and).then_inc(sel_step, 1)
                dve.wait_ge(sel_step, 3)
                v.tensor_scalar(minus_odd[:], rowno[:], -1.0, None, ALU.mult).then_inc(sel_step, 1)
                dve.wait_ge(small_loaded, 16 * SMALL)
                v.tensor_copy(bias_rows[:], bias_raw[:]).then_inc(sel_step, 1)
                v.tensor_copy(gwh[:], gw[:]).then_inc(sel_step, 1)
                dve.wait_ge(sel_step, 6)
                v.scalar_tensor_tensor(bias_rows[:], f(bias_rows[:]), minus_odd[:], bias_raw[:], ALU.mult, ALU.add).then_inc(sel_step, 1)
                v.tensor_tensor(gwl[:], gw[:], f(gwh[:]), ALU.subtract).then_inc(sel_step, 1)
                v.tensor_scalar(noise[:], noise[:], freq[:], 1.0 / PERIOD, ALU.mult, ALU.mult).then_inc(emb_step, 1)
                dve.wait_ge(emb_step, 1)
                v.tensor_scalar(noise[:], noise[:], quarter[:], None, ALU.add).then_inc(emb_step, 1)
                dve.wait_ge(emb_step, 2)
                v.tensor_scalar(rnd[:], noise[:], MAGIC, MAGIC, ALU.add, ALU.subtract).then_inc(emb_step, 1)
                dve.wait_ge(emb_step, 3)
                v.tensor_tensor(noise[:], noise[:], rnd[:], ALU.subtract).then_inc(emb_step, 1)

            def silu_argument():
                ready(pre, pre.base, "z1")
                v.tensor_scalar(sil[1][:], bank(pre, "z1")[0:COND, :], fb1[:], None, ALU.add).then_inc(tile_taken, 1)

            def silu():
                dve.wait_ge(emb_act, 2)
                v.tensor_scalar(sil[0][:], sil[0][:], 1.0, None, ALU.add).then_inc(emb_step, 1)
                dve.wait_ge(emb_step, 5)
                v.reciprocal(sil[0][:], sil[0][:]).then_inc(emb_step, 1)
                dve.wait_ge(emb_step, 6)
                v.tensor_tensor(sil[0][:], sil[0][:], sil[1][:], ALU.mult).then_inc(emb_step, 1)

            def stack_conditioning():
                xn_c = selv[:, 0, 0:NT, :].rearrange("p a b -> p (a b)")
                ready(pre, pre.base, "z2")
                v.tensor_scalar(xn_c, bank(pre, "z2"), cb[:], None, ALU.add).then_inc(tile_taken, 1)
                taken(pre, pre.base, "z2")
                v.tensor_copy(stk[:], xn_c).then_inc(emb_step, 1)
                dve.wait_ge(emb_step, 8)
                v.scalar_tensor_tensor(stk[:], f(stk[:]), minus_low[:], xn_c, ALU.mult, ALU.add).then_inc(emb_step, 1)

            def split_cond(n, count):
                dve.wait_ge(cond_loaded, count * 128 + 128)
                v.tensor_copy(cond[:, 2 * n:2 * n + 2, :], craw[:]).then_inc(cond_hi, 1)
                dve.wait_ge(cond_hi, count + 1)
                v.scalar_tensor_tensor(cond[:, 2 * n:2 * n + 2, :], f(cond[:, 2 * n:2 * n + 2, :]), minus_loww[:], craw[:],
                                       ALU.mult, ALU.add).then_inc(cond_ready, 1)

            v.engine_nop().then_inc(basis_used, BSLOTS)

            def mix_at(c, g, s):
                n = c * BASES + g * BSLOTS + s
                dve.wait_ge(basis_loaded[s], c * (16 * BASES // BSLOTS) + (g * 16 + 16))
                dve.wait_ge(basis_used, n + BSLOTS)
                pieces, sums = ((bas, macc), (bas, macc), (bas1, macc1))[c]
                for r in range(2):
                    k = r * BASES + g * BSLOTS + s
                    coef = att[:, PIECES[c][0], k:k + 1]
                    if g == s == 0:
                        if c and r == 0:
                            dve.wait_ge(mix_stored, 16 * c)
                        last = v.tensor_scalar(sums[:, r, :], pieces[:, s, :], coef, None, ALU.mult)
                    else:
                        last = v.scalar_tensor_tensor(sums[:, r, :], pieces[:, s, :], coef, sums[:, r, :], ALU.mult, ALU.add)
                last.then_inc(basis_used, 1)

            matrices = [(c, g, s) for c in range(len(PIECES)) for g in range(BASES // BSLOTS) for s in range(BSLOTS)]

            def mix(count):
                for c, g, s in matrices[:count]:
                    mix_at(c, g, s)
                del matrices[:count]

            def turn(m, q, bits):
                with dve.If(((bits >> q) & 1) > 0):
                    for u in range(BODY):
                        n = q * BODY + (m * ET + u)
                        s, e = u % SLOTS, bass.ds(q * BODY + u, 1)
                        dve.wait_ge(onehot_used, n + 1)
                        cols = iota[:, m * P:(m + 1) * P]
                        v.tensor_scalar(ohd[:, s, 0, :], cols, dstT[:, e], None, ALU.is_equal).then_inc(dst_ready, 1)
                        for r in range(scaled_by_act(u), 4):
                            v.tensor_scalar(ohd[:, s, r, :], cols, dstT[:, e], scales[r][:, e], ALU.is_equal, ALU.mult)
                        v.tensor_scalar(ohs[:, s, :], iota[:], srcT[:, e], None, ALU.is_equal).then_inc(onehot_ready, 1)
                with dve.Else():
                    dve.drain().then_inc(dst_ready, BODY)
                    dve.drain().then_inc(onehot_ready, BODY)

            dve.wait_ge(flags_ready, 1)
            dve.wait_ge(tile_taken, pre.base + 1)

            def some_turns(m, g, bits):
                with dve.If(((bits >> (g * SPAN)) & (2 ** SPAN - 1)) > 0):
                    with dve.Fori(0, SPAN) as q:
                        turn(m, g * SPAN + q, bits)
                with dve.Else():
                    dve.drain().then_inc(dst_ready, SPAN * BODY)
                    dve.drain().then_inc(onehot_ready, SPAN * BODY)

            between = [(selectors_and_angles,), (silu_argument,), (silu,), (stack_conditioning, lambda: split_cond(0, 0))]
            for m in range(NT):
                bits = dve.value_load(turn_bits[0:1, m:m + 1], min_val=0, max_val=2 ** TURNS - 1)
                with dve.Fori(0, TURNS // SPAN) as g:
                    some_turns(m, g, bits)
                for step in between[m]:
                    step()
                if m == 0:
                    dve.wait_ge(small_loaded, 16 * SMALL)
                mix(BSLOTS)
                dve.wait_ge(pass_ready, m + 1)
                v.tensor_copy(Csum[:, m, :], edge_ps[m][1])
                dve.wait_ge(pass_act, 2 * m + 1)
                v.tensor_tensor(CT[0][:, m, :], edge_ps[m][1], CT[1][:, m, :], ALU.subtract).then_inc(pass_dve, 1)

            dve.wait_ge(x_loaded, 16)
            for t in range(NT):
                norm_stats(x[:, t, :], t, t)
            for t in range(NT):
                normalise(xn0[:, t, :], x[:, t, :], t, t)
            mix(MIX_MID[0])
            ready(mid, mid.base, "deg")
            v.tensor_copy(dg[:, 0, :], bank(mid, "deg")[:, 0:2 * NT:2]).then_inc(tile_taken, 1)
            taken(mid, mid.base, "deg")
            v.tensor_scalar(dg[:, 1, :], dg[:, 0, :], 1e-37, None, ALU.max).then_inc(deg_step, 1)
            for t in range(NT):
                dve.wait_ge(h0_hi, t + 1)
                v.scalar_tensor_tensor(hb_l[0][:, t, :], xn0[:, t, :], 0.0, f(hb_h[0][:, t, :]), ALU.max, ALU.subtract).then_inc(h0_ready, 1)
            split_cond(1, 1)
            mix(MIX_MID[1])
            dve.wait_ge(deg_pool, 1)
            v.scalar_tensor_tensor(dg[:, 3, :], dg[:, 0, :], 0.0, dg[:, 2, :], ALU.is_gt, ALU.mult).then_inc(deg_step, 1)
            dve.wait_ge(deg_step, 2)
            for j in range(NT):
                v.tensor_scalar(diag[:, j, :], ident[:], dg[:, 3, j:j + 1], None, ALU.mult).then_inc(deg_step, 1)
            mix(MIX_MID[2])
            ready(mid, mid.base, "dinv")
            v.tensor_copy(D2[:], bank(mid, "dinv")).then_inc(tile_taken, 1)
            taken(mid, mid.base, "dinv")
            dve.wait_ge(pass_act, 2 * NT)
            for m in range(NT):
                v.scalar_tensor_tensor(Araw[:, m, :], Araw[:, m, :], dg[:, 3, m:m + 1], D2[:], ALU.mult, ALU.mult).then_inc(deg_step, 1)
            for m in range(NT):
                dve.wait_ge(deg_act, m + 1)
                v.tensor_tensor(An_l[:, m, :], Araw[:, m, :], f(An_h[:, m, :]), ALU.subtract).then_inc(deg_step, 1)

            for l in range(2):
                gb, ub = 1 - l, l
                for m in range(KT):
                    low(n0, n0.base, ("G", l, m), hi0[("G", l, m)], hb_l[gb][:, m, :], hb_h[gb][:, m, :])
                    mix(MIX_G[m])
                for m in range(KT):
                    low(n0, n0.base, ("U", l, m), hi0[("U", l, m)], hb_l[ub][:, m, :], hb_h[ub][:, m, :])
                    mix(MIX_G[m])
                for t in range(NT):
                    dve.wait_ge(slope_ready, 4 * l + t + 1)
                    v.tensor_tensor(hv[:, t % 2, :], bank(n0, ("H", l, t)), slope[:, t % 2, :], ALU.max).then_inc(leaky_ready, 1)
                    dve.wait_ge(leaky_ready, 4 * l + t + 1)
                    if l == 0:
                        dve.wait_ge(hi_ready, hi0[("H", 0, t)] + 1)
                        v.tensor_tensor(hb_l[1][:, t, :], hv[:, t % 2, :], f(hb_h[1][:, t, :]), ALU.subtract).then_inc(tile_taken, 1)
                    else:
                        v.tensor_tensor(x[:, t, :], x[:, t, :], hv[:, t % 2, :], ALU.add).then_inc(tile_taken, 1)
                    mix(MIX_H[t])

            step = [0]

            def counted(ins):
                step[0] += 1
                ins.then_inc(cnt_step, 1)
                return step[0]

            for j in range(NT):
                ready(cnt, cnt.base, ("C", j))
                if j:
                    dve.wait_ge(cnt_step, CNT * j)
                C = bank(cnt, ("C", j))
                counted(v.tensor_scalar(ctmp[0][:], C, 0.0, NOEDGE, ALU.is_equal, ALU.mult))
                counted(v.tensor_scalar(ctmp[1][:], C, 1.0, None, ALU.max))
                top_c = counted(v.reduce_max(rowsum[:, 1, j:j + 1], C, AX.X))
                v.tensor_tensor(both[:, j, :], C, Csum[:, j, :], ALU.add).then_inc(tile_taken, 1)
                dve.wait_ge(cnt_step, top_c)
                counted(v.tensor_scalar(hasedge[:, j:j + 1], rowsum[:, 1, j:j + 1], 1.0, None, ALU.min))
                dve.wait_ge(cnt_act, j + 1)
                counted(v.scalar_tensor_tensor(mask[:, j, :], ctmp[2][:], 1.0 / SCALE, ctmp[0][:], ALU.mult, ALU.add))
                assert step[0] == CNT * (j + 1)
            mix(len(matrices) - BASES)
            for t in range(NT):
                norm_stats(x[:, t, :], t, NT + t)
            for t in range(NT):
                normalise(xl[:, t, :], x[:, t, :], t, NT + t)
                dve.wait_ge(ln_xn, NT + t + 1)
                v.tensor_scalar(xl[:, t, :], xl[:, t, :], 0.0, None, ALU.max).then_inc(xl_ready, 1)
            dve.wait_ge(xl_ready, NT)
            dve.wait_ge(ct_stored, 32)

            for t in range(NT):
                norm_stats(xl[:, t, :], t, 2 * NT + t)
            dve.wait_ge(row_sums, NT)
            v.reciprocal(rinv[:], rowsum[:, 0, :]).then_inc(cnt_step, 1)
            dve.wait_ge(cnt_step, CNT * NT + 1)
            for k in range(STEPS):
                v.tensor_scalar(rdw[:, k, :], rinv[:], dw[:, k + 1:k + 2], None, ALU.mult).then_inc(l2_step, 1)

            with dve.Fori(0, BLOCKS) as i:
                b = i * PER + n1.base
                hb = i * PERH + HI1

                def lo(name, out, hi, **kw):
                    low(n1, b, name, hb + hi1[name], out, hi, **kw)

                def stats_of(n, name, t):
                    taken(n1, b, (name, t))
                    norm_stats(xl[:, t, :], t, n)

                def conditioned(s, t):
                    n = i * 8 + (8 + 4 * "ab".index(s) + t)
                    dve.wait_ge(ln_mv, n + 1)
                    ready(n1, b, ("S" + s, t))
                    v.scalar_tensor_tensor(yp[:, t, :], xl[:, t, :], mv[:, t, 0:1], bank(n1, ("S" + s, t)), ALU.subtract,
                                           ALU.mult).then_inc(tile_taken, 1)
                    dve.wait_ge(ln_rstd, n + 1)
                    taken(n1, b, ("S" + s, t))
                    ready(n1, b, ("B" + s, t))
                    v.scalar_tensor_tensor(yp[:, t, :], yp[:, t, :], rstd[:, t:t + 1], bank(n1, ("B" + s, t)), ALU.mult,
                                           ALU.add).then_inc(tile_taken, 1)

                def transposed(s, t):
                    c = slice(t * P, (t + 1) * P)
                    lo(("T" + s, t), yT_l[:, :, c], yT_h[:, :, c])

                def value(t):
                    lo(("v", t), vm_l[:, t, :], vm_h[:, t, :])

                def residual(name, t):
                    ready(n1, b, (name, t))
                    v.tensor_tensor(xl[:, t, :], xl[:, t, :], bank(n1, (name, t)), ALU.add).then_inc(tile_taken, 1)

                def masked(h):
                    if h == 1:
                        dve.wait_ge(x_stored, 16)
                    for j in range(NT):
                        ready(n1, b, ("s", h, j))
                        hold()
                        v.tensor_tensor_reduce(out=probs_of[h % 2][:, j, :], in0=bank(n1, ("s", h, j)), in1=mask[:, j, :],
                                               scale=-SCALE, scalar=3e38, op0=ALU.add, op1=ALU.min,
                                               accum_out=nmin[:, h % 2, j:j + 1]).then_inc(tile_taken, 1)

                def inverse_sums(h):
                    n = i * (2 * HEADS) + (2 * h + 1)
                    dve.wait_ge(exp_ready, i * 16 + (4 * h + 4))
                    v.reciprocal(rden[:, h % 2, :], rsum[:, h % 2, :]).then_inc(rden_ready, 1)
                    dve.wait_ge(rden_ready, n)
                    v.tensor_tensor(rden[:, h % 2, :], rden[:, h % 2, :], hasedge[:], ALU.mult).then_inc(rden_ready, 1)

                def query(h):
                    lo(("q", h), qk_l[:, 0, :], qk_h[:, 0, :])

                def key(h):
                    lo(("k", h), qk_l[:, 1, :], qk_h[:, 1, :])

                def probs_T(h):
                    for m in range(NT):
                        lo(("PT", h, m), PT_l[:, m, :], PT_h[:, m, :])

                def mean_value(h):
                    lo(("PV", h), oT_l[:, h, :], oT_h[:, h, :])

                conditioned("a", 0)
                conditioned("a", 1)
                transposed("a", 0)
                dve.wait_ge(braw_loaded, i * 96 + 96)
                v.tensor_copy(brow[:], braw[:]).then_inc(brow_hi, 1)
                dve.wait_ge(brow_hi, i + 1)
                v.scalar_tensor_tensor(brow[:], f(brow[:]), minus_odd[:], braw[:], ALU.mult, ALU.add).then_inc(brow_ready, 1)
                conditioned("a", 2)
                transposed("a", 1)
                value(0)
                conditioned("a", 3)
                transposed("a", 2)
                value(1)
                transposed("a", 3)
                query(0)
                key(0)
                value(2)
                split_cond(0, i * 2 + 2)
                masked(0)
                inverse_sums(0)
                query(1)
                key(1)
                for h in range(1, HEADS):
                    probs_T(h - 1)
                    if h == 1:
                        value(3)
                    masked(h)
                    mean_value(h - 1)
                    inverse_sums(h)
                    if h + 1 < HEADS:
                        query(h + 1)
                        key(h + 1)
                probs_T(HEADS - 1)
                mean_value(HEADS - 1)
                nb = i * 8 + 12
                for t in range(2):
                    residual("o", t)
                    stats_of(nb + t, "o", t)
                conditioned("b", 0)
                conditioned("b", 1)
                for t in range(2, NT):
                    residual("o", t)
                    stats_of(nb + t, "o", t)
                    if t == 2:
                        transposed("b", 0)
                        transposed("b", 1)
                    conditioned("b", t)
                for t in range(2, NT):
                    transposed("b", t)
                for m in range(KT):
                    lo(("M", m), vm_l[:, m, :], vm_h[:, m, :], func=ALU.max, scalar=0.0)
                split_cond(1, i * 2 + 3)
                for t in range(NT):
                    residual("X", t)
                    stats_of(i * 8 + (16 + t), "X", t)

            dve.wait_ge(tile_taken, n2.base)
            dve.wait_ge(x_loaded, 32)
            for t in range(NT):
                v.tensor_tensor(x[:, t, :], x[:, t, :], xl[:, t, :], ALU.add).then_inc(l2_step, 1)
            dve.wait_ge(ln_rstd, 44)
            for t in range(NT):
                dve.wait_ge(l2_step, STEPS + t + 1)
                norm_stats(x[:, t, :], t, 44 + t)
            for t in range(NT):
                normalise(y2[:, t, :], x[:, t, :], t, 44 + t)
                dve.wait_ge(ln_xn, 2 * NT + t + 1)
                v.tensor_scalar(y2[:, t, :], y2[:, t, :], 0.0, None, ALU.max).then_inc(y_ready, 1)
            v.tensor_copy(adj_r[:], adj[:]).then_inc(l2_step, 1)
            for t in range(NT):
                c = slice(t * P, (t + 1) * P)
                low(n2, n2.base, ("T", t), hi2[("T", t)], y2T_l[:, :, c], y2T_h[:, :, c])
            base = STEPS + NT + 1
            for t in range(NT):
                dve.wait_ge(hi_ready, hi2[("A", 0, t)] + 1)
                v.tensor_scalar(acc2[:, t, :], bank(n2, ("A", 0, t)), dw[:, 0:1], None, ALU.mult).then_inc(l2_step, 1)
                low(n2, n2.base, ("A", 0, t), hi2[("A", 0, t)], cur_l[:, 0, t, :], cur_h[:, 0, t, :])
            for k in range(1, STEPS + 1):
                for t in range(NT):
                    name = ("A", k, t)
                    if k < STEPS:
                        dve.wait_ge(hi_ready, hi2[name] + 1)
                    else:
                        ready(n2, n2.base, name)
                    dve.wait_ge(l2_step, base + 4 * (k - 1) + t + 1)
                    ins = v.scalar_tensor_tensor(acc2[:, t, :], bank(n2, name), rdw[:, k - 1, t:t + 1], acc2[:, t, :], ALU.mult, ALU.add)
                    if k < STEPS:
                        ins.then_inc(l2_step, 1)
                        low(n2, n2.base, name, hi2[name], cur_l[:, k % 2, t, :], cur_h[:, k % 2, t, :], func=ALU.mult,
                            scalar=rinv[:, t:t + 1])
                    else:
                        ins.then_inc(tile_taken, 1)
            for t in range(NT):
                taken(n2, n2.base, ("A", STEPS, t))
                v.scalar_tensor_tensor(x[:, t, :], acc2[:, t, :], 0.0, x[:, t, :], ALU.max, ALU.add).then_inc(l2_step, 1)

            base += 4 * STEPS
            for t in range(NT):
                dve.wait_ge(l2_step, base + t + 1)
                norm_stats(x[:, t, :], t, 48 + t)
            for t in range(NT):
                normalise(y3[:, t, :], x[:, t, :], t, 48 + t)
                dve.wait_ge(ln_xn, 3 * NT + t + 1)
                v.tensor_scalar(y3[:, t, :], y3[:, t, :], 0.0, None, ALU.max).then_inc(y_ready, 1)
            for t in range(NT):
                c = slice(t * P, (t + 1) * P)
                low(n3, n3.base, ("T", t), hi3[("T", t)], hT_l[0][:, :, c], hT_h[0][:, :, c])
            mix(MIX_3[0])
            for r in range(2):
                dve.wait_ge(c_hi, r + 1)
                v.tensor_tensor(C_l[:, r, :, :], Cr[r][:], f(C_h[:, r, :, :]), ALU.subtract).then_inc(c_ready, 1)
            for l in range(2):
                dve.wait_ge(gate_exp, l + 1)
                v.tensor_scalar(gate[:], ge[:], 1.0, None, ALU.add).then_inc(tile_taken, 1)
                taken(n3, n3.base, ("g", l))
                v.reciprocal(gate[:], gate[:]).then_inc(gate_step, 1)
                dve.wait_ge(gate_step, l + 1)
                for r in range(2):
                    for t in range(NT):
                        name = ("Z", l, r, t)
                        low(n3, n3.base, name, hi3[name], Z_l[:, r, t, :], Z_h[:, r, t, :], func=ALU.mult,
                            scalar=gate[:, 2 * t + r:2 * t + r + 1])
                        mix(MIX_3[1 + r])
                mix(len(matrices))
                for t in range(NT):
                    name = ("R", l, t)
                    if l == 0:
                        low(n3, n3.base, name, hi3[name], hT_l[1][:, t, :], hT_h[1][:, t, :], func=ALU.max, scalar=0.0)
                    else:
                        ready(n3, n3.base, name)
                        v.tensor_tensor(x[:, t, :], x[:, t, :], bank(n3, name), ALU.add).then_inc(tile_taken, 1)

        @block.tensor
        def _(pe):
            te = nc.tensor

            def begin(T, base, name):
                j = T.at[name]
                if j >= RING or not isinstance(base, int):
                    pe.wait_ge(tile_taken, base + (j - RING + 1))
                elif j == 0:
                    pe.wait_ge(tile_taken, base)
                return ring[:, T.bank(name), :]

            def taken(T, base, name):
                pe.wait_ge(tile_taken, base + (T.at[name] + 1))

            def multiply(out, pairs):
                for n, (l, r) in enumerate(pairs):
                    last = te.matmul(out, l, r, start=n == 0, stop=n == len(pairs) - 1)
                return last

            def three(lh, ll, rh, rl):
                return [(lh, rh), (lh, rl), (ll, rh)]

            def cols(ap, k, m):
                return ap[:, k, m * P:(m + 1) * P]

            def bias_to_rows(j, rows_ap):
                return (sel[:, j, :], rows_ap[:])

            def bias_to_columns(j, rows_ap, m):
                return (rows_ap[:, m * P:(m + 1) * P], sel[:, j:j + 1, :].broadcast_to([P, NT, P]))

            def transposes(out, ins):
                for n, ap in enumerate(ins):
                    last = te.transpose(out[:, n * P:(n + 1) * P], ap, ident[:])
                return last

            def mix_product(t, j):
                u = j // PAIR
                if j == 0 and not (isinstance(t, int) and t == 0):
                    pe.wait_ge(set_taken, t)
                if j % PAIR == 0:
                    pe.wait_ge(quad_loaded[u % 2], t * (UNITS // 2 * 16 * QUADS) + (u // 2 + 1) * 16 * QUADS)
                layer = 0 if isinstance(t, int) and t < SETS0 else 1
                ins = te.matmul(mix_ps[:], att_shift[0:QUADS * BASES, layer, SHIFTS - 1 - j:SHIFTS - 1 - j + P],
                                quad[0:QUADS * BASES, u % 2, j % PAIR, :], start=j == 0, stop=j == SHIFTS - 1)
                if j % PAIR == PAIR - 1:
                    ins.then_inc(quad_used, 1)

            early = [(t, j) for t in range(EARLY_SETS) for j in range(SHIFTS)]
            late = [(t, j) for t in range(EARLY_SETS + BLOCKS, SETS) for j in range(SHIFTS)]

            def mix_products(which, count):
                for t, j in which[:count]:
                    mix_product(t, j)
                del which[:count]

            pe.wait_ge(const_ready, 2)
            pe.wait_ge(edges_loaded, 64)
            pe.wait_ge(table_ready, 1)
            out = ring[:, pre.bank("tab"), :]
            transposes(out, [efl[:, 0, :], efl[:, 1, :], efl[:, 2, :], ewt[:]]).then_inc(tile_ready, 1)
            pe.wait_ge(table_ready, 7)
            te.matmul(ring[:, pre.bank("flag"), 0:NT * TURNS], ones[:], turn_hit[:].rearrange("p m q -> p (m q)"),
                      start=True, stop=True).then_inc(tile_ready, 1)
            zeros = zero_l[:].unsqueeze(1).broadcast_to([P, NODES // P, P])
            pe.wait_ge(flags_ready, 1)

            def turn(m, q, bits):
                ps_w, ps_c, ps_c1 = edge_ps[m]
                with pe.If(((bits >> q) & 1) > 0):
                    for u in range(BODY):
                        n = q * BODY + (m * ET + u)
                        s = u % SLOTS
                        pe.wait_ge(onehot_ready, n + 1)
                        te.matmul(ps_c, ohd[:, s, 0, :], ohs[:, s, :], start=False, stop=False)
                        pe.wait_ge(scaled_ready, n + 1)
                        for r, ps in ((1, ps_c1), (2, ps_w), (3, ps_w)):
                            last = te.matmul(ps, ohd[:, s, r, :], ohs[:, s, :], start=False, stop=False)
                        last.then_inc(onehot_used, 1)
                with pe.Else():
                    pe.drain().then_inc(onehot_used, BODY)

            for m in range(NT):
                if m:
                    if m == 1:
                        pe.wait_ge(small_loaded, 16 * SMALL)
                    mix_products(early, 8)
                if m == 1:
                    pe.wait_ge(tile_taken, pre.base + pre.at["flag"] + 1)
                if m >= 2:
                    pe.wait_ge(pass_act, 2 * m - 2)
                    pe.wait_ge(pass_dve, m - 1)
                bits = pe.value_load(turn_bits[0:1, m:m + 1], min_val=0, max_val=2 ** TURNS - 1)
                for ps in edge_ps[m]:
                    last = te.matmul(ps, zero_l[:], zeros, start=True, stop=False)
                if m == 0:
                    last.then_inc(onehot_used, SLOTS)
                with pe.Fori(0, TURNS // SPAN) as g:
                    with pe.If(((bits >> (g * SPAN)) & (2 ** SPAN - 1)) > 0):
                        with pe.Fori(0, SPAN) as q:
                            turn(m, g * SPAN + q, bits)
                    with pe.Else():
                        pe.drain().then_inc(onehot_used, SPAN * BODY)
                for ps in edge_ps[m]:
                    last = te.matmul(ps, zero_l[:], zeros, start=False, stop=True)
                last.then_inc(pass_ready, 1)
                if m == 1:
                    pe.wait_ge(emb_act, 1)
                    pe.wait_ge(tile_taken, pre.base + 1)
                    te.matmul(ring[0:COND, pre.bank("z1"), :], fw1[:], rnd[:], start=True, stop=True).then_inc(tile_ready, 1)
                if m == 3:
                    pe.wait_ge(emb_step, 7)
                    te.matmul(ring[:, pre.bank("z2"), :], fw2[:], sil[0][:], start=True, stop=True).then_inc(tile_ready, 1)

            mix_products(early, 4)
            pe.wait_ge(pass_act, 2 * NT)
            pe.wait_ge(pass_dve, NT)
            out = begin(mid, mid.base, "deg")
            for j in range(NT):
                last = multiply(out[:, 2 * j:2 * j + 2], [(cols(Araw, m, j), ones[:, 0:2]) for m in range(NT)])
            last.then_inc(tile_ready, 1)
            mix_products(early, 4)
            pe.wait_ge(deg_step, 2 + NT)
            out = begin(mid, mid.base, "dinv")
            for j in range(NT):
                last = te.matmul(out[:, j * P:(j + 1) * P], ones[:], diag[:, j, :], start=True, stop=True)
            last.then_inc(tile_ready, 1)

            mix_products(early, 4)
            pe.wait_ge(sel_step, 8)
            pe.wait_ge(deg_step, 2 + 3 * NT)
            pe.wait_ge(h0_ready, NT)
            for l in range(2):
                B = n0.base
                hh, hl, gh, gl, uh, ul = hb_h[l], hb_l[l], hb_h[1 - l], hb_l[1 - l], hb_h[l], hb_l[l]
                if l:
                    mix_products(early, 4)
                    taken(n0, B, ("H", 0, NT - 1))
                for m in range(KT):
                    out = begin(n0, B, ("G", l, m))
                    multiply(out, [p for t in range(NT) for p in three(cols(hh, t, m), cols(hl, t, m), An_h[:, t, :], An_l[:, t, :])]
                             ).then_inc(tile_ready, 1)
                s = slot(2 * l)
                mix_products(early, 4)
                pe.wait_ge(weight_lo, 2 * l + 1)
                taken(n0, B, ("G", l, KT - 1))
                for m in range(KT):
                    out = begin(n0, B, ("U", l, m))
                    multiply(out, [bias_to_columns(2 * l, bias_rows, m)]
                             + [p for k in range(KT) for p in three(cols(wh[s], k, m), cols(wl[s], k, m), gh[:, k, :], gl[:, k, :])]
                             ).then_inc(tile_ready, 1)
                s = slot(2 * l + 1)
                mix_products(early, 4)
                pe.wait_ge(weight_lo, 2 * l + 2)
                taken(n0, B, ("U", l, KT - 1))
                for t in range(NT):
                    out = begin(n0, B, ("H", l, t))
                    multiply(out, [bias_to_rows(2 * l + 1, bias_rows)]
                             + [p for k in range(KT) for p in three(cols(uh, k, t), cols(ul, k, t), wh[s][:, k, :], wl[s][:, k, :])]
                             ).then_inc(tile_ready, 1)

            mix_products(early, 4)
            for j in range(NT):
                out = begin(cnt, cnt.base, ("C", j))
                transposes(out, [cols(Csum, m, j) for m in range(NT)]).then_inc(tile_ready, 1)
            mix_products(early, len(early))

            pe.wait_ge(tile_taken, n1.base)
            pe.wait_ge(emb_step, 9)
            with pe.Fori(0, BLOCKS) as i:
                b = i * PER + n1.base

                def weight(j):
                    pe.wait_ge(weight_lo, i * 6 + (W1 + j + 1))
                    return wh[j % 3], wl[j % 3]

                def done(name):
                    taken(n1, b, name)

                def tile(name, pairs):
                    multiply(begin(n1, b, name), pairs).then_inc(tile_ready, 1)

                def condition(s, t):
                    n = "ab".index(s)
                    if t == 0:
                        pe.wait_ge(cond_ready, i * 2 + (n + 1))
                    tile(("S" + s, t), [(stk[:, t * P:(t + 1) * P], cond[:, 2 * n, :])])
                    tile(("B" + s, t), [(stk[:, t * P:(t + 1) * P], cond[:, 2 * n + 1, :])])

                def transpose_rows(s, t):
                    done(("B" + s, t))
                    out = begin(n1, b, ("T" + s, t))
                    transposes(out, [cols(yp, t, k) for k in range(KT)]).then_inc(tile_ready, 1)

                def part(out, pairs, first=False, last=False):
                    for n, (l, r) in enumerate(pairs):
                        ins = te.matmul(out, l, r, start=first and n == 0, stop=last and n == len(pairs) - 1)
                    return ins

                def rows_product(name, t, lh, ll, w, bias):
                    tile((name, t), [bias_to_rows(bias, brow)] + [p for k in range(KT) for p in
                         three(cols(lh, k, t), cols(ll, k, t), w[0][:, k, :], w[1][:, k, :])])

                def columns_product(name, m, w, rh, rl, bias):
                    tile((name, m), [bias_to_columns(bias, brow, m)] + [p for k in range(KT) for p in
                         three(cols(w[0], k, m), cols(w[1], k, m), rh[:, k, :], rl[:, k, :])])

                def value(t, w):
                    done(("Ta", t))
                    out = begin(n1, b, ("v", t))
                    part(out, [p for k in range(KT) for p in three(cols(yT_h, k, t), cols(yT_l, k, t), w[0][:, k, :], w[1][:, k, :])],
                         first=True)
                    if t == 0:
                        pe.wait_ge(brow_ready, i + 1)
                    part(out, [bias_to_rows(0, brow)], last=True).then_inc(tile_ready, 1)

                def query_key(h):
                    columns_product("q", h, wq, yT_h, yT_l, 1)
                    if h == 0:
                        weight(2)
                    columns_product("k", h, wk, yT_h, yT_l, 2)

                def scores(h):
                    done(("k", h))
                    for j in range(NT):
                        tile(("s", h, j), three(qk_h[:, 0, j * P:(j + 1) * P], qk_l[:, 0, j * P:(j + 1) * P], qk_h[:, 1, :], qk_l[:, 1, :]))

                def probs_T(h):
                    for m in range(NT):
                        if m == 0:
                            pe.wait_ge(probs_ready, i * 16 + (4 * h + 4))
                        out = begin(n1, b, ("PT", h, m))
                        transposes(out, [cols(probs_of[h % 2], j, m) for j in range(NT)]).then_inc(tile_ready, 1)

                def mean_value(h):
                    out = begin(n1, b, ("PV", h))
                    if h == 0:
                        done(("v", NT - 1))
                    for m in range(NT):
                        done(("PT", h, m))
                        last = part(out, three(cols(vm_h, m, h), cols(vm_l, m, h), PT_h[:, m, :], PT_l[:, m, :]),
                                    first=m == 0, last=m == NT - 1)
                    last.then_inc(tile_ready, 1)

                def hidden(m, half, w):
                    out = begin(n1, b, ("M", m)) if half == 0 else bank_of(("M", m))
                    c = slice(half * NODES // 2, (half + 1) * NODES // 2)
                    pairs = [(brow[:, m * P:(m + 1) * P], sel[:, 4:5, :].broadcast_to([P, NT // 2, P]))]
                    pairs += [p for k in range(KT) for p in three(cols(w[0], k, m), cols(w[1], k, m), yT_h[:, k, c], yT_l[:, k, c])]
                    ins = part(out[:, c], pairs, first=True, last=True)
                    if half:
                        ins.then_inc(tile_ready, 1)

                def bank_of(name):
                    return ring[:, n1.bank(name), :]

                block_products = list(range(SHIFTS))

                def mix_in_block(count):
                    for j in block_products[:count]:
                        mix_product(i + EARLY_SETS, j)
                    del block_products[:count]

                condition("a", 0)
                condition("a", 1)
                mix_in_block(4)
                transpose_rows("a", 0)
                condition("a", 2)
                transpose_rows("a", 1)
                w = weight(0)
                value(0, w)
                condition("a", 3)
                transpose_rows("a", 2)
                value(1, w)
                transpose_rows("a", 3)
                mix_in_block(2)
                done(("Ta", NT - 1))
                wq, wk = weight(1), (wh[2], wl[2])
                query_key(0)
                value(2, w)
                scores(0)
                query_key(1)
                for h in range(1, HEADS):
                    if h <= 2:
                        mix_in_block(2)
                    probs_T(h - 1)
                    if h == 1:
                        value(3, w)
                    scores(h)
                    mean_value(h - 1)
                    if h + 1 < HEADS:
                        query_key(h + 1)
                w = weight(3)
                head = lambda t, h: three(cols(oT_h, h, t), cols(oT_l, h, t), w[0][:, h, :], w[1][:, h, :])
                early = {}
                for t in range(2):
                    early[t] = begin(n1, b, ("o", t))
                    part(early[t], [bias_to_rows(3, brow)] + head(t, 0) + head(t, 1), first=True)
                done(("PV", HEADS - 2))
                for t in range(2):
                    part(early[t], head(t, 2))
                probs_T(HEADS - 1)
                mix_in_block(2)
                mean_value(HEADS - 1)
                mix_in_block(2)
                done(("PV", HEADS - 1))
                for t in range(2):
                    part(early[t], head(t, 3), last=True).then_inc(tile_ready, 1)
                condition("b", 0)
                condition("b", 1)
                for t in range(2, NT):
                    rows_product("o", t, oT_h, oT_l, w, 3)
                    if t == 2:
                        mix_in_block(2)
                        transpose_rows("b", 0)
                        transpose_rows("b", 1)
                    condition("b", t)
                w = weight(4)
                done(("Tb", 1))
                hidden(0, 0, w)
                hidden(1, 0, w)
                transpose_rows("b", 2)
                hidden(2, 0, w)
                transpose_rows("b", 3)
                hidden(3, 0, w)
                done(("Tb", NT - 1))
                for m in range(KT):
                    hidden(m, 1, w)
                w = weight(5)
                for t in range(NT):
                    out = begin(n1, b, ("X", t))
                    part(out, [bias_to_rows(5, brow)], first=True)
                    for k in range(KT):
                        if t == 0:
                            done(("M", k))
                        last = part(out, three(cols(vm_h, k, t), cols(vm_l, k, t), w[0][:, k, :], w[1][:, k, :]), last=k == KT - 1)
                    last.then_inc(tile_ready, 1)

            B = n2.base
            mix_products(late, 4)
            for t in range(NT):
                pe.wait_ge(y_ready, t + 1)
                transposes(begin(n2, B, ("T", t)), [cols(y2, t, k) for k in range(KT)]).then_inc(tile_ready, 1)
            mix_products(late, 4)
            pe.wait_ge(weight_lo, W2 + 1)
            s = slot(W2)
            for t in range(NT):
                taken(n2, B, ("T", t))
                multiply(begin(n2, B, ("A", 0, t)), [bias_to_rows(4, bias_rows)] + [p for k in range(KT) for p in
                         three(cols(y2T_h, k, t), cols(y2T_l, k, t), wh[s][:, k, :], wl[s][:, k, :])]).then_inc(tile_ready, 1)
            pe.wait_ge(l2_step, STEPS + NT + 1)
            for k in range(1, STEPS + 1):
                c = (k - 1) % 2
                mix_products(late, 4)
                taken(n2, B, ("A", k - 1, NT - 1))
                for t in range(NT):
                    multiply(begin(n2, B, ("A", k, t)), [p for m in range(NT) for p in
                             ((cols(adj_r, m, t), cur_h[:, c, m, :]), (cols(adj_r, m, t), cur_l[:, c, m, :]))]).then_inc(tile_ready, 1)

            B = n3.base
            assert not late
            for t in range(NT):
                pe.wait_ge(y_ready, NT + t + 1)
                transposes(begin(n3, B, ("T", t)), [cols(y3, t, k) for k in range(KT)]).then_inc(tile_ready, 1)
            for l in range(2):
                h, hl = hT_h[l], hT_l[l]
                taken(n3, B, ("T", NT - 1) if l == 0 else ("R", 0, KT - 1))
                out = begin(n3, B, ("g", l))
                for t in range(NT):
                    last = multiply(out[:, 2 * t:2 * t + 2], [p for k in range(KT) for p in
                                    three(cols(h, k, t), cols(hl, k, t), gwh[:, l, k, :], gwl[:, l, k, :])])
                last.then_inc(tile_ready, 1)
                for r in range(2):
                    w = W3 + 3 * l + r
                    pe.wait_ge(weight_lo, w + 1)
                    for t in range(NT):
                        multiply(begin(n3, B, ("Z", l, r, t)), [p for k in range(KT) for p in
                                 three(cols(h, k, t), cols(hl, k, t), wh[slot(w)][:, k, :], wl[slot(w)][:, k, :])]).then_inc(tile_ready, 1)
                w = W3 + 3 * l + 2
                pe.wait_ge(weight_lo, w + 1)
                wrh, wrl = wh[slot(w)], wl[slot(w)]
                pe.wait_ge(c_ready, 2)
                taken(n3, B, ("Z", l, 1, NT - 1))
                for m in range(NT):
                    if l == 0:
                        pairs = [bias_to_columns(5, bias_rows, m)]
                        pairs += [p for k in range(KT) for p in three(cols(wrh, k, m), cols(wrl, k, m), h[:, k, :], hl[:, k, :])]
                        pairs += [p for r in range(2) for t in range(NT) for p in
                                  three(Z_h[:, r, t, m * P:(m + 1) * P], Z_l[:, r, t, m * P:(m + 1) * P], C_h[:, r, t, :], C_l[:, r, t, :])]
                    else:
                        pairs = [bias_to_rows(6, bias_rows)]
                        pairs += [p for k in range(KT) for p in three(cols(h, k, m), cols(hl, k, m), wrh[:, k, :], wrl[:, k, :])]
                        pairs += [p for r in range(2) for t in range(NT) for p in
                                  three(C_h[:, r, t, m * P:(m + 1) * P], C_l[:, r, t, m * P:(m + 1) * P], Z_h[:, r, t, :], Z_l[:, r, t, :])]
                    multiply(begin(n3, B, ("R", l, m)), pairs).then_inc(tile_ready, 1)


SMALL = 2 + 2 * QUADS + 4 + 7 + 1 + 2 + 6 + 1
CNT = 5
MIX_MID = (3, 1, 0)
MIX_G = (2, 2, 2, 2)
MIX_H = (2, 1, 1, 2)
MIX_3 = (6, 2, 2)
GROUPS_MID = (1, 1)
_mixed = [BSLOTS * NT + sum(MIX_MID) + l * (2 * sum(MIX_G) + sum(MIX_H)) + n for l in range(2)
          for n in (sum(MIX_G), 2 * sum(MIX_G), 2 * sum(MIX_G) + sum(MIX_H))]
_loaded = [NT + sum(GROUPS_MID)] + [min(n // BSLOTS + 1, 2 * BASES // BSLOTS) for n in _mixed]
GROUPS_0 = [b - a for a, b in zip(_loaded, _loaded[1:])]


_L0 = ["W_gcn", "b_gcn", "W_mlp", "b_mlp"]
_L1 = ["f_w1", "f_b1", "f_w2", "f_b2", "s1_w", "s1_b", "b1_w", "b1_b", "wq", "bq", "wk", "bk", "wv", "bv", "wo", "bo",
       "s2_w", "s2_b", "b2_w", "b2_b", "m_w1", "m_b1", "m_w2", "m_b2"]
_L2 = ["W", "b", "diffusion_weights"]
_L3 = [f"{n}{l}" for l in (1, 2) for n in ("basis", "att", "gate_w", "root", "bias")]
_INS = (["x", "src", "dst", "edge_type_2", "edge_weight", "node_vec1"] + [f"L0_gnn_{n}" for n in _L0]
        + [f"L1_gnn_{n}" for n in _L1] + [f"L2_gnn_{n}" for n in _L2] + [f"L3_gnn_{n}" for n in _L3])


def kernel(**inputs):
    import numpy as _np
    import concourse.bacc as _bacc
    from concourse import mybir as _mybir
    from concourse.bass_utils import run_bass_kernel_spmd as _run

    nc = _bacc.Bacc("TRN2", target_bir_lowering=False, num_devices=1)
    arrays, d = {}, {}
    for name in _INS:
        a = _np.ascontiguousarray(inputs[name])
        arrays[f"in_{name}"] = a
        d[name] = nc.dram_tensor(f"in_{name}", a.shape, _mybir.dt.from_np(a.dtype), kind="ExternalInput").ap()
    out = nc.dram_tensor("out", (NODES, D), _mybir.dt.float32, kind="ExternalOutput").ap()
    mix_d = nc.dram_tensor("mix_scratch", (2, 2, D, D), _mybir.dt.float32).ap()
    ct_d = nc.dram_tensor("count_scratch", (2, P, NT, NODES), _mybir.dt.int16).ap()
    x_s = nc.dram_tensor("row_scratch", (NODES, D), _mybir.dt.float32).ap()
    l0 = {n: d[f"L0_gnn_{n}"] for n in _L0}
    l1 = {n: d[f"L1_gnn_{n}"] for n in _L1}
    l2 = {"W": d["L2_gnn_W"], "b": d["L2_gnn_b"], "dw": d["L2_gnn_diffusion_weights"]}
    l3 = {n: [d[f"L3_gnn_{n}{l}"] for l in (1, 2)] for n in ("basis", "att", "gate_w", "root", "bias")}
    program(nc, d["x"], d["src"], d["dst"], d["edge_type_2"], d["edge_weight"], d["node_vec1"], l0, l1, l2, l3, out, mix_d, ct_d, x_s)
    r = _run(nc, [arrays], core_ids=[0])
    return r.results[0]["out"]
```
